# Optimizing a Trainium2 kernel written in Bass

```python
import numpy as np
import jax
import jax.numpy as jnp

def _softmax(x, axis=-1):
    return jax.nn.softmax(x, axis=axis)

def _gelu(x):
    return jax.nn.gelu(x, approximate=True)

def _silu(x):
    return jax.nn.silu(x)

def _sigmoid(x):
    return jax.nn.sigmoid(x)

def _layernorm(x, axis=-1, eps=1e-05):
    m = jnp.mean(x, axis=axis, keepdims=True)
    v = jnp.var(x, axis=axis, keepdims=True)
    return (x - m) / jnp.sqrt(v + eps)

def _scatter_add(tgt, idx, src, axis=0):
    return tgt.at[idx].add(src)

def _segment_sum(src, seg, n):
    return jax.ops.segment_sum(src, seg, n)
kernel_name = 'mk_flamingo_gated_d2_seqx_r4_d0e684'

def setup_inputs(seed: int=0):
    np.random.seed(seed)
    _w = jnp.asarray

    def _rec_inputs():
        import jax
        import jax.numpy as jnp
        _rk = jax.random.key(seed)
        x = -0.0002928 + 1 * jax.random.normal(jax.random.fold_in(_rk, 1), (16, 100, 256), jnp.float32)
        _lenS = 100 - jax.random.randint(jax.random.fold_in(_rk, 7), (16,), 0, max(1, 100 // 4) + 1, jnp.int32)
        _lenS2 = 361 - jax.random.randint(jax.random.fold_in(_rk, 8), (16,), 0, max(1, 361 // 4) + 1, jnp.int32)
        _ctx_1024P = jax.random.normal(jax.random.fold_in(_rk, 11), (16, 16, 256), jnp.float32)
        _ctx_1024c = jax.random.dirichlet(jax.random.fold_in(_rk, 511), 0.3 * jnp.ones((16,), jnp.float32), (16, 361))
        _ctx_1024t = jnp.einsum('bsk,bkd->bsd', _ctx_1024c, _ctx_1024P)
        _ctx_1024t = _ctx_1024t * jax.lax.rsqrt(jnp.mean(jnp.square(_ctx_1024t)) + 1e-12) * 0.953939
        ctx_1024 = -1.39393e-06 + 0.999914 * (_ctx_1024t + 0.3 * jax.random.normal(jax.random.fold_in(_rk, 611), (16, 361, 256), jnp.float32))
        _g = jax.random.normal(jax.random.fold_in(_rk, 9001), (2, 2), jnp.float32)
        _g = jnp.sign(_g) * jnp.maximum(jnp.abs(_g), 1.0) + (_g == 0) * 1.0
        g_xattn = _g[0]
        g_ffn = _g[1]
        return (x, ctx_1024, g_xattn, g_ffn)
    x, ctx_1024, g_xattn, g_ffn = _rec_inputs()

    def _L0_xattn_setup():
        import jax, jax.numpy as jnp
        import numpy as np
        import math
        EMBED_DIM = 256
        NUM_HEADS = 16
        HEAD_DIM = EMBED_DIM // NUM_HEADS
        SUB_HEAD_DIM = HEAD_DIM // 2
        SCALING = 1.0 / math.sqrt(SUB_HEAD_DIM)
        LAMBDA_INIT = 0.8 - 0.6 * math.exp(-0.3 * 0)
        key = jax.random.key(seed)
        ks = jax.random.split(key, 10)
        B, T, D = (2, 512, EMBED_DIM)
        xav = math.sqrt(6.0 / (D + D))
        return {'query': jax.random.normal(ks[0], (B, T, D), jnp.float32), 'key': jax.random.normal(ks[1], (B, T, D), jnp.float32), 'value': jax.random.normal(ks[2], (B, T, D), jnp.float32), 'in_proj_weight': jax.random.uniform(ks[3], (3 * D, D), jnp.float32, -xav, xav), 'in_proj_bias': jnp.zeros((3 * D,), jnp.float32), 'out_proj_weight': jax.random.uniform(ks[4], (D, D), jnp.float32, -xav, xav), 'out_proj_bias': jnp.zeros((D,), jnp.float32), 'lambda_q1': 0.1 * jax.random.normal(ks[5], (SUB_HEAD_DIM,), jnp.float32), 'lambda_k1': 0.1 * jax.random.normal(ks[6], (SUB_HEAD_DIM,), jnp.float32), 'lambda_q2': 0.1 * jax.random.normal(ks[7], (SUB_HEAD_DIM,), jnp.float32), 'lambda_k2': 0.1 * jax.random.normal(ks[8], (SUB_HEAD_DIM,), jnp.float32)}
    _L0_xattn_all = _L0_xattn_setup()
    _L0_xattn_in = {k: v for k, v in _L0_xattn_all.items() if k in ('in_proj_weight', 'in_proj_bias', 'out_proj_weight', 'out_proj_bias', 'lambda_q1', 'lambda_k1', 'lambda_q2', 'lambda_k2')}
    del _L0_xattn_all

    def _L0_ffn_setup():
        import jax, jax.numpy as jnp
        import numpy as np
        B, S, D, H, E = (2, 512, 256, 16, 8)
        DH = D // H
        CAP_FACTOR = 1.2

        def _forward(embed, Wq, bq, Wk, bk, Wv, bv, We, be, Wsw, bsw, gamma, beta):
            b, s, d = embed.shape
            h, e = (Wq.shape[0], We.shape[0])
            q = jnp.einsum('bsd,hed->bhse', embed, Wq) + bq[None, :, None, :]
            k = jnp.einsum('bsd,hed->bhse', embed, Wk) + bk[None, :, None, :]
            v = jnp.einsum('bsd,hed->bhse', embed, Wv) + bv[None, :, None, :]
            att = jnp.einsum('bhse,bhte->bhst', q, k)
            tril = jnp.tril(jnp.ones((s, s), bool))
            att = jnp.where(tril, att, 0.0) / jnp.sqrt(jnp.float32(d))
            att = jax.nn.softmax(att, axis=-1)
            out = jnp.einsum('bhst,bhte->bhse', att, v)
            hiddens = out.transpose(0, 2, 1, 3).reshape(b, s, d)
            x = hiddens.reshape(-1, d)
            n = b * s
            capacity = int(CAP_FACTOR * n / e)
            logits = x @ Wsw.T + bsw
            probs = jax.nn.softmax(logits, axis=-1)
            route_probs = jnp.max(probs, axis=-1)
            routes = jnp.argmax(probs, axis=-1)
            onehot = jax.nn.one_hot(routes, e, dtype=jnp.int32)
            pos = jnp.cumsum(onehot, axis=0) - 1
            pos = jnp.take_along_axis(pos, routes[:, None], axis=1)[:, 0]
            kept = pos < capacity
            slot = jnp.where(kept, routes * capacity + pos, e * capacity)
            dispatch = jnp.zeros((e * capacity + 1, d), x.dtype).at[slot].set(x)
            expert_in = dispatch[:e * capacity].reshape(e, capacity, d)
            expert_out = jnp.einsum('ecd,efd->ecf', expert_in, We) + be[:, None, :]
            expert_flat = jnp.concatenate([expert_out.reshape(e * capacity, d), jnp.zeros((1, d), x.dtype)], 0)
            gathered = expert_flat[slot]
            y = jnp.where(kept[:, None], gathered, x)
            y = (y * route_probs[:, None]).reshape(b, s, d)
            x2 = y + embed
            mean = jnp.mean(x2, axis=-1, keepdims=True)
            var = jnp.var(x2, axis=-1, keepdims=True)
            return (x2 - mean) / jnp.sqrt(var + 1e-05) * gamma + beta
        key = jax.random.key(seed)
        ks = jax.random.split(key, 14)
        s = 0.02
        return {'embed': jax.random.normal(ks[0], (B, S, D), jnp.float32), 'Wq': jax.random.normal(ks[1], (H, DH, D), jnp.float32) * s, 'bq': jnp.zeros((H, DH), jnp.float32), 'Wk': jax.random.normal(ks[2], (H, DH, D), jnp.float32) * s, 'bk': jnp.zeros((H, DH), jnp.float32), 'Wv': jax.random.normal(ks[3], (H, DH, D), jnp.float32) * s, 'bv': jnp.zeros((H, DH), jnp.float32), 'We': jax.random.normal(ks[4], (E, D, D), jnp.float32) * s, 'be': jnp.zeros((E, D), jnp.float32), 'Wsw': jax.random.normal(ks[5], (E, D), jnp.float32) * s, 'bsw': jnp.zeros((E,), jnp.float32), 'gamma': jnp.ones((D,), jnp.float32), 'beta': jnp.zeros((D,), jnp.float32)}
    _L0_ffn_all = _L0_ffn_setup()
    _L0_ffn_in = {k: v for k, v in _L0_ffn_all.items() if k in ('Wq', 'bq', 'Wk', 'bk', 'Wv', 'bv', 'We', 'be', 'Wsw', 'bsw', 'gamma', 'beta')}
    del _L0_ffn_all

    def _L1_xattn_setup():
        import jax, jax.numpy as jnp
        import numpy as np
        D1, D2, D3 = (256, 256, 256)
        key = jax.random.key(seed)
        k1, k2, kw, kb = jax.random.split(key, 4)
        x1 = jax.random.normal(k1, (8, 512, D1), dtype=jnp.float32)
        x2 = jax.random.normal(k2, (8, 512, D2), dtype=jnp.float32)
        bound = 1.0 / np.sqrt(D1 + D2)
        W = jax.random.uniform(kw, (D3, D1 + D2), minval=-bound, maxval=bound, dtype=jnp.float32)
        b = jax.random.uniform(kb, (D3,), minval=-bound, maxval=bound, dtype=jnp.float32)
        return {'x1': x1, 'x2': x2, 'W': W, 'b': b}
    _L1_xattn_all = _L1_xattn_setup()
    _L1_xattn_in = {k: v for k, v in _L1_xattn_all.items() if k in ('W', 'b')}
    del _L1_xattn_all

    def _L1_ffn_setup():
        import jax, jax.numpy as jnp
        import numpy as np
        DIM = 256
        NUM_EXPERTS = 8
        TOP_K = 2
        HIDDEN = int(DIM * 1.5)
        key = jax.random.key(seed)
        k_x, k_r, k_w1, k_w2, k_w3 = jax.random.split(key, 5)
        B, T = (2, 1024)
        s_in = 1.0 / np.sqrt(DIM)
        s_h = 1.0 / np.sqrt(HIDDEN)
        return {'x': jax.random.normal(k_x, (B, T, DIM), dtype=jnp.float32), 'Wr': jax.random.uniform(k_r, (DIM, NUM_EXPERTS), minval=-s_in, maxval=s_in, dtype=jnp.float32), 'W1': jax.random.uniform(k_w1, (NUM_EXPERTS, DIM, HIDDEN), minval=-s_in, maxval=s_in, dtype=jnp.float32), 'W2': jax.random.uniform(k_w2, (NUM_EXPERTS, HIDDEN, DIM), minval=-s_h, maxval=s_h, dtype=jnp.float32), 'W3': jax.random.uniform(k_w3, (NUM_EXPERTS, DIM, HIDDEN), minval=-s_in, maxval=s_in, dtype=jnp.float32)}
    _L1_ffn_all = _L1_ffn_setup()
    _L1_ffn_in = {k: v for k, v in _L1_ffn_all.items() if k in ('Wr', 'W1', 'W2', 'W3')}
    del _L1_ffn_all
    return {'x': x, 'ctx_1024': ctx_1024, 'g_xattn': g_xattn, 'g_ffn': g_ffn, 'L0_xattn_in_proj_weight': _L0_xattn_in['in_proj_weight'], 'L0_xattn_in_proj_bias': _L0_xattn_in['in_proj_bias'], 'L0_xattn_out_proj_weight': _L0_xattn_in['out_proj_weight'], 'L0_xattn_out_proj_bias': _L0_xattn_in['out_proj_bias'], 'L0_xattn_lambda_q1': _L0_xattn_in['lambda_q1'], 'L0_xattn_lambda_k1': _L0_xattn_in['lambda_k1'], 'L0_xattn_lambda_q2': _L0_xattn_in['lambda_q2'], 'L0_xattn_lambda_k2': _L0_xattn_in['lambda_k2'], 'L0_ffn_Wq': _L0_ffn_in['Wq'], 'L0_ffn_bq': _L0_ffn_in['bq'], 'L0_ffn_Wk': _L0_ffn_in['Wk'], 'L0_ffn_bk': _L0_ffn_in['bk'], 'L0_ffn_Wv': _L0_ffn_in['Wv'], 'L0_ffn_bv': _L0_ffn_in['bv'], 'L0_ffn_We': _L0_ffn_in['We'], 'L0_ffn_be': _L0_ffn_in['be'], 'L0_ffn_Wsw': _L0_ffn_in['Wsw'], 'L0_ffn_bsw': _L0_ffn_in['bsw'], 'L0_ffn_gamma': _L0_ffn_in['gamma'], 'L0_ffn_beta': _L0_ffn_in['beta'], 'L1_xattn_W': _L1_xattn_in['W'], 'L1_xattn_b': _L1_xattn_in['b'], 'L1_ffn_Wr': _L1_ffn_in['Wr'], 'L1_ffn_W1': _L1_ffn_in['W1'], 'L1_ffn_W2': _L1_ffn_in['W2'], 'L1_ffn_W3': _L1_ffn_in['W3']}

def reference(x, ctx_1024, g_xattn, g_ffn, L0_xattn_in_proj_weight, L0_xattn_in_proj_bias, L0_xattn_out_proj_weight, L0_xattn_out_proj_bias, L0_xattn_lambda_q1, L0_xattn_lambda_k1, L0_xattn_lambda_q2, L0_xattn_lambda_k2, L0_ffn_Wq, L0_ffn_bq, L0_ffn_Wk, L0_ffn_bk, L0_ffn_Wv, L0_ffn_bv, L0_ffn_We, L0_ffn_be, L0_ffn_Wsw, L0_ffn_bsw, L0_ffn_gamma, L0_ffn_beta, L1_xattn_W, L1_xattn_b, L1_ffn_Wr, L1_ffn_W1, L1_ffn_W2, L1_ffn_W3):
    import jax
    import jax.numpy as jnp

    def _L0_xattn_ref(query, key, value, in_proj_weight, in_proj_bias, out_proj_weight, out_proj_bias, lambda_q1, lambda_k1, lambda_q2, lambda_k2):
        import jax, jax.numpy as jnp
        import numpy as np
        import math
        EMBED_DIM = 256
        NUM_HEADS = 16
        HEAD_DIM = EMBED_DIM // NUM_HEADS
        SUB_HEAD_DIM = HEAD_DIM // 2
        SCALING = 1.0 / math.sqrt(SUB_HEAD_DIM)
        LAMBDA_INIT = 0.8 - 0.6 * math.exp(-0.3 * 0)
        B, T, D = query.shape
        S = key.shape[1]
        H, hd, sd = (NUM_HEADS, HEAD_DIM, SUB_HEAD_DIM)
        qw, kw, vw = jnp.split(in_proj_weight, 3, axis=0)
        qb, kb, vb = jnp.split(in_proj_bias, 3, axis=0)
        q = query @ qw.T + qb
        k = key @ kw.T + kb
        v = value @ vw.T + vb
        q = q.reshape(B, T, H, hd).transpose(0, 2, 1, 3)
        k = k.reshape(B, S, H, hd).transpose(0, 2, 1, 3)
        v = v.reshape(B, S, H, hd).transpose(0, 2, 1, 3)
        q1, q2 = (q[..., :sd], q[..., sd:])
        k1, k2 = (k[..., :sd], k[..., sd:])
        logits_1 = jnp.einsum('bhtd,bhsd->bhts', q1, k1) * SCALING
        logits_2 = jnp.einsum('bhtd,bhsd->bhts', q2, k2) * SCALING
        a1 = jax.nn.softmax(logits_1, axis=-1)
        a2 = jax.nn.softmax(logits_2, axis=-1)
        lam = jnp.exp(jnp.dot(lambda_q1, lambda_k1)) - jnp.exp(jnp.dot(lambda_q2, lambda_k2)) + LAMBDA_INIT
        diff_weights = a1 - lam * a2
        attn_output = jnp.einsum('bhts,bhsd->bhtd', diff_weights, v)
        attn_output = attn_output * (1.0 - LAMBDA_INIT)
        attn_output = attn_output.transpose(0, 2, 1, 3).reshape(B, T, D)
        output = attn_output @ out_proj_weight.T + out_proj_bias
        return output

    def _L0_ffn_ref(embed, Wq, bq, Wk, bk, Wv, bv, We, be, Wsw, bsw, gamma, beta):
        import jax, jax.numpy as jnp
        import numpy as np
        B, S, D, H, E = (2, 512, 256, 16, 8)
        DH = D // H
        CAP_FACTOR = 1.2

        def _forward(embed, Wq, bq, Wk, bk, Wv, bv, We, be, Wsw, bsw, gamma, beta):
            b, s, d = embed.shape
            h, e = (Wq.shape[0], We.shape[0])
            q = jnp.einsum('bsd,hed->bhse', embed, Wq) + bq[None, :, None, :]
            k = jnp.einsum('bsd,hed->bhse', embed, Wk) + bk[None, :, None, :]
            v = jnp.einsum('bsd,hed->bhse', embed, Wv) + bv[None, :, None, :]
            att = jnp.einsum('bhse,bhte->bhst', q, k)
            tril = jnp.tril(jnp.ones((s, s), bool))
            att = jnp.where(tril, att, 0.0) / jnp.sqrt(jnp.float32(d))
            att = jax.nn.softmax(att, axis=-1)
            out = jnp.einsum('bhst,bhte->bhse', att, v)
            hiddens = out.transpose(0, 2, 1, 3).reshape(b, s, d)
            x = hiddens.reshape(-1, d)
            n = b * s
            capacity = int(CAP_FACTOR * n / e)
            logits = x @ Wsw.T + bsw
            probs = jax.nn.softmax(logits, axis=-1)
            route_probs = jnp.max(probs, axis=-1)
            routes = jnp.argmax(probs, axis=-1)
            onehot = jax.nn.one_hot(routes, e, dtype=jnp.int32)
            pos = jnp.cumsum(onehot, axis=0) - 1
            pos = jnp.take_along_axis(pos, routes[:, None], axis=1)[:, 0]
            kept = pos < capacity
            slot = jnp.where(kept, routes * capacity + pos, e * capacity)
            dispatch = jnp.zeros((e * capacity + 1, d), x.dtype).at[slot].set(x)
            expert_in = dispatch[:e * capacity].reshape(e, capacity, d)
            expert_out = jnp.einsum('ecd,efd->ecf', expert_in, We) + be[:, None, :]
            expert_flat = jnp.concatenate([expert_out.reshape(e * capacity, d), jnp.zeros((1, d), x.dtype)], 0)
            gathered = expert_flat[slot]
            y = jnp.where(kept[:, None], gathered, x)
            y = (y * route_probs[:, None]).reshape(b, s, d)
            x2 = y + embed
            mean = jnp.mean(x2, axis=-1, keepdims=True)
            var = jnp.var(x2, axis=-1, keepdims=True)
            return (x2 - mean) / jnp.sqrt(var + 1e-05) * gamma + beta
        return _forward(embed, Wq, bq, Wk, bk, Wv, bv, We, be, Wsw, bsw, gamma, beta)

    def _L1_xattn_ref(x1, x2, W, b):
        import jax, jax.numpy as jnp
        import numpy as np
        D1, D2, D3 = (256, 256, 256)
        d1 = x1.shape[-1]
        W1 = W[:, :d1]
        W2 = W[:, d1:]
        part1 = jnp.einsum('bld,ed->ble', x1, W1)
        part2 = jnp.einsum('bld,ed->be', x2, W2) / x2.shape[1]
        return part1 + part2[:, None, :] + b

    def _L1_ffn_ref(x, Wr, W1, W2, W3):
        import jax, jax.numpy as jnp
        import numpy as np
        DIM = 256
        NUM_EXPERTS = 8
        TOP_K = 2
        HIDDEN = int(DIM * 1.5)
        B, T, C = x.shape
        xf = x.reshape(-1, C)
        gate_logits = xf @ Wr
        w, idx = jax.lax.top_k(gate_logits, TOP_K)
        w = jax.nn.softmax(w, axis=-1)
        comb = jnp.sum(w[:, :, None] * jax.nn.one_hot(idx, NUM_EXPERTS, dtype=w.dtype), axis=1)
        h = jnp.einsum('nc,ech->neh', xf, W1)
        g = jnp.einsum('nc,ech->neh', xf, W3)
        y = jnp.einsum('neh,ehc->nec', jax.nn.silu(h) * g, W2)
        out = jnp.einsum('nec,ne->nc', y, comb)
        return out.reshape(B, T, C)
    x = x + jnp.tanh(g_xattn[0]) * _L0_xattn_ref(_layernorm(x, axis=-1), ctx_1024, ctx_1024, L0_xattn_in_proj_weight, L0_xattn_in_proj_bias, L0_xattn_out_proj_weight, L0_xattn_out_proj_bias, L0_xattn_lambda_q1, L0_xattn_lambda_k1, L0_xattn_lambda_q2, L0_xattn_lambda_k2)
    x = x + jnp.tanh(g_ffn[0]) * _L0_ffn_ref(_layernorm(x, axis=-1), L0_ffn_Wq, L0_ffn_bq, L0_ffn_Wk, L0_ffn_bk, L0_ffn_Wv, L0_ffn_bv, L0_ffn_We, L0_ffn_be, L0_ffn_Wsw, L0_ffn_bsw, L0_ffn_gamma, L0_ffn_beta)
    x = x + jnp.tanh(g_xattn[1]) * _L1_xattn_ref(_layernorm(x, axis=-1), ctx_1024, L1_xattn_W, L1_xattn_b)
    x = x + jnp.tanh(g_ffn[1]) * _L1_ffn_ref(_layernorm(x, axis=-1), L1_ffn_Wr, L1_ffn_W1, L1_ffn_W2, L1_ffn_W3)
    return x

_drawn_inputs = setup_inputs


def setup_inputs(seed=0):
    import zlib

    import numpy as np

    out = dict(_drawn_inputs(seed))
    spreads = {'g_ffn': (-1.0, 0.6),
     'L0_xattn_in_proj_bias': (0.0, 0.1),
     'L0_xattn_out_proj_bias': (0.0, 0.1),
     'L0_ffn_bq': (0.0, 0.8),
     'L0_ffn_bk': (0.0, 0.8),
     'L0_ffn_bv': (0.0, 0.1),
     'L0_ffn_be': (0.0, 0.451),
     'L0_ffn_bsw': (0.0, 0.1),
     'L0_ffn_gamma': (1.0, 0.2),
     'L0_ffn_beta': (0.0, 0.1)}
    factors = {'L0_xattn_lambda_q1': 6.481,
     'L0_xattn_lambda_k1': 3.42,
     'L0_ffn_Wq': 8.0,
     'L0_ffn_Wk': 8.0,
     'L0_ffn_We': 7.47,
     'L0_ffn_Wsw': 2.9}
    for name, (base, spread) in spreads.items():
        noise = np.random.default_rng([zlib.crc32(name.encode()), seed]).standard_normal(out[name].shape)
        drawn = base * np.exp(spread * noise) if base else spread * noise
        out[name] = jnp.asarray(drawn.astype(out[name].dtype))
    for name, factor in factors.items():
        out[name] = (out[name] * factor).astype(out[name].dtype)
    return out
```

```python
from contextlib import ExitStack
import math

import concourse.bass as bass
from concourse import mybir

F32 = mybir.dt.float32
BF16 = mybir.dt.bfloat16
ALU = mybir.AluOpType
ACT = mybir.ActivationFunctionType
AX = mybir.AxisListType

B, T, D = 16, 100, 256
S = 361
H, HD = 16, 16
SUB = HD // 2
KC = D // 128
SC = 3
SP_ = SC * 128
SCALING = 1.0 / math.sqrt(SUB)
LAMBDA_INIT = 0.8 - 0.6 * math.exp(-0.3 * 0)
EPS = 1e-5
RING = 3
BRING = 4

K_PARTS = (0, 0, 0, 1, 1, 2)
Q_PARTS = (0, 1, 2, 0, 1, 0)
G = len(K_PARTS)
E = 8
CAP = int(1.2 * B * T / E)
HALF = CAP // 2
HID2 = D * 3 // 2
E1_BLOCKS = (2 * B * T + E * 127) // 128
ROWS = 16 * G


def batch(off, i=None, stride=3):
    return (i, off, stride)


def later(n, d):
    return (n[0], n[1] + d, n[2])


def count(n, per, extra):
    return n[1] * per + extra if n[0] is None else n[0] * (n[2] * per) + (n[1] * per + extra)


def slot(n, ring=3):
    return n[1] % ring


def uses(n, ring=None):
    ring = ring or n[2]
    return n[1] // ring if n[0] is None else n[0] * (n[2] // ring) + n[1] // ring


def uses_value(n, per, ring=None):
    return (uses(n, ring) + 1) * per


def exists(n, total=16):
    return n[0] is not None or 0 <= n[1] < total


def at(n, width=1):
    if n[0] is None:
        return slice(n[1] * width, n[1] * width + width)
    return bass.ds(n[0] * (n[2] * width) + n[1] * width, width)


def at_batch(tensor, n):
    return tensor[:, n[1], :] if n[0] is None else tensor[:, at(n), :].rearrange("p b d -> p (b d)")


def wait(eng, sem, value):
    if not isinstance(value, int) or value > 0:
        eng.wait_ge(sem, value)


def waits(eng, settled, *pairs):
    if all(isinstance(v, int) for _, v in pairs):
        for sem, value in pairs:
            wait(eng, sem, value)
        return
    values = [(sem, v if isinstance(v, int) else eng.snap(eng.to_reg(v))) for sem, v in pairs]
    eng.wait_ge(*settled)
    for sem, value in values:
        wait(eng, sem, value)


def schedule(eng, body, first, last, rolled=2, stride=3, turns=4):
    for n in range(first, rolled):
        body(batch(n, stride=stride))
    with eng.Fori(0, turns) as i:
        for u in range(stride):
            body(batch(rolled + u, i, stride))
    for n in range(rolled + stride * turns, last + 1):
        body(batch(n, stride=stride))


def cross_attention(nc, x, ctxT, w, X1, csum, consts):
    with ExitStack() as ctx:
        sb = lambda name, shape, dt=F32: ctx.enter_context(nc.sbuf_tensor("a_" + name, shape, dt))
        ps = lambda name: ctx.enter_context(nc.psum_tensor("a_" + name, [128, 512], F32))
        sem = lambda name: nc.alloc_semaphore("a_" + name)
        ring = lambda name, shape, dt=F32: [sb(f"{name}{s}", shape, dt) for s in range(RING)]

        ident, neg_half = consts["ident"], consts["neg_half"]
        Wq, Wk, Wv, Wo = (sb(n_, [128, KC, D]) for n_ in ("Wq", "Wk", "Wv", "Wo"))
        qb, kb = sb("qb", [128, KC]), sb("kb", [128, KC])
        vb, ob = sb("vb", [128, D]), sb("ob", [128, D])
        lamv = sb("lamv", [128, 4, SUB])
        lamp = sb("lamp", [128, 2, SUB])
        lamd, lame, lam = sb("lamd", [128, 2]), sb("lame", [128, 2]), sb("lam", [128, 1])
        gate, tgate = sb("gate", [128, 1]), sb("tgate", [128, 1])
        coef = sb("coef", [128, 4, 4])

        xin = ring("xin", [T, D])
        ctxs = ring("ctx", [128, KC, S])
        Kst = ring("Kst", [ROWS + 2, H, SP_], BF16)
        Qst = ring("Qst", [ROWS + 2, H, 2 * T], BF16)
        V = ring("V", [128, SC, H, 32])
        mx = ring("mx", [T, 2 * H])
        xres = ring("xres", [T, D])
        stats, mv = sb("stats", [T, 6]), sb("mv", [T, 2])
        ve, rstd = sb("ve", [T, 1]), sb("rstd", [T, 1])
        xn, xnT = sb("xn", [T, D]), sb("xnT", [128, KC, T])
        qf = sb("qf", [128, KC, 2, T])
        kf = sb("kf", [128, KC, S])
        qrem, krem = sb("qrem", [128, KC, 2 * T]), sb("krem", [128, KC, S])
        qpart, kpart = sb("qpart", [128, 3, KC, 2 * T], BF16), sb("kpart", [128, 3, KC, S], BF16)
        mrow = [sb(f"mrow{a}", [H, 2, T], BF16) for a in range(2)]
        probs = [sb(f"probs{k}", [128, 4 * T]) for k in range(6)]
        O = sb("O", [128, 4, 2 * T])
        rec, rc = sb("rec", [T, 2, 4, 4]), sb("rc", [T, 2, 4, 4])
        numer = sb("numer", [T, 2, 4, 4, HD])
        attn, attnT = sb("attn", [T, D]), sb("attnT", [128, KC, T])

        pM, pE, pA, pX = ([ps(f"p{c}{s}") for s in range(2)] for c in "MEAX")

        weights_in, gates_in, consts_ok = sem("weights_in"), sem("gates_in"), sem("consts_ok")
        lam_prod, lam_dot, lam_exp, lam_ok, coef_ok = (sem(n_) for n_ in ("lam_prod", "lam_dot", "lam_exp", "lam_ok", "coef_ok"))
        tgate_ok, ob_ok = sem("tgate_ok"), sem("ob_ok")
        x_in = [sem(f"x_in{s}") for s in range(RING)]
        ctx_in = [sem(f"ctx_in{s}") for s in range(RING)]
        res_in = [sem(f"res_in{s}") for s in range(RING)]
        kst_in = [sem(f"kst_in{s}") for s in range(RING)]
        qst_in = [sem(f"qst_in{s}") for s in range(RING)]
        mrow_in = [[sem(f"mrow_in{a}{s}") for s in range(RING)] for a in range(2)]
        ln_steps, rstd_ok, xn_ok = sem("ln_steps"), sem("rstd_ok"), sem("xn_ok")
        csum_ok = sem("csum_ok")
        qsplit, ksplit = sem("qsplit"), sem("ksplit")
        m_filled, m_reduced = sem("m_filled"), sem("m_reduced")
        e_filled, e_done = sem("e_filled"), sem("e_done")
        av_done, o_ok = sem("av_done"), sem("o_ok")
        msplit = [sem(f"msplit{a}") for a in range(2)]
        f_steps = sem("f_steps")
        resb_ok = sem("resb_ok")

        TURNS = [("f0", -1), ("f1", -1), ("p0", 2), ("p1", 2), ("p2", 2), ("f2", -1), ("p3", 2),
                 ("f3", -1), ("p4", 2), ("mA", 1), ("p5", 2), ("p6", 2), ("mB", 1)]
        NAMES = [u for u, _ in TURNS]
        filled = {u: sem("filled_" + u) for u in NAMES}
        taken = {u: sem("taken_" + u) for u in NAMES}
        bank = {u: pX[k % 2] for k, u in enumerate(NAMES)}

        def free_bank(eng, n, u):
            k = NAMES.index(u)
            before = [(n, *t) for t in TURNS[:k]][::-1] + [(later(n, -1), *t) for t in TURNS][::-1]
            for m, name, d in before:
                if bank[name] is bank[u] and exists(later(m, d)):
                    wait(eng, taken[name], count(later(m, d), 1, 1))
                    return

        block = ctx.enter_context(nc.Block())

        @block.sync
        def _(sp):
            loaded = (weights_in, 16 * 7)
            for dst, name in ((Wq, "wq"), (Wk, "wk"), (Wv, "wv"), (Wo, "wo"), (qb, "qb"), (kb, "kb")):
                sp.dma_start(dst[:], w[name]).then_inc(weights_in, 16)
            sp.dma_start(vb[:], w["vb"].partition_broadcast(128)).then_inc(weights_in, 16)
            sp.dma_start(ob[:], w["ob"].partition_broadcast(128)).then_inc(gates_in, 16)
            for k in range(4):
                sp.dma_start(lamv[:, k, :], w["lam"][k].partition_broadcast(128)).then_inc(gates_in, 16)
            sp.dma_start(gate[:], w["gate"].partition_broadcast(128)).then_inc(gates_in, 16)

            def load(n):
                waits(sp, loaded, (xn_ok, count(n, 1, 1 - RING)))
                waits(sp, loaded, (filled["p6"], count(n, 1, 1 - RING)))
                waits(sp, loaded, (csum_ok, count(n, 1, 1 - RING)))
                sp.dma_start(xin[slot(n)][:], x[at(n)]).then_inc(x_in[slot(n)], 16)
                sp.dma_start(ctxs[slot(n)][:], ctxT[at(n)]).then_inc(ctx_in[slot(n)], 16)

            def body(n):
                nF, nM, nP, nL = later(n, -1), later(n, 1), later(n, 2), later(n, 3)
                if exists(nL):
                    load(nL)
                if exists(nF):
                    sp.dma_start(xres[slot(nF)][:], x[at(nF)]).then_inc(res_in[slot(nF)], 16)
                if exists(nP):
                    waits(sp, loaded, (e_filled, count(nP, 24, 24 * (1 - RING))))
                    waits(sp, loaded, (qsplit, count(nP, 4, 4)))
                    for g in range(G):
                        sp.dma_start(Qst[slot(nP)][16 * g:16 * g + 16, :, :], qpart[:, Q_PARTS[g]]).then_inc(qst_in[slot(nP)], 16)
                if exists(nM):
                    rows(nM, 0)
                if exists(nP):
                    waits(sp, loaded, (ksplit, count(nP, 4, 4)))
                    for g in range(G):
                        sp.dma_start(Kst[slot(nP)][16 * g:16 * g + 16, :, 0:S], kpart[:, K_PARTS[g]]).then_inc(kst_in[slot(nP)], 16)
                if exists(nM):
                    rows(nM, 1)

            def rows(n, a):
                waits(sp, loaded, (taken["m" + "AB"[a]], count(n, 1, 1)))
                for r in range(2):
                    sp.dma_start(Qst[slot(n)][ROWS + r:ROWS + r + 1, 8 * a:8 * a + 8, :], mrow[a][:, r, :]).then_inc(mrow_in[a][slot(n)], 16)

            load(batch(0))
            schedule(sp, body, -2, B, rolled=1)

        @block.gpsimd
        def _(pool):
            zeros = [Kst[s][:, :, S:SP_] for s in range(RING)] + [V[s][:] for s in range(RING)] + [qf[:]]
            ones = [Kst[s][ROWS:ROWS + 2, :, 0:S] for s in range(RING)]
            ones += [V[s][0:r, c, :, HD:HD + 1] for s in range(RING) for c, r in enumerate((128, 128, S - 256))]
            for k, part in enumerate(zeros + ones):
                if k:
                    pool.wait_ge(consts_ok, k)
                pool.memset(part, 0.0 if k < len(zeros) else 1.0).then_inc(consts_ok, 1)
            started = (tgate_ok, 1)
            pool.wait_ge(*started)
            pool.tensor_scalar(ob[:], ob[:], tgate[:, 0:1], None, ALU.mult).then_inc(ob_ok, 1)
            pool.wait_ge(ob_ok, 1)

            def split(n, full, rem, part, steps, ready, sent):
                m = later(n, -1)
                waits(pool, started, (ready, count(n, 1, 1)), *([(sent[slot(m)], uses_value(m, 16 * G))] if exists(m) else []))
                src = full[:].rearrange("p c s t -> p c (s t)") if full is qf else full[:]
                pool.tensor_copy(part[:, 0], src).then_inc(steps, 1)
                pool.wait_ge(steps, count(n, 4, 1))
                pool.tensor_tensor(rem[:], src, part[:, 0], ALU.subtract).then_inc(steps, 1)
                waits(pool, started, (steps, count(n, 4, 2)))
                pool.tensor_copy(part[:, 1], rem[:]).then_inc(steps, 1)
                pool.wait_ge(steps, count(n, 4, 3))
                pool.tensor_tensor(part[:, 2], rem[:], part[:, 1], ALU.subtract).then_inc(steps, 1)

            def body(n):
                nF, nP = later(n, -1), later(n, 2)
                if exists(nP):
                    pool.wait_ge(ln_steps, count(nP, 3, 3))
                    pool.tensor_tensor(rstd[:], ve[:], neg_half[0:T, :], ALU.pow).then_inc(rstd_ok, 1)
                if exists(nF):
                    pool.wait_ge(res_in[slot(nF)], uses_value(nF, 16))
                    pool.tensor_tensor(xres[slot(nF)][:], xres[slot(nF)][:], ob[0:T, :], ALU.add).then_inc(resb_ok, 1)
                if exists(nP):
                    split(nP, qf, qrem, qpart, qsplit, taken["p1"], qst_in)
                    split(nP, kf, krem, kpart, ksplit, taken["p3"], kst_in)

            schedule(pool, body, -2, B)

        AT = dict(f0=0, f1=2, p0=3, p1=5, p2=7, f2=8, p3=9, f3=11, p4=12, mA=15, p5=16, p6=18, mB=24)

        @block.tensor
        def _(pe):
            pe.wait_ge(weights_in, 16 * 7)
            pe.wait_ge(consts_ok, 19)

            def use(n, u):
                stage = later(n, dict(TURNS)[u])
                if not exists(stage):
                    return
                free_bank(pe, n, u)
                X = bank[u]
                if u == "p0":
                    pe.wait_ge(xn_ok, count(stage, 1, 1))
                    for c in range(KC):
                        mm = pe.transpose(X[:, T * c:T * (c + 1)], xn[:, 128 * c:128 * (c + 1)], ident[0:T, 0:T])
                elif u == "p1":
                    pe.wait_ge(taken["p0"], count(stage, 1, 1))
                    for m in range(KC):
                        for c in range(KC):
                            mm = pe.matmul(X[:, T * m:T * (m + 1)], Wq[:, c, 128 * m:128 * (m + 1)], xnT[:, c, :], start=(c == 0), stop=(c == KC - 1))
                elif u in ("p2", "p3"):
                    m = int(u[1]) - 2
                    pe.wait_ge(ctx_in[slot(stage)], uses_value(stage, 16))
                    for c in range(KC):
                        mm = pe.matmul(X[:, 0:S], Wk[:, c, 128 * m:128 * (m + 1)], ctxs[slot(stage)][:, c, :], start=(c == 0), stop=(c == KC - 1))
                elif u in ("p4", "p5", "p6"):
                    k = int(u[1]) - 4
                    r = min(128, S - 128 * k)
                    for c in range(KC):
                        mm = pe.matmul(X[0:r, 0:D], ctxs[slot(stage)][:, c, 128 * k:128 * k + r], Wv[:, c, :], start=(c == 0), stop=(c == KC - 1))
                elif u in ("mA", "mB"):
                    a = "AB".index(u[1])
                    pe.wait_ge(m_reduced, count(stage, 32, 16 * (a + 1)))
                    mm = pe.transpose(X[0:16, 0:T], mx[slot(stage)][:, 16 * a:16 * a + 16], ident[0:T, 0:T])
                elif u in ("f0", "f1"):
                    f = int(u[1])
                    pe.wait_ge(o_ok, count(stage, 4, 2 * f + 2))
                    for q in range(2):
                        for s in range(2):
                            k = 2 * q + s
                            mm = pe.transpose(X[0:T, 128 * k:128 * (k + 1)], O[:, 2 * f + q, T * s:T * (s + 1)], ident[:])
                elif u == "f2":
                    pe.wait_ge(f_steps, count(stage, 6, 6))
                    for c in range(KC):
                        mm = pe.transpose(X[:, T * c:T * (c + 1)], attn[:, 128 * c:128 * (c + 1)], ident[0:T, 0:T])
                elif u == "f3":
                    pe.wait_ge(taken["f2"], count(stage, 1, 1))
                    for c in range(KC):
                        mm = pe.matmul(X[0:T, 0:D], attnT[:, c, :], Wo[:, c, :], start=(c == 0), stop=(c == KC - 1))
                mm.then_inc(filled[u], 1)

            def e_tile(n, k):
                q, c, half = k // 6, k % 6 // 2, k % 2
                if k in (0, 12):
                    pe.wait_ge(mrow_in[k // 12][slot(n)], uses_value(n, 32))
                wait(pe, e_done, count(n, 24, k - 1))
                for j in range(2):
                    h = 4 * q + 2 * half + j
                    mm = pe.matmul(pE[k % 2][:, 2 * T * j:2 * T * (j + 1)], Kst[slot(n)][:, h, 128 * c:128 * (c + 1)],
                                   Qst[slot(n)][:, h, :], start=True, stop=True)
                mm.then_inc(e_filled, 1)

            def m_tile(n, j):
                if j == 0:
                    pe.wait_ge(qst_in[slot(n)], uses_value(n, 16 * G))
                    pe.wait_ge(kst_in[slot(n)], uses_value(n, 16 * G))
                wait(pe, m_reduced, count(n, 32, j - 1))
                pe.matmul(pM[j % 2][0:T, 0:S], Qst[slot(n)][0:ROWS, j // 2, T * (j % 2):T * (j % 2 + 1)],
                          Kst[slot(n)][0:ROWS, j // 2, 0:S], start=True, stop=True).then_inc(m_filled, 1)

            def av(n, g):
                q, c = g // 3, g % 3
                if g == 0:
                    pe.wait_ge(taken["p6"], count(n, 1, 1))
                if c == 0:
                    wait(pe, o_ok, count(n, 4, q - 1))
                pe.wait_ge(e_done, count(n, 24, 2 * g + 2))
                for j in range(4):
                    mm = pe.matmul(pA[q % 2][32 * j:32 * j + 32, 0:2 * T], V[slot(n)][:, c, 4 * q + j, :],
                                   probs[(2 * g + j // 2) % 6][:, 2 * T * (j % 2):2 * T * (j % 2 + 1)],
                                   start=(c == 0), stop=(c == SC - 1))
                mm.then_inc(av_done, 1)

            def body(n):
                for k in range(24):
                    if exists(n):
                        e_tile(n, k)
                    if exists(later(n, 1)):
                        for j in range(4 * k // 3, 4 * (k + 1) // 3):
                            m_tile(later(n, 1), j)
                    if exists(n) and k % 2 and k >= 3:
                        av(n, k // 2 - 1)
                    for u in NAMES:
                        if AT[u] == k:
                            use(n, u)
                if exists(n):
                    av(n, 11)
                use(n, "mB")

            schedule(pe, body, -2, B)

        @block.vector
        def _(dve):
            dve.wait_ge(gates_in, 16 * 6)
            dve.tensor_tensor(lamp[:], lamv[:, 0:4:2, :], lamv[:, 1:4:2, :], ALU.mult).then_inc(lam_prod, 1)
            dve.wait_ge(lam_prod, 1)
            dve.tensor_reduce(lamd[:], lamp[:], AX.X, ALU.add).then_inc(lam_dot, 1)
            dve.wait_ge(lam_exp, 1)
            dve.tensor_tensor(lam[:], lame[:, 1:2], lame[:, 0:1], ALU.subtract).then_inc(lam_ok, 1)
            dve.wait_ge(lam_ok, 1)
            dve.tensor_scalar(lam[:], lam[:], -LAMBDA_INIT, 1.0 - LAMBDA_INIT, ALU.add, ALU.mult).then_inc(lam_ok, 1)
            dve.memset(coef[:], 1.0 - LAMBDA_INIT).then_inc(coef_ok, 1)
            dve.wait_ge(lam_ok, 2)
            dve.wait_ge(coef_ok, 1)
            dve.tensor_scalar(coef[:, 1:4:2, :], coef[:, 1:4:2, :], 0.0, lam[:, 0:1], ALU.mult, ALU.add).then_inc(coef_ok, 1)
            dve.wait_ge(coef_ok, 2)
            loaded = (weights_in, 16 * 7)
            dve.wait_ge(*loaded)
            dve.wait_ge(consts_ok, 19)

            def norm(n):
                s = slot(n)
                dve.wait_ge(x_in[s], uses_value(n, 16))
                dve.bn_stats(stats[:], xin[s][:]).then_inc(ln_steps, 1)
                waits(dve, loaded, (ln_steps, count(n, 3, 1)))
                dve.bn_aggr(mv[:], stats[:]).then_inc(ln_steps, 1)
                dve.wait_ge(ln_steps, count(n, 3, 2))
                dve.tensor_scalar(ve[:], mv[:, 1:2], EPS, None, ALU.add).then_inc(ln_steps, 1)

            def norm_end(n):
                dve.wait_ge(rstd_ok, count(n, 1, 1))
                wait(dve, filled["p0"], count(n, 1, 0))
                dve.tensor_scalar(xn[:], xin[slot(n)][:], mv[:, 0:1], rstd[:, 0:1], ALU.subtract, ALU.mult).then_inc(xn_ok, 1)

            def take(n, u):
                stage = later(n, dict(TURNS)[u])
                if not exists(stage):
                    return
                X = bank[u]
                dve.wait_ge(filled[u], count(stage, 1, 1))
                if u == "p1":
                    wait(dve, qsplit, count(stage, 4, 0))
                    for s in range(2):
                        r = slice(64 * s, 64 * s + 64)
                        ins = dve.tensor_tensor(qf[r, :, s, :], X[r, 0:2 * T].rearrange("p (c t) -> p c t", c=KC),
                                                qb[r, :].unsqueeze(2).broadcast_to([64, KC, T]), ALU.add)
                    ins.then_inc(taken[u], 1)
                elif u in ("p4", "p5", "p6"):
                    k = int(u[1]) - 4
                    r = min(128, S - 128 * k)
                    wait(dve, av_done, count(stage, 12, 12 * (1 - RING)))
                    dve.tensor_tensor(V[slot(stage)][0:r, k, :, 0:HD], X[0:r, 0:D].rearrange("p (h d) -> p h d", h=H),
                                      vb[0:r, :].rearrange("p (h d) -> p h d", h=H), ALU.add).then_inc(taken[u], 1)
                elif u in ("mA", "mB"):
                    a = "AB".index(u[1])
                    m = later(stage, -1)
                    if exists(m):
                        dve.wait_ge(mrow_in[a][slot(m)], uses_value(m, 32))
                    dve.tensor_scalar(mrow[a][:, 0, :], X[0:16, 0:T], -1.0, None, ALU.mult).then_inc(msplit[a], 1)
                    dve.wait_ge(msplit[a], count(stage, 1, 1))
                    dve.scalar_tensor_tensor(mrow[a][:, 1, :], X[0:16, 0:T], -1.0, mrow[a][:, 0, :], ALU.mult, ALU.subtract).then_inc(taken[u], 1)
                elif u in ("f0", "f1"):
                    f = int(u[1])
                    sums = X[0:T, :].rearrange("p (k j d) -> p k j d", k=4, j=4)
                    dve.reciprocal(rec[:, f], sums[:, :, :, HD]).then_inc(f_steps, 1)
                    dve.wait_ge(f_steps, count(stage, 6, 3 * f + 1))
                    dve.tensor_tensor(rc[:, f], rec[:, f], coef[0:T], ALU.mult).then_inc(f_steps, 1)
                    dve.wait_ge(f_steps, count(stage, 6, 3 * f + 2))
                    dve.tensor_tensor(numer[:, f], sums[:, :, :, 0:HD], rc[:, f].unsqueeze(3).broadcast_to([T, 4, 4, HD]), ALU.mult).then_inc(taken[u], 1)
                    dve.wait_ge(taken[u], count(stage, 1, 1))
                    two = numer[:, f].rearrange("p (q s) j d -> p q s (j d)", s=2)
                    dve.tensor_tensor(attn[:, 128 * f:128 * f + 128].rearrange("p (q x) -> p q x", q=2),
                                      two[:, :, 0], two[:, :, 1], ALU.add).then_inc(f_steps, 1)
                elif u == "f3":
                    dve.wait_ge(resb_ok, count(stage, 1, 1))
                    dve.scalar_tensor_tensor(at_batch(X1, stage), X[0:T, 0:D], tgate[0:T, 0:1], xres[slot(stage)][:], ALU.mult, ALU.add).then_inc(taken[u], 1)

            def body(n):
                nM, nP = later(n, 1), later(n, 2)
                if exists(nP):
                    norm(nP)
                for k in range(25):
                    for u in ("f0", "f1", "p1", "f3", "p4", "mA", "p5", "p6", "mB"):
                        if AT[u] == k - 1:
                            take(n, u)
                    if k == 1 and exists(nP):
                        norm_end(nP)
                    if k == 10 and exists(nP):
                        dve.wait_ge(ctx_in[slot(nP)], uses_value(nP, 16))
                        dve.tensor_reduce(csum[:, :, at(nP)], ctxs[slot(nP)][:], AX.X, ALU.add).then_inc(csum_ok, 1)
                    if k < 24 and exists(nM):
                        for j in range(4 * k // 3, 4 * (k + 1) // 3):
                            dve.wait_ge(m_filled, count(nM, 32, j + 1))
                            dve.tensor_reduce(mx[slot(nM)][:, j:j + 1], pM[j % 2][0:T, 0:S], AX.X, ALU.max).then_inc(m_reduced, 1)
                take(n, "mB")

            schedule(dve, body, -2, B)

        @block.scalar
        def _(act):
            act.wait_ge(lam_dot, 1)
            act.activation(lame[:], lamd[:], ACT.Exp).then_inc(lam_exp, 1)
            act.activation(tgate[:], gate[:], ACT.Tanh).then_inc(tgate_ok, 1)
            act.wait_ge(weights_in, 16 * 7)

            def take(n, u):
                stage = later(n, dict(TURNS)[u])
                if not exists(stage):
                    return
                X = bank[u]
                act.wait_ge(filled[u], count(stage, 1, 1))
                if u == "p0":
                    wait(act, filled["p1"], count(stage, 1, 0))
                    act.activation(xnT[:].rearrange("p c t -> p (c t)"), X[:, 0:KC * T], ACT.Copy).then_inc(taken[u], 1)
                elif u in ("p2", "p3"):
                    m = int(u[1]) - 2
                    wait(act, ksplit, count(stage, 4, 0))
                    ins = act.activation(kf[:, m, :], X[:, 0:S], ACT.Identity, bias=kb[:, m:m + 1])
                    ins.then_inc(taken[u], 1)
                elif u == "f2":
                    wait(act, filled["f3"], count(stage, 1, 0))
                    act.activation(attnT[:].rearrange("p c t -> p (c t)"), X[:, 0:KC * T], ACT.Copy).then_inc(taken[u], 1)

            def sums_out(n, q):
                act.wait_ge(av_done, count(n, 12, 3 * q + 3))
                wait(act, filled["f0" if q < 2 else "f1"], count(n, 1, 0))
                act.activation(O[:, q, :], pA[q % 2][:, 0:2 * T], ACT.Copy).then_inc(o_ok, 1)

            def body(n):
                for k in range(24):
                    for u in ("p0", "p2", "p3", "f2"):
                        if AT[u] == k - 1:
                            take(n, u)
                    if exists(n):
                        if k >= 8 and k % 6 == 2:
                            sums_out(n, k // 6 - 1)
                        act.wait_ge(e_filled, count(n, 24, k + 1))
                        wait(act, av_done, count(n, 12, (k - 6) // 2 + 1))
                        act.activation(probs[k % 6][:], pE[k % 2][:, 0:4 * T], ACT.Exp, scale=SCALING).then_inc(e_done, 1)
                if exists(n):
                    sums_out(n, 3)

            schedule(act, body, -2, B)


def constants(nc, ctx, gates, tables):
    sb = lambda name, shape, dt=F32: ctx.enter_context(nc.sbuf_tensor("c_" + name, shape, dt))
    made = nc.alloc_semaphore("c_made")
    c = dict(ident=sb("ident", [128, 128]), identb=sb("identb", [128, 128], BF16), neg_half=sb("neg_half", [128, 1]),
             far_s=sb("far_s", [T, 4 * T], BF16), far_t=sb("far_t", [T, 4 * T], BF16), behind=sb("behind", [T, T]),
             before=sb("before", [T, T]), ones=sb("ones", [T, T]), floor=sb("floor", [128, 1]),
             numbers=sb("numbers", [T, E1_BLOCKS]), zero=sb("zero", [128, 1024]), tgates=sb("tgates", [128, 4]))
    whole = sb("whole", [T, E1_BLOCKS], mybir.dt.int32)
    gates_in, gates_ok = nc.alloc_semaphore("c_gates_in"), nc.alloc_semaphore("c_gates_ok")
    c["tables_zero"] = nc.alloc_semaphore("c_tables_zero")
    FAR = -1.0e30
    starts = dict(ident=0.0, identb=0.0, neg_half=-0.5, far_s=0.0, far_t=0.0, behind=1.0, before=1.0, ones=1.0, floor=0.0, zero=0.0)
    with nc.Block() as block:
        @block.gpsimd
        def _(pool):
            for name, value in starts.items():
                pool.memset(c[name][:], value).then_inc(made, 1)
            pool.wait_ge(made, len(starts))
            four = lambda name: c[name][:].rearrange("p (h t) -> p h t", h=4)
            selects = [(c["ident"][:], [[-1, 128]], 1, 0, ALU.not_equal, 1.0),
                       (c["identb"][:], [[-1, 128]], 1, 0, ALU.not_equal, 1.0),
                       (four("far_s"), [[0, 4], [-1, T]], 1, 0, ALU.is_ge, FAR),
                       (four("far_t"), [[0, 4], [1, T]], -1, 0, ALU.is_ge, FAR),
                       (c["behind"][:], [[-1, T]], 1, 0, ALU.is_gt, 0.0),
                       (c["before"][:], [[1, T]], -1, 0, ALU.is_gt, 0.0),
                       (c["floor"][:], [[0, 1]], -1, T - 2, ALU.is_ge, -3.0e38)]
            for out, pattern, factor, base, compare, other in selects:
                pool.affine_select(out=out, in_=out, compare_op=compare, fill=other, base=base, pattern=pattern,
                                   channel_multiplier=factor).then_inc(made, 1)
            pool.iota(whole[:], pattern=[[1, E1_BLOCKS]], base=0, channel_multiplier=0).then_inc(made, 1)
            pool.wait_ge(made, len(starts) + len(selects) + 1)
            pool.tensor_copy(c["numbers"][:], whole[:]).then_inc(made, 1)
            pool.wait_ge(made, len(starts) + len(selects) + 2)

        @block.scalar
        def _(act):
            act.dma_start(c["tgates"][:], gates.partition_broadcast(128)).then_inc(gates_in, 16)
            act.wait_ge(gates_in, 16)
            act.activation(c["tgates"][:], c["tgates"][:], ACT.Tanh).then_inc(gates_ok, 1)
            act.wait_ge(gates_ok, 1)

        @block.sync
        def _(sp):
            sp.wait_ge(made, len(starts))
            for table in tables:
                rows = table.rearrange("(p k) d -> p (k d)", p=128)
                for a in range(0, rows.shape[1], 1024):
                    b = min(a + 1024, rows.shape[1])
                    sp.dma_start(rows[:, a:b], c["zero"][:, 0:b - a]).then_inc(c["tables_zero"], 16)
    return c


def self_attention(nc, w, X1, EMB, HID, RL, consts):
    run = dict(rolled=2, stride=BRING, turns=2)
    bslot = lambda n: slot(n, BRING)
    with ExitStack() as ctx:
        sb = lambda name, shape, dt=F32: ctx.enter_context(nc.sbuf_tensor("b_" + name, shape, dt))
        ps = lambda name: ctx.enter_context(nc.psum_tensor("b_" + name, [128, 512], F32))
        sem = lambda name: nc.alloc_semaphore("b_" + name)
        ring = lambda name, shape, dt=F32: [sb(f"{name}{s}", shape, dt) for s in range(BRING)]

        ident, identb, neg_half = consts["ident"], consts["identb"], consts["neg_half"]
        far_s, far_t = consts["far_s"], consts["far_t"]
        behind, floor = consts["behind"], consts["floor"]
        Wq, Wk, Wv = (sb(n_, [128, KC, D]) for n_ in ("Wq", "Wk", "Wv"))
        Wr = sb("Wr", [128, KC, 8])
        qkb, vb, rb = sb("qkb", [128, 2 * KC]), sb("vb", [128, D]), sb("rb", [128, 8])

        Kst = ring("Kst", [ROWS + 3, H, T], BF16)
        Qst = ring("Qst", [ROWS + 3, H, T], BF16)
        V = ring("V", [T, H, 32])
        mxr = ring("mxr", [T, H])
        mx = ring("mx", [T, H])
        stats, mv = sb("stats", [T, 6]), sb("mv", [T, 2])
        ve, rstd = sb("ve", [T, 1]), sb("rstd", [T, 1])
        xn, xnT = sb("xn", [T, D]), sb("xnT", [128, KC, T])
        qk, rem = sb("qk", [128, 2 * KC, T]), sb("rem", [128, 2 * KC, T])
        part = sb("part", [128, 3, 2 * KC, T], BF16)
        mrow, mrem = sb("mrow", [H, 3, T], BF16), sb("mrem", [H, T])
        probs = [sb(f"probs{k}", [T, 4 * T]) for k in range(4)]
        O = sb("O", [128, 4, T])
        expm = sb("expm", [T, H])
        later_sum, total = sb("later_sum", [T, H, HD + 1]), sb("total", [T, H, HD + 1])
        rec = sb("rec", [T, H])
        hid, hidT = sb("hid", [T, D]), sb("hidT", [128, KC, T])

        pM, pE, pA, pX = ([ps(f"p{c}{s}") for s in range(2)] for c in "MEAX")

        weights_in, consts_ok = sem("weights_in"), sem("consts_ok")
        qst_in = [sem(f"qst_in{s}") for s in range(BRING)]
        kst_in = [sem(f"kst_in{s}") for s in range(BRING)]
        mrow_in = [sem(f"mrow_in{s}") for s in range(BRING)]
        ln_steps, rstd_ok, xn_ok = sem("ln_steps"), sem("rstd_ok"), sem("xn_ok")
        split_steps = sem("split_steps")
        m_filled, m_reduced, m_floored, m_steps = sem("m_filled"), sem("m_reduced"), sem("m_floored"), sem("m_steps")
        e_filled, e_done, av_done, o_ok = sem("e_filled"), sem("e_done"), sem("av_done"), sem("o_ok")
        expm_ok, f_steps, hid_kept = sem("expm_ok"), sem("f_steps"), sem("hid_kept")

        TURNS = [("f1", -1), ("f0", -1), ("p0", 3), ("p1", 3), ("mA", 1), ("f2", -1), ("p2", 3), ("f3", -1)]
        NAMES = [u for u, _ in TURNS]
        filled = {u: sem("filled_" + u) for u in NAMES}
        taken = {u: sem("taken_" + u) for u in NAMES}
        bank = {u: pX[k % 2] for k, u in enumerate(NAMES)}

        def free_bank(eng, n, u):
            k = NAMES.index(u)
            before = [(n, *t) for t in TURNS[:k]][::-1] + [(later(n, -1), *t) for t in TURNS][::-1]
            for m, name, d in before:
                if bank[name] is bank[u] and exists(later(m, d)):
                    wait(eng, taken[name], count(later(m, d), 1, 1))
                    return

        block = ctx.enter_context(nc.Block())
        LOADS = 7

        @block.sync
        def _(sp):
            loaded = (weights_in, 16 * LOADS)
            for dst, name in ((Wq, "wq"), (Wk, "wk"), (Wv, "wv"), (Wr, "wr"), (qkb, "qkb")):
                sp.dma_start(dst[:], w[name]).then_inc(weights_in, 16)
            sp.dma_start(vb[:], w["vb"].partition_broadcast(128)).then_inc(weights_in, 16)
            sp.dma_start(rb[:], w["rb"].partition_broadcast(128)).then_inc(weights_in, 16)

            def body(n):
                nM, nP = later(n, 1), later(n, 3)
                if exists(nM):
                    waits(sp, loaded, (m_steps, count(nM, 3, 3)))
                    for r in range(3):
                        sp.dma_start(Qst[bslot(nM)][ROWS + r:ROWS + r + 1, :, :], mrow[:, r, :]).then_inc(mrow_in[bslot(nM)], 16)
                if exists(nP):
                    waits(sp, loaded, (e_filled, count(nP, 4, 4 * (1 - BRING))), (split_steps, count(nP, 4, 4)))
                    for g in range(G):
                        sp.dma_start(Qst[bslot(nP)][16 * g:16 * g + 16, :, :], part[:, Q_PARTS[g], 0:KC]).then_inc(qst_in[bslot(nP)], 16)
                        sp.dma_start(Kst[bslot(nP)][16 * g:16 * g + 16, :, :], part[:, K_PARTS[g], KC:2 * KC]).then_inc(kst_in[bslot(nP)], 16)

            schedule(sp, body, -3, B, **run)

        @block.gpsimd
        def _(pool):
            inits = [(Kst[s][ROWS:ROWS + 3, :, :], 1.0) for s in range(BRING)] + [(V[s][:], 0.0) for s in range(BRING)]
            inits += [(V[s][:, :, HD:HD + 1], 1.0) for s in range(BRING)]
            for k, (out, value) in enumerate(inits):
                if k:
                    pool.wait_ge(consts_ok, k)
                pool.memset(out, value).then_inc(consts_ok, 1)
            started = (consts_ok, len(inits))
            pool.wait_ge(*started)

            def body(n):
                nF, nP = later(n, -1), later(n, 3)
                if exists(nP):
                    pool.wait_ge(ln_steps, count(nP, 3, 3))
                    pool.tensor_tensor(rstd[:], ve[:], neg_half[0:T, :], ALU.pow).then_inc(rstd_ok, 1)
                if exists(nF):
                    waits(pool, started, (f_steps, count(nF, 4, 4)))
                    pool.tensor_copy(at_batch(HID, nF), hid[:]).then_inc(hid_kept, 1)
                if exists(nP):
                    for k in range(2):
                        pool.wait_ge(split_steps, count(nP, 4, 2 * k + 1))
                        out = part[:, 2] if k else rem[:]
                        pool.tensor_tensor(out, rem[:] if k else qk[:], part[:, k], ALU.subtract).then_inc(split_steps, 1)

            schedule(pool, body, -3, B, **run)

        @block.tensor
        def _(pe):
            pe.wait_ge(weights_in, 16 * LOADS)
            pe.wait_ge(consts_ok, 3 * BRING)

            def use(n, u):
                stage = later(n, dict(TURNS)[u])
                if not exists(stage):
                    return
                free_bank(pe, n, u)
                X = bank[u]
                if u == "p0":
                    pe.wait_ge(xn_ok, count(stage, 1, 1))
                    for c in range(KC):
                        mm = pe.transpose(X[:, T * c:T * (c + 1)], xn[:, 128 * c:128 * (c + 1)], ident[0:T, 0:T])
                elif u == "p1":
                    pe.wait_ge(taken["p0"], count(stage, 1, 1))
                    for k, W in enumerate((Wq, Wk)):
                        for m in range(KC):
                            for c in range(KC):
                                mm = pe.matmul(X[:, T * (KC * k + m):T * (KC * k + m + 1)], W[:, c, 128 * m:128 * (m + 1)], xnT[:, c, :],
                                               start=(c == 0), stop=(c == KC - 1))
                elif u == "p2":
                    for c in range(KC):
                        mm = pe.matmul(X[0:T, 0:D], xnT[:, c, :], Wv[:, c, :], start=(c == 0), stop=(c == KC - 1))
                elif u == "mA":
                    pe.wait_ge(m_floored, count(stage, 1, 1))
                    mm = pe.transpose(X[0:H, 0:T], mx[bslot(stage)][:], ident[0:T, 0:T])
                elif u == "f0":
                    pe.wait_ge(o_ok, count(stage, 2, 2))
                    for q in range(4):
                        mm = pe.transpose(X[0:T, 128 * q:128 * (q + 1)], O[:, q, :], ident[:])
                elif u == "f1":
                    mm = pe.matmul(X[0:T, 0:H * (HD + 1)], behind[:], V[bslot(stage)][:, :, 0:HD + 1], start=True, stop=True)
                elif u == "f2":
                    pe.wait_ge(f_steps, count(stage, 4, 4))
                    for c in range(KC):
                        mm = pe.transpose(X[:, T * c:T * (c + 1)], hid[:, 128 * c:128 * (c + 1)], ident[0:T, 0:T])
                elif u == "f3":
                    pe.wait_ge(taken["f2"], count(stage, 1, 1))
                    for c in range(KC):
                        mm = pe.matmul(X[0:T, 0:8], hidT[:, c, :], Wr[:, c, :], start=(c == 0), stop=(c == KC - 1))
                mm.then_inc(filled[u], 1)

            def m_tile(n, k):
                if k == 0:
                    pe.wait_ge(qst_in[bslot(n)], uses_value(n, 16 * G))
                    pe.wait_ge(kst_in[bslot(n)], uses_value(n, 16 * G))
                wait(pe, m_reduced, count(n, 4, k - 1))
                pe.matmul(pM[k % 2][0:T, 0:4 * T], identb[0:T, 0:T], far_s[:], start=True, stop=True)
                for j in range(4):
                    mm = pe.matmul(pM[k % 2][0:T, T * j:T * (j + 1)], Qst[bslot(n)][0:ROWS, 4 * k + j, :],
                                   Kst[bslot(n)][0:ROWS, 4 * k + j, :], start=False, stop=True, skip_group_check=True)
                mm.then_inc(m_filled, 1)

            def e_tile(n, k):
                if k == 0:
                    pe.wait_ge(mrow_in[bslot(n)], uses_value(n, 48))
                wait(pe, e_done, count(n, 4, k - 1))
                pe.matmul(pE[k % 2][0:T, 0:4 * T], identb[0:T, 0:T], far_t[:], start=True, stop=True)
                for j in range(4):
                    mm = pe.matmul(pE[k % 2][0:T, T * j:T * (j + 1)], Kst[bslot(n)][:, 4 * k + j, :],
                                   Qst[bslot(n)][:, 4 * k + j, :], start=False, stop=True, skip_group_check=True)
                mm.then_inc(e_filled, 1)

            def av(n, q):
                if q < 2:
                    wait(pe, o_ok, count(n, 2, q - 1))
                if q == 0:
                    pe.wait_ge(taken["p2"], count(n, 1, 1))
                pe.wait_ge(e_done, count(n, 4, q + 1))
                for j in range(4):
                    mm = pe.matmul(pA[q % 2][32 * j:32 * j + 32, T * (q // 2):T * (q // 2 + 1)], V[bslot(n)][:, 4 * q + j, :],
                                   probs[q][:, T * j:T * (j + 1)], start=True, stop=True)
                mm.then_inc(av_done, 1)

            def body(n):
                for step in ("m0 m1 f1 f0 m2 m3 p0 e0 p1 mA e1 f2 a0 p2 e2 a1 f3 e3 a2 a3").split():
                    k = int(step[1]) if step != "mA" else None
                    if step in NAMES:
                        use(n, step)
                    elif step[0] == "m":
                        if exists(later(n, 1)):
                            m_tile(later(n, 1), k)
                    elif exists(n):
                        (e_tile if step[0] == "e" else av)(n, k)

            schedule(pe, body, -3, B, **run)

        @block.vector
        def _(dve):
            loaded = (weights_in, 16 * LOADS)
            dve.wait_ge(*loaded)
            dve.wait_ge(consts_ok, 3 * BRING)

            def norm(n):
                dve.bn_stats(stats[:], at_batch(X1, n)).then_inc(ln_steps, 1)
                waits(dve, loaded, (ln_steps, count(n, 3, 1)))
                dve.bn_aggr(mv[:], stats[:]).then_inc(ln_steps, 1)
                dve.wait_ge(ln_steps, count(n, 3, 2))
                dve.tensor_scalar(ve[:], mv[:, 1:2], EPS, None, ALU.add).then_inc(ln_steps, 1)

            def norm_end(n):
                dve.wait_ge(rstd_ok, count(n, 1, 1))
                wait(dve, filled["p0"], count(n, 1, 0))
                dve.tensor_scalar(xn[:], at_batch(X1, n), mv[:, 0:1], rstd[:, 0:1], ALU.subtract, ALU.mult).then_inc(xn_ok, 1)
                dve.tensor_scalar(at_batch(EMB, n), at_batch(X1, n), mv[:, 0:1], rstd[:, 0:1], ALU.subtract, ALU.mult)

            def take(n, u):
                stage = later(n, dict(TURNS)[u])
                if not exists(stage):
                    return
                X = bank[u]
                dve.wait_ge(filled[u], count(stage, 1, 1))
                if u == "p1":
                    wait(dve, split_steps, count(stage, 4, 0))
                    dve.tensor_tensor(qk[:], X[:, 0:4 * T].rearrange("p (c t) -> p c t", t=T),
                                      qkb[:].unsqueeze(2).broadcast_to([128, 2 * KC, T]), ALU.add).then_inc(taken[u], 1)
                elif u == "p2":
                    wait(dve, av_done, count(stage, 4, 4 * (1 - BRING)))
                    wait(dve, filled["f1"], count(stage, 1, 1 - BRING))
                    dve.tensor_tensor(V[bslot(stage)][:, :, 0:HD], X[0:T, 0:D].rearrange("p (h d) -> p h d", h=H),
                                      vb[0:T, :].rearrange("p (h d) -> p h d", h=H), ALU.add).then_inc(taken[u], 1)
                elif u == "mA":
                    m = later(stage, -1)
                    if exists(m):
                        dve.wait_ge(mrow_in[bslot(m)], uses_value(m, 48))
                    dve.tensor_scalar(mrow[:, 0, :], X[0:H, 0:T], -1.0, None, ALU.mult).then_inc(m_steps, 1)
                    dve.wait_ge(m_steps, count(stage, 3, 1))
                    dve.scalar_tensor_tensor(mrem[:], X[0:H, 0:T], -1.0, mrow[:, 0, :], ALU.mult, ALU.subtract).then_inc(taken[u], 1)
                    waits(dve, loaded, (taken[u], count(stage, 1, 1)))
                    dve.tensor_copy(mrow[:, 1, :], mrem[:]).then_inc(m_steps, 1)
                    dve.wait_ge(m_steps, count(stage, 3, 2))
                    dve.tensor_tensor(mrow[:, 2, :], mrem[:], mrow[:, 1, :], ALU.subtract).then_inc(m_steps, 1)
                elif u == "f1":
                    dve.wait_ge(expm_ok, count(stage, 1, 1))
                    dve.tensor_tensor(later_sum[:], X[0:T, 0:H * (HD + 1)].rearrange("p (h d) -> p h d", h=H),
                                      expm[:].unsqueeze(2).broadcast_to([T, H, HD + 1]), ALU.mult).then_inc(taken[u], 1)
                elif u == "f0":
                    dve.wait_ge(taken["f1"], count(stage, 1, 1))
                    wait(dve, filled["f2"], count(stage, 1, 0))
                    wait(dve, hid_kept, count(stage, 1, 0))
                    dve.tensor_tensor(total[:], X[0:T, :].rearrange("p (h d) -> p h d", h=H)[:, :, 0:HD + 1],
                                      later_sum[:], ALU.add).then_inc(taken[u], 1)
                    dve.wait_ge(taken[u], count(stage, 1, 1))
                    dve.reciprocal(rec[:], total[:, :, HD]).then_inc(f_steps, 2)
                    dve.wait_ge(f_steps, count(stage, 4, 2))
                    dve.tensor_tensor(hid[:].rearrange("p (h d) -> p h d", h=H), total[:, :, 0:HD],
                                      rec[:].unsqueeze(2).broadcast_to([T, H, HD]), ALU.mult).then_inc(f_steps, 2)
                elif u == "f3":
                    dve.tensor_tensor(at_batch(RL, stage), X[0:T, 0:8], rb[0:T, :], ALU.add).then_inc(taken[u], 1)

            def body(n):
                nM, nP = later(n, 1), later(n, 3)

                def reduce(k):
                    if exists(nM):
                        dve.wait_ge(m_filled, count(nM, 4, k + 1))
                        dve.tensor_reduce(mxr[bslot(nM)][:, 4 * k:4 * k + 4], pM[k % 2][0:T, 0:4 * T].rearrange("p (h t) -> p h t", h=4),
                                          AX.X, ALU.max).then_inc(m_reduced, 1)

                if exists(nP):
                    norm(nP)
                reduce(0)
                if exists(nP):
                    norm_end(nP)
                reduce(1)
                take(n, "f1")
                take(n, "f0")
                reduce(2)
                reduce(3)
                if exists(nM):
                    dve.wait_ge(m_reduced, count(nM, 4, 4))
                    dve.tensor_scalar(mx[bslot(nM)][:], mxr[bslot(nM)][:], floor[0:T, 0:1], None, ALU.max).then_inc(m_floored, 1)
                take(n, "p1")
                take(n, "mA")
                take(n, "p2")
                take(n, "f3")

            schedule(dve, body, -3, B, **run)

        @block.scalar
        def _(act):
            def take(n, u):
                stage = later(n, dict(TURNS)[u])
                if not exists(stage):
                    return
                act.wait_ge(filled[u], count(stage, 1, 1))
                wait(act, filled["p2" if u == "p0" else "f3"], count(stage, 1, 0))
                out = xnT if u == "p0" else hidT
                act.activation(out[:].rearrange("p c t -> p (c t)"), bank[u][:, 0:KC * T], ACT.Copy).then_inc(taken[u], 1)

            def exp_tile(n, k):
                act.wait_ge(e_filled, count(n, 4, k + 1))
                wait(act, av_done, count(n, 4, k - 3))
                act.activation(probs[k][:], pE[k % 2][0:T, 0:4 * T], ACT.Exp, scale=D ** -0.5).then_inc(e_done, 1)

            def split(n, k):
                m = later(n, -1)
                if k == 0:
                    act.wait_ge(taken["p1"], count(n, 1, 1))
                    if exists(m):
                        act.wait_ge(qst_in[bslot(m)], uses_value(m, 16 * G))
                        act.wait_ge(kst_in[bslot(m)], uses_value(m, 16 * G))
                else:
                    act.wait_ge(split_steps, count(n, 4, 2))
                act.activation(part[:, k], rem[:] if k else qk[:], ACT.Copy).then_inc(split_steps, 1)

            def body(n):
                nF, nP = later(n, -1), later(n, 3)
                if exists(nF):
                    wait(act, taken["f1"], count(nF, 1, 0))
                    act.activation(expm[:], mx[bslot(nF)][:], ACT.Exp, scale=-D ** -0.5).then_inc(expm_ok, 1)
                take(n, "p0")
                if exists(n):
                    exp_tile(n, 0)
                if exists(nP):
                    split(nP, 0)
                if exists(n):
                    exp_tile(n, 1)
                if exists(nP):
                    split(nP, 1)
                take(n, "f2")
                if exists(n):
                    exp_tile(n, 2)
                    exp_tile(n, 3)
                    for a in range(2):
                        act.wait_ge(av_done, count(n, 4, a + 3))
                        wait(act, filled["f0"], count(n, 1, 0))
                        act.activation(O[:, a:4:2, :], pA[a][:, 0:2 * T].rearrange("p (q t) -> p q t", q=2), ACT.Copy).then_inc(o_ok, 1)

            schedule(act, body, -3, B, **run)


def chain(eng, sem):
    done = [0]

    def link(ins):
        done[0] += 1
        ins.then_inc(sem, 1)
        eng.wait_ge(sem, done[0])
    return link


def per_expert(t):
    return t.unsqueeze(2).broadcast_to([T, B, E])


def per_batch(t):
    return t.unsqueeze(1).broadcast_to([T, B, E])


def first_max(dve, link, logits, top, onehot, work, best, falling):
    link(dve.tensor_reduce(top[:], logits, AX.X, ALU.max))
    link(dve.tensor_tensor(work[:], logits, per_expert(top[:]), ALU.is_equal))
    link(dve.tensor_tensor(work[:], work[:], per_batch(falling[:]), ALU.mult))
    link(dve.tensor_reduce(best[:], work[:], AX.X, ALU.max))
    link(dve.tensor_tensor(onehot[:], work[:], per_expert(best[:]), ALU.is_equal))


def running_count(dve, link, totals, bufs):
    a, b = bufs
    link(dve.memset(a[:, 0:1, :], 0.0))
    link(dve.tensor_copy(a[:, 1:B, :], totals[:, 0:B - 1, :]))
    for d in (1, 2, 4, 8):
        link(dve.tensor_copy(b[:, 0:d, :], a[:, 0:d, :]))
        link(dve.tensor_tensor(b[:, d:B, :], a[:, d:B, :], a[:, 0:B - d, :], ALU.add))
        a, b = b, a


def first_mixture(nc, w, EMB, HID, RL, table, done_table, weight_kept, consts):
    U32 = mybir.dt.uint32
    with ExitStack() as ctx:
        sb = lambda name, shape, dt=F32: ctx.enter_context(nc.sbuf_tensor("r_" + name, shape, dt))
        ps = lambda name: ctx.enter_context(nc.psum_tensor("r_" + name, [128, 512], F32))
        sem = lambda name: nc.alloc_semaphore("r_" + name)
        top, best = sb("top", [T, B]), sb("best", [T, B])
        falling, base = sb("falling", [T, E]), sb("base", [T, E])
        onehot, chosen, work, diff, expd = (sb(n_, [T, B, E]) for n_ in ("onehot", "chosen", "work", "diff", "expd"))
        counts = [sb(f"counts{k}", [T, B, E]) for k in range(2)]
        rank = sb("rank", [T, B, E])
        total, prob, kept, lost, row = (sb(n_, [T, B]) for n_ in ("total", "prob", "kept", "lost", "row"))
        to_row, from_row = sb("to_row", [T, B], U32), sb("from_row", [T, B], U32)
        We, be = sb("We", [128, E, KC, D]), sb("be", [128, E, D])
        xs = [sb(f"xs{h}", [HALF, D]) for h in range(4)]
        xT = [sb(f"xT{h}", [128, KC, HALF]) for h in range(2)]
        ys = [sb(f"ys{h}", [HALF, D]) for h in range(2)]
        pR, pT, pY = ps("pR"), [ps(f"pT{h}") for h in range(2)], [ps(f"pY{h}") for h in range(2)]

        we_in, steps, onehot_ok, ranked, diff_ok, exp_ok = (sem(n_) for n_ in ("we_in", "steps", "onehot_ok", "ranked", "diff_ok", "exp_ok"))
        rows_ok, sent, passed, got = sem("rows_ok"), sem("sent"), sem("passed"), sem("got")
        xs_in = [sem(f"xs_in{h}") for h in range(4)]
        y_out = [sem(f"y_out{h}") for h in range(2)]
        turned, xT_ok, y_ok, ys_ok = sem("turned"), sem("xT_ok"), sem("y_ok"), sem("ys_ok")
        BLOCKS = 2 * E
        run = dict(first=-2, last=BLOCKS - 1, rolled=2, stride=4, turns=3)
        block = ctx.enter_context(nc.Block())

        @block.sync
        def _(sp):
            sp.dma_start(We[:], w["we"]).then_inc(we_in, 16)
            sp.dma_start(be[:].rearrange("p e d -> p (e d)"), w["be"].partition_broadcast(128)).then_inc(we_in, 16)
            sp.wait_ge(sent, 16 * B)
            ready = (sent, 16 * B)

            def body(n):
                nL = later(n, 2)
                if exists(nL, BLOCKS):
                    waits(sp, ready, (turned, count(nL, 1, -3)))
                    sp.dma_start(xs[slot(nL, 4)][:], table[at(nL, HALF), :]).then_inc(xs_in[slot(nL, 4)], 16)
                if exists(n, BLOCKS):
                    waits(sp, ready, (ys_ok, count(n, 1, 1)))
                    sp.dma_start(done_table[at(n, HALF), :], ys[slot(n, 2)][:]).then_inc(y_out[slot(n, 2)], 16)

            schedule(sp, body, **run)

        @block.scalar
        def _(act):
            act.wait_ge(diff_ok, 1)
            act.activation(expd[:], diff[:], ACT.Exp).then_inc(exp_ok, 1)

            def body(n):
                nL = later(n, 1)
                if exists(nL, BLOCKS):
                    act.wait_ge(turned, count(nL, 1, 1))
                    wait(act, y_ok, count(nL, 1, -1))
                    act.activation(xT[slot(nL, 2)][:].rearrange("p c t -> p (c t)"), pT[slot(nL, 2)][:, 0:KC * HALF], ACT.Copy).then_inc(xT_ok, 1)

            schedule(act, body, **run)

        @block.tensor
        def _(pe):
            pe.wait_ge(onehot_ok, 1)
            chosen_ = chosen[:].rearrange("p b e -> p (b e)")
            pe.matmul(pR[0:T, 0:B * E], consts["before"][:], chosen_, start=True, stop=True)
            pe.matmul(pR[0:T, B * E:2 * B * E], consts["ones"][:], chosen_, start=True, stop=True).then_inc(ranked, 1)
            pe.wait_ge(we_in, 32)

            def body(n):
                nL = later(n, 1)
                if exists(nL, BLOCKS):
                    pe.wait_ge(xs_in[slot(nL, 4)], uses_value(nL, 16))
                    wait(pe, xT_ok, count(nL, 1, -1))
                    for c in range(KC):
                        mm = pe.transpose(pT[slot(nL, 2)][:, HALF * c:HALF * (c + 1)], xs[slot(nL, 4)][:, 128 * c:128 * (c + 1)],
                                          consts["ident"][0:HALF, 0:HALF])
                    mm.then_inc(turned, 1)
                if exists(n, BLOCKS):
                    pe.wait_ge(xT_ok, count(n, 1, 1))
                    wait(pe, ys_ok, count(n, 1, -1))
                    e = uses(n, 2)
                    for c in range(KC):
                        mm = pe.matmul(pY[slot(n, 2)][0:HALF, 0:D], xT[slot(n, 2)][:, c, :],
                                       We[:].rearrange("p e c f -> p (e c f)")[:, bass.ds((e * KC + c) * D, D)], start=(c == 0), stop=(c == KC - 1))
                    mm.then_inc(y_ok, 1)

            schedule(pe, body, **run)

        @block.vector
        def _(dve):
            link = chain(dve, steps)
            numbers = consts["numbers"]
            link(dve.tensor_scalar(falling[:], numbers[:, 0:E], -1.0, float(E), ALU.mult, ALU.add))
            link(dve.tensor_scalar(base[:], numbers[:, 0:E], float(CAP), None, ALU.mult))
            first_max(dve, link, RL[:], top, onehot, work, best, falling)
            dve.tensor_tensor(diff[:], RL[:], per_expert(top[:]), ALU.subtract).then_inc(diff_ok, 1)
            dve.tensor_copy(chosen[:], onehot[:]).then_inc(onehot_ok, 1)
            dve.wait_ge(ranked, 1)
            ranks = pR[0:T, :].rearrange("p (k b e) -> p k b e", k=4, b=B)
            running_count(dve, link, ranks[:, 1], counts)
            link(dve.tensor_tensor(rank[:], ranks[:, 0], counts[0][:], ALU.add))
            link(dve.tensor_scalar(work[:], rank[:], float(CAP), None, ALU.is_lt))
            link(dve.tensor_tensor(work[:], work[:], onehot[:], ALU.mult))
            link(dve.tensor_reduce(kept[:], work[:], AX.X, ALU.add))
            link(dve.tensor_tensor(work[:], rank[:], per_batch(base[:]), ALU.add))
            link(dve.tensor_tensor(work[:], work[:], onehot[:], ALU.mult))
            link(dve.tensor_reduce(row[:], work[:], AX.X, ALU.add))
            link(dve.tensor_tensor(total[:], row[:], kept[:], ALU.mult))
            link(dve.tensor_copy(from_row[:], total[:]))
            link(dve.tensor_scalar(lost[:], kept[:], -float(4 * B * T), float(4 * B * T), ALU.mult, ALU.add))
            link(dve.tensor_tensor(row[:], row[:], lost[:], ALU.add))
            dve.tensor_copy(to_row[:], row[:]).then_inc(rows_ok, 1)
            dve.wait_ge(exp_ok, 1)
            link(dve.tensor_reduce(total[:], expd[:], AX.X, ALU.add))
            link(dve.reciprocal(prob[:], total[:]))
            link(dve.tensor_tensor(weight_kept[:], prob[:], kept[:], ALU.mult))
            link(dve.tensor_tensor(lost[:], prob[:], weight_kept[:], ALU.subtract))
            for b in range(B):
                dve.scalar_tensor_tensor(EMB[:, b, :], HID[:, b, :], lost[:, b:b + 1], EMB[:, b, :], ALU.mult, ALU.add).then_inc(passed, 1)

            dve.wait_ge(we_in, 32)

            def body(n):
                if exists(n, BLOCKS):
                    dve.wait_ge(y_ok, count(n, 1, 1))
                    m = later(n, -2)
                    if exists(m, BLOCKS):
                        dve.wait_ge(y_out[slot(m, 2)], uses_value(m, 16, 2))
                    e = uses(n, 2)
                    dve.tensor_tensor(ys[slot(n, 2)][:], pY[slot(n, 2)][0:HALF, 0:D],
                                      be[0:HALF].rearrange("p e f -> p (e f)")[:, bass.ds(e * D, D)], ALU.add).then_inc(ys_ok, 1)

            schedule(dve, body, **run)

        @block.gpsimd
        def _(pool):
            pool.wait_ge(rows_ok, 1)
            pool.wait_ge(consts["tables_zero"], consts["tables_zero_value"])
            for b in range(B):
                pool.indirect_dma_start(table, bass.IndirectOffsetOnAxis(ap=to_row[:, b:b + 1], axis=0), HID[:, b, :], None,
                                        bounds_check=E * CAP - 1, oob_is_err=False).then_inc(sent, 16)
            pool.wait_ge(sent, 16 * B)
            for h in range(2):
                pool.wait_ge(y_out[h], 16 * E)
            for b in range(B):
                pool.wait_ge(passed, b + 1)
                pool.indirect_dma_start(HID[:, b, :], None, done_table, bass.IndirectOffsetOnAxis(ap=from_row[:, b:b + 1], axis=0)).then_inc(got, 16)
            pool.wait_ge(got, 16 * B)


def middle(nc, w, X, EMB, HID, RL, csum, weight_kept, part_dram, consts):
    with ExitStack() as ctx:
        sb = lambda name, shape, dt=F32: ctx.enter_context(nc.sbuf_tensor("m_" + name, shape, dt))
        ps = lambda name: ctx.enter_context(nc.psum_tensor("m_" + name, [128, 512], F32))
        sem = lambda name: nc.alloc_semaphore("m_" + name)
        tg, neg_half, ident = consts["tgates"], consts["neg_half"], consts["ident"]
        gamma, beta = sb("gamma", [128, D]), sb("beta", [128, D])
        W1, W2, Wr, b1 = sb("W1", [128, KC, D]), sb("W2", [128, KC, D]), sb("Wr", [128, KC, E]), sb("b1", [128, D])
        part, stats = sb("part", [B, D]), sb("stats", [T, B, 6])
        mean = [sb(f"mean{k}", [T, B]) for k in range(3)]
        apart = sb("apart", [T, B])
        ve = [sb(f"ve{k}", [T, B]) for k in range(3)]
        rstd = [sb(f"rstd{k}", [T, B]) for k in range(3)]
        temp = [sb(f"temp{h}", [T, D]) for h in range(2)]
        xn = [[sb(f"xn{k}{h}", [T, D]) for h in range(2)] for k in range(2)]
        xnT = [[sb(f"xnT{k}{h}", [128, KC, T]) for h in range(2)] for k in range(2)]
        pT, pY, pP = [ps(f"pT{h}") for h in range(2)], [ps(f"pY{h}") for h in range(2)], ps("pP")

        w_in, shifted, part_ps, part_ok, part_out, part_in = (sem(n_) for n_ in ("w_in", "shifted", "part_ps", "part_ok", "part_out", "part_in"))
        scaled, gb_ok, y_read, ve_ok, rstd_ok = sem("scaled"), sem("gb_ok"), sem("y_read"), sem("ve_ok"), sem("rstd_ok")
        stat_ok, steps, x2_steps, x3_base = sem("stat_ok"), sem("steps"), sem("x2_steps"), sem("x3_base")
        xn_ok, turned, xnT_ok, mm_ok, taken, kept = ([sem(f"{n_}{k}") for k in range(2)] for n_ in ("xn_ok", "turned", "xnT_ok", "mm_ok", "taken", "kept"))
        run = dict(first=0, last=B - 1, rolled=2, stride=2, turns=7)
        block = ctx.enter_context(nc.Block())

        def one(t, n):
            return t[:, at(n)]

        @block.sync
        def _(sp):
            for dst, name in ((W1, "w1"), (W2, "w2"), (Wr, "wr2")):
                sp.dma_start(dst[:], w[name]).then_inc(w_in, 16)
            for dst, name in ((b1, "b1"), (gamma, "gamma"), (beta, "beta")):
                sp.dma_start(dst[:], w[name].partition_broadcast(128)).then_inc(w_in, 16)
            sp.wait_ge(part_ok, 2)
            sp.dma_start(part_dram, part[:]).then_inc(part_out, 16)
            sp.wait_ge(part_out, 16)
            sp.wait_ge(y_read, B)
            sp.dma_start(HID[:].rearrange("p b d -> p (b d)"), part_dram.rearrange("b d -> (b d)").partition_broadcast(T)).then_inc(part_in, 16)

        @block.gpsimd
        def _(pool):
            pool.wait_ge(w_in, 16 * 6)
            pool.tensor_scalar(gamma[:], gamma[:], tg[:, 2:3], None, ALU.mult).then_inc(gb_ok, 1)
            pool.tensor_scalar(beta[:], beta[:], tg[:, 2:3], None, ALU.mult).then_inc(gb_ok, 1)
            pool.wait_ge(gb_ok, 2)
            for b in range(B):
                pool.tensor_tensor(X[:, b, :], X[:, b, :], beta[0:T, :], ALU.add).then_inc(shifted, 1)
            pool.wait_ge(ve_ok, 1)
            pool.tensor_tensor(rstd[0][:], ve[0][:], neg_half[0:T, :].broadcast_to([T, B]), ALU.pow).then_inc(rstd_ok, 1)
            pool.wait_ge(ve_ok, 2)
            pool.tensor_tensor(rstd[1][:], ve[1][:], neg_half[0:T, :].broadcast_to([T, B]), ALU.pow).then_inc(rstd_ok, 1)
            pool.wait_ge(part_in, 16)

            def add_part(n):
                pool.wait_ge(xn_ok[0], count(n, 1, 1))
                pool.tensor_tensor(at_batch(X, n), at_batch(X, n), at_batch(HID, n), ALU.add).then_inc(x3_base, 1)

            schedule(pool, add_part, **run)
            pool.wait_ge(ve_ok, 3)
            pool.tensor_tensor(rstd[2][:], ve[2][:], neg_half[0:T, :].broadcast_to([T, B]), ALU.pow).then_inc(rstd_ok, 1)
            started = (part_in, 16)

            def keep(n):
                waits(pool, started, (xn_ok[1], count(n, 1, 1)))
                pool.tensor_copy(at_batch(EMB, n), xn[1][slot(n, 2)][:]).then_inc(kept[1], 1)

            schedule(pool, keep, **run)

        @block.tensor
        def _(pe):
            pe.wait_ge(w_in, 16 * 6)
            for c in range(KC):
                mm = pe.matmul(pP[0:B, 0:D], csum[:, c, :], W2[:, c, :], start=(c == 0), stop=(c == KC - 1))
            mm.then_inc(part_ps, 1)
            for k in range(2):
                def turn(n):
                    pe.wait_ge(xn_ok[k], count(n, 1, 1))
                    wait(pe, xnT_ok[k], count(n, 1, -1))
                    for c in range(KC):
                        mm = pe.transpose(pT[slot(n, 2)][:, T * c:T * (c + 1)], xn[k][slot(n, 2)][:, 128 * c:128 * (c + 1)], ident[0:T, 0:T])
                    mm.then_inc(turned[k], 1)

                def multiply(n):
                    W, width = ((W1, D), (Wr, E))[k]
                    pe.wait_ge(xnT_ok[k], count(n, 1, 1))
                    wait(pe, taken[k], count(n, 1, -1))
                    for c in range(KC):
                        mm = pe.matmul(pY[slot(n, 2)][0:T, 0:width], xnT[k][slot(n, 2)][:, c, :], W[:, c, :], start=(c == 0), stop=(c == KC - 1))
                    mm.then_inc(mm_ok[k], 1)

                def body(n):
                    if n[0] is not None or n[1] + 1 < B:
                        turn(later(n, 1))
                    multiply(n)

                if k == 1:
                    pe.wait_ge(taken[0], B)
                turn(batch(0, stride=2))
                schedule(pe, body, 0, B - 1, rolled=1, stride=2, turns=7)

        @block.scalar
        def _(act):
            act.wait_ge(w_in, 16 * 6)
            for k in range(2):
                def body(n):
                    act.wait_ge(turned[k], count(n, 1, 1))
                    wait(act, mm_ok[k], count(n, 1, -1))
                    act.activation(xnT[k][slot(n, 2)][:].rearrange("p c t -> p (c t)"), pT[slot(n, 2)][:, 0:KC * T], ACT.Copy).then_inc(xnT_ok[k], 1)

                schedule(act, body, **run)

        @block.vector
        def _(dve):
            ready = (w_in, 16 * 6)
            dve.wait_ge(*ready)
            dve.wait_ge(part_ps, 1)
            dve.scalar_tensor_tensor(part[:], pP[0:B, 0:D], 1.0 / S, b1[0:B, :], ALU.mult, ALU.add).then_inc(part_ok, 1)
            dve.wait_ge(part_ok, 1)
            dve.tensor_scalar(part[:], part[:], tg[0:B, 1:2], None, ALU.mult).then_inc(part_ok, 1)

            def statistics(n, k, source):
                dve.bn_stats(at_batch(stats, n), source).then_inc(stat_ok, 1)

            link = chain(dve, steps)

            def variance(k):
                dve.wait_ge(stat_ok, B * (k + 1))
                link(dve.tensor_tensor(apart[:], stats[:, :, 1], stats[:, :, 4], ALU.subtract))
                link(dve.tensor_tensor(mean[k][:], stats[:, :, 1], stats[:, :, 4], ALU.add))
                link(dve.tensor_scalar(mean[k][:], mean[k][:], 0.5, None, ALU.mult))
                link(dve.tensor_tensor(ve[k][:], stats[:, :, 2], stats[:, :, 5], ALU.add))
                link(dve.tensor_scalar(ve[k][:], ve[k][:], 1.0 / D, EPS, ALU.mult, ALU.add))
                link(dve.scalar_tensor_tensor(apart[:], apart[:], 0.25, apart[:], ALU.mult, ALU.mult))
                dve.tensor_tensor(ve[k][:], ve[k][:], apart[:], ALU.add).then_inc(ve_ok, 1)

            def sums(n):
                dve.scalar_tensor_tensor(at_batch(EMB, n), at_batch(HID, n), one(weight_kept, n), at_batch(EMB, n), ALU.mult, ALU.add).then_inc(y_read, 1)
                dve.wait_ge(y_read, count(n, 1, 1))
                statistics(n, 0, at_batch(EMB, n))

            schedule(dve, sums, **run)
            variance(0)
            dve.wait_ge(shifted, B)
            dve.wait_ge(gb_ok, 2)
            dve.wait_ge(rstd_ok, 1)

            def second(n):
                t = temp[slot(n, 2)]
                dve.scalar_tensor_tensor(t[:], at_batch(EMB, n), one(mean[0], n), gamma[0:T, :], ALU.subtract, ALU.mult).then_inc(x2_steps, 1)
                dve.wait_ge(x2_steps, count(n, 2, 1))
                dve.scalar_tensor_tensor(at_batch(X, n), t[:], one(rstd[0], n), at_batch(X, n), ALU.mult, ALU.add).then_inc(x2_steps, 1)
                dve.wait_ge(x2_steps, count(n, 2, 2))
                statistics(n, 1, at_batch(X, n))

            schedule(dve, second, **run)
            variance(1)
            dve.wait_ge(rstd_ok, 2)

            def normalise(n, k):
                wait(dve, turned[k], count(n, 1, -1))
                if k == 1:
                    wait(dve, kept[1], count(n, 1, -1))
                dve.tensor_scalar(xn[k][slot(n, 2)][:], at_batch(X, n), one(mean[k + 1], n), one(rstd[k + 1], n), ALU.subtract, ALU.mult).then_inc(xn_ok[k], 1)

            def third(n):
                if n[0] is not None or n[1] + 1 < B:
                    normalise(later(n, 1), 0)
                dve.wait_ge(mm_ok[0], count(n, 1, 1))
                dve.wait_ge(x3_base, count(n, 1, 1))
                dve.scalar_tensor_tensor(at_batch(X, n), pY[slot(n, 2)][0:T, 0:D], tg[0:T, 1:2], at_batch(X, n), ALU.mult, ALU.add).then_inc(taken[0], 1)
                dve.wait_ge(taken[0], count(n, 1, 1))
                statistics(n, 2, at_batch(X, n))

            normalise(batch(0, stride=2), 0)
            schedule(dve, third, 0, B - 1, rolled=1, stride=2, turns=7)
            variance(2)
            dve.wait_ge(rstd_ok, 3)

            def fourth(n):
                if n[0] is not None or n[1] + 1 < B:
                    normalise(later(n, 1), 1)
                waits(dve, ready, (mm_ok[1], count(n, 1, 1)))
                dve.tensor_copy(at_batch(RL, n), pY[slot(n, 2)][0:T, 0:E]).then_inc(taken[1], 1)

            normalise(batch(0, stride=2), 1)
            schedule(dve, fourth, 0, B - 1, rolled=1, stride=2, turns=7)


def second_mixture(nc, w, Ws, X, EMB, HID, RL, table, done_table, out, consts):
    U32, I32 = mybir.dt.uint32, mybir.dt.int32
    W13, W2s, ws_in, ws_value = Ws
    with ExitStack() as ctx:
        sb = lambda name, shape, dt=F32: ctx.enter_context(nc.sbuf_tensor("t_" + name, shape, dt))
        ps = lambda name: ctx.enter_context(nc.psum_tensor("t_" + name, [128, 512], F32))
        sem = lambda name: nc.alloc_semaphore("t_" + name)
        NB, HC = E1_BLOCKS, HID2 // 128
        SIZES = (B * T + 127) // 128
        top = [sb(f"top{k}", [T, B]) for k in range(2)]
        best, falling = sb("best", [T, B]), sb("falling", [T, E])
        onehot = [sb(f"onehot{k}", [T, B, E]) for k in range(2)]
        work, masked, both, rank = (sb(n_, [T, B, E]) for n_ in ("work", "masked", "both", "rank"))
        counts = [sb(f"counts{k}", [T, B, E]) for k in range(2)]
        limits, over = sb("limits", [T, SIZES]), sb("over", [T, E, SIZES])
        sizes, nblocks, base = sb("sizes", [T, E]), sb("nblocks", [T, E]), sb("base", [T, E])
        ends = [sb(f"ends{k}", [T, E]) for k in range(2)]
        ended, idf, ids = sb("ended", [T, NB, E]), sb("idf", [T, NB]), sb("ids", [T, NB], I32)
        gap, ratio = sb("gap", [T, B]), sb("ratio", [T, B])
        factor = [sb(f"factor{k}", [T, B]) for k in range(2)]
        row = [sb(f"row{k}", [T, B]) for k in range(2)]
        rows = [sb(f"rows{k}", [T, B], U32) for k in range(2)]
        xs = [sb(f"xs{h}", [128, D]) for h in range(4)]
        xT = [sb(f"xT{h}", [128, KC, 128]) for h in range(2)]
        silu = [sb(f"silu{h}", [128, HID2]) for h in range(2)]
        act_ = [sb(f"act{h}", [128, HID2]) for h in range(2)]
        aT = [sb(f"aT{h}", [128, HC, 128]) for h in range(2)]
        ys = [sb(f"ys{h}", [128, D]) for h in range(2)]
        pT, pH, pG, pY = ([ps(f"p{c}{h}") for h in range(2)] for c in "THGY")

        steps, gap_ok, ratio_ok, both_ok, ranked, ids_ok, rows_ok = (sem(n_) for n_ in ("steps", "gap_ok", "ratio_ok", "both_ok", "ranked", "ids_ok", "rows_ok"))
        sent, summed, out_done = sem("sent"), sem("summed"), sem("out_done")
        got = [sem(f"got{k}") for k in range(2)]
        xs_in = [sem(f"xs_in{h}") for h in range(4)]
        y_out = [sem(f"y_out{h}") for h in range(2)]
        turned, xT_ok, h_ok, g_ok, silu_ok, act_ok = (sem(n_) for n_ in ("turned", "xT_ok", "h_ok", "g_ok", "silu_ok", "act_ok"))
        aturned, aT_ok, y_ok, ys_ok = (sem(n_) for n_ in ("aturned", "aT_ok", "y_ok", "ys_ok"))
        run = dict(first=-2, last=NB, rolled=2, stride=4, turns=(NB - 4) // 4)
        block = ctx.enter_context(nc.Block())

        @block.sync
        def _(sp):
            sp.wait_ge(sent, 16 * 2 * B)
            ready = (sent, 16 * 2 * B)

            def body(n):
                nL, nY = later(n, 2), later(n, -1)
                if exists(nL, NB):
                    waits(sp, ready, (turned, count(nL, 1, -3)))
                    sp.dma_start(xs[slot(nL, 4)][:], table[at(nL, 128), :]).then_inc(xs_in[slot(nL, 4)], 16)
                if exists(nY, NB):
                    waits(sp, ready, (ys_ok, count(nY, 1, 1)))
                    sp.dma_start(done_table[at(nY, 128), :], ys[slot(nY, 2)][:]).then_inc(y_out[slot(nY, 2)], 16)

            schedule(sp, body, **run)
            for b in range(B):
                sp.wait_ge(summed, 2 * (b + 1))
                sp.dma_start(out[b], X[:, b, :]).then_inc(out_done, 16)
            sp.wait_ge(out_done, 16 * B)

        @block.gpsimd
        def _(pool):
            pool.wait_ge(rows_ok, 2)
            for b in range(B):
                for k in range(2):
                    pool.indirect_dma_start(table, bass.IndirectOffsetOnAxis(ap=rows[k][:, b:b + 1], axis=0), EMB[:, b, :], None,
                                            bounds_check=NB * 128 - 1, oob_is_err=False).then_inc(sent, 16)
            pool.wait_ge(sent, 16 * 2 * B)
            for h in range(2):
                pool.wait_ge(y_out[h], 16 * NB // 2)
            for b in range(B):
                for k, to in enumerate((HID, EMB)):
                    pool.indirect_dma_start(to[:, b, :], None, done_table, bass.IndirectOffsetOnAxis(ap=rows[k][:, b:b + 1], axis=0)).then_inc(got[k], 16)
            for k in range(2):
                pool.wait_ge(got[k], 16 * B)

        @block.tensor
        def _(pe):
            pe.wait_ge(both_ok, 1)
            chosen = both[:].rearrange("p b e -> p (b e)")
            pe.matmul(pY[0][0:T, 0:B * E], consts["before"][:], chosen, start=True, stop=True)
            pe.matmul(pY[0][0:T, B * E:2 * B * E], consts["ones"][:], chosen, start=True, stop=True).then_inc(ranked, 1)
            pe.wait_ge(ids_ok, 1)
            pe.wait_ge(ws_in, ws_value)
            up, down = W13[:].rearrange("p e k c f -> p (e k c f)"), W2s[:].rearrange("p e c f -> p (e c f)")

            def expert(n):
                return pe.value_load(ids[0:1, at(n)], min_val=0, max_val=E - 1)

            def body(n):
                nL, nY = later(n, 1), later(n, -1)
                if exists(nY, NB):
                    s = slot(nY, 2)
                    pe.wait_ge(act_ok, count(nY, 1, 1))
                    pe.wait_ge(xT_ok, count(nY, 1, 1))
                    for c in range(HC):
                        mm = pe.transpose(pT[s][:, 128 * c:128 * (c + 1)], act_[s][:, 128 * c:128 * (c + 1)], consts["ident"][:])
                    mm.then_inc(aturned, 1)
                if exists(n, NB):
                    s = slot(n, 2)
                    e = expert(n)
                    pe.wait_ge(xT_ok, count(n, 1, 1))
                    wait(pe, act_ok, count(n, 1, -1))
                    for k, (P, ok) in enumerate(((pH[s], h_ok), (pG[s], g_ok))):
                        for c in range(KC):
                            mm = pe.matmul(P[:, 0:HID2], xT[s][:, c, :], up[:, bass.ds(e * (2 * KC * HID2) + (k * KC + c) * HID2, HID2)],
                                           start=(c == 0), stop=(c == KC - 1))
                        mm.then_inc(ok, 1)
                if exists(nY, NB):
                    s = slot(nY, 2)
                    e = expert(nY)
                    pe.wait_ge(aT_ok, count(nY, 1, 1))
                    wait(pe, ys_ok, count(nY, 1, -1))
                    for c in range(HC):
                        mm = pe.matmul(pY[s][:, 0:D], aT[s][:, c, :], down[:, bass.ds(e * (HC * D) + c * D, D)], start=(c == 0), stop=(c == HC - 1))
                    mm.then_inc(y_ok, 1)
                if exists(nL, NB):
                    pe.wait_ge(xs_in[slot(nL, 4)], uses_value(nL, 16))
                    wait(pe, aT_ok, count(nL, 1, -1))
                    for c in range(KC):
                        mm = pe.transpose(pT[slot(nL, 2)][:, 128 * c:128 * (c + 1)], xs[slot(nL, 4)][:, 128 * c:128 * (c + 1)], consts["ident"][:])
                    mm.then_inc(turned, 1)

            schedule(pe, body, **run)

        @block.scalar
        def _(act):
            act.wait_ge(gap_ok, 1)
            act.activation(ratio[:], gap[:], ACT.Exp).then_inc(ratio_ok, 1)

            def body(n):
                nL, nY = later(n, 1), later(n, -1)
                if exists(nY, NB):
                    s = slot(nY, 2)
                    act.wait_ge(aturned, count(nY, 1, 1))
                    wait(act, y_ok, count(nY, 1, -1))
                    act.activation(aT[s][:].rearrange("p c t -> p (c t)"), pT[s][:, 0:HC * 128], ACT.Copy).then_inc(aT_ok, 1)
                if exists(n, NB):
                    s = slot(n, 2)
                    act.wait_ge(h_ok, count(n, 1, 1))
                    wait(act, act_ok, count(n, 1, -1))
                    act.activation(silu[s][:], pH[s][:, 0:HID2], ACT.Silu).then_inc(silu_ok, 1)
                if exists(nL, NB):
                    s = slot(nL, 2)
                    act.wait_ge(turned, count(nL, 1, 1))
                    wait(act, g_ok, count(nL, 1, -1))
                    act.activation(xT[s][:].rearrange("p c t -> p (c t)"), pT[s][:, 0:KC * 128], ACT.Copy).then_inc(xT_ok, 1)

            schedule(act, body, **run)

        @block.vector
        def _(dve):
            link = chain(dve, steps)
            numbers = consts["numbers"]
            link(dve.tensor_scalar(falling[:], numbers[:, 0:E], -1.0, float(E), ALU.mult, ALU.add))
            first_max(dve, link, RL[:], top[0], onehot[0], work, best, falling)
            link(dve.scalar_tensor_tensor(masked[:], onehot[0][:], -3.0e38, RL[:], ALU.mult, ALU.add))
            first_max(dve, link, masked[:], top[1], onehot[1], work, best, falling)
            dve.tensor_tensor(both[:], onehot[0][:], onehot[1][:], ALU.add).then_inc(both_ok, 1)
            dve.tensor_tensor(gap[:], top[1][:], top[0][:], ALU.subtract).then_inc(gap_ok, 1)
            dve.wait_ge(ratio_ok, 1)
            link(dve.tensor_scalar(work[:, :, 0], ratio[:], 1.0, None, ALU.add))
            link(dve.reciprocal(factor[0][:], work[:, :, 0]))
            link(dve.tensor_scalar(factor[0][:], factor[0][:], consts["tgates"][0:T, 3:4], None, ALU.mult))
            link(dve.tensor_tensor(factor[1][:], factor[0][:], ratio[:], ALU.mult))
            dve.wait_ge(ranked, 1)
            ranks = pY[0][0:T, :].rearrange("p (k b e) -> p k b e", k=4, b=B)
            running_count(dve, link, ranks[:, 1], counts)
            link(dve.tensor_tensor(rank[:], ranks[:, 0], counts[0][:], ALU.add))
            link(dve.tensor_tensor(sizes[:], ranks[:, 1, B - 1], counts[0][:, B - 1], ALU.add))
            link(dve.tensor_scalar(limits[:], numbers[:, 0:SIZES], 128.0, None, ALU.mult))
            link(dve.tensor_tensor(over[:], sizes[:].unsqueeze(2).broadcast_to([T, E, SIZES]), limits[:].unsqueeze(1).broadcast_to([T, E, SIZES]), ALU.is_gt))
            link(dve.tensor_reduce(nblocks[:], over[:], AX.X, ALU.add))
            a, b_ = nblocks, ends[0]
            for d in (1, 2, 4):
                link(dve.tensor_copy(b_[:, 0:d], a[:, 0:d]))
                link(dve.tensor_tensor(b_[:, d:E], a[:, d:E], a[:, 0:E - d], ALU.add))
                a, b_ = b_, ends[1] if b_ is ends[0] else ends[0]
            end = a
            link(dve.tensor_tensor(base[:], end[:], nblocks[:], ALU.subtract))
            link(dve.tensor_scalar(base[:], base[:], 128.0, None, ALU.mult))
            link(dve.tensor_tensor(rank[:], rank[:], per_batch(base[:]), ALU.add))
            for k in range(2):
                link(dve.tensor_tensor(work[:], rank[:], onehot[k][:], ALU.mult))
                link(dve.tensor_reduce(row[k][:], work[:], AX.X, ALU.add))
                dve.tensor_copy(rows[k][:], row[k][:]).then_inc(rows_ok, 1)
            link(dve.tensor_tensor(ended[:], end[:].unsqueeze(1).broadcast_to([T, NB, E]), numbers[:, 0:NB].unsqueeze(2).broadcast_to([T, NB, E]), ALU.is_le))
            link(dve.tensor_reduce(idf[:], ended[:], AX.X, ALU.add))
            link(dve.tensor_scalar(idf[:], idf[:], float(E - 1), None, ALU.min))
            dve.tensor_copy(ids[:], idf[:]).then_inc(ids_ok, 1)
            ready = (rows_ok, 2)

            def body(n):
                nY = later(n, -1)
                if exists(n, NB):
                    s = slot(n, 2)
                    dve.wait_ge(silu_ok, count(n, 1, 1))
                    dve.wait_ge(g_ok, count(n, 1, 1))
                    wait(dve, aturned, count(n, 1, -1))
                    dve.tensor_tensor(act_[s][:], silu[s][:], pG[s][:, 0:HID2], ALU.mult).then_inc(act_ok, 1)
                if exists(nY, NB):
                    s, m = slot(nY, 2), later(nY, -2)
                    pairs = [(y_ok, count(nY, 1, 1))]
                    if m[0] is not None or m[1] >= 0:
                        pairs.append((y_out[slot(m, 2)], uses_value(m, 16, 2)))
                    waits(dve, ready, *pairs)
                    dve.tensor_copy(ys[s][:], pY[s][:, 0:D]).then_inc(ys_ok, 1)

            schedule(dve, body, **run)
            for b in range(B):
                for k, y in enumerate((HID, EMB)):
                    dve.wait_ge(got[k], 16 * B)
                    if k:
                        dve.wait_ge(summed, 2 * b + 1)
                    dve.scalar_tensor_tensor(X[:, b, :], y[:, b, :], factor[k][:, b:b + 1], X[:, b, :], ALU.mult, ALU.add).then_inc(summed, 1)


def build(nc, a, out):
    with ExitStack() as ctx:
        sb = lambda name, shape, dt=F32: ctx.enter_context(nc.sbuf_tensor(name, shape, dt))
        dram = lambda name, shape: nc.dram_tensor(name, shape, F32, kind="Internal").ap()
        table0, done0 = dram("table0", [E * CAP, D]), dram("done0", [E * CAP, D])
        table1, done1 = dram("table1", [E1_BLOCKS * 128, D]), dram("done1", [E1_BLOCKS * 128, D])
        part_dram = dram("part", [B, D])
        csum = sb("csum", [128, KC, B])
        X, EMB, HID = sb("X", [T, B, D]), sb("EMB", [T, B, D]), sb("HID", [T, B, D])
        RL, weight_kept = sb("RL", [T, B, E]), sb("weight_kept", [T, B])
        consts = constants(nc, ctx, a["gates"], (table0, table1))
        consts["tables_zero_value"] = 16 * (4 + 8)
        group = lambda prefix: {k[len(prefix):]: v for k, v in a.items() if k.startswith(prefix)}
        with nc.cleanup_on_exit():
            cross_attention(nc, a["x"], a["ctxT"], group("a_"), X, csum, consts)
        W13, W2s = sb("W13", [128, E, 2, KC, HID2]), sb("W2s", [128, E, HID2 // 128, D])
        ws_in = nc.alloc_semaphore("ws_in")
        with nc.Block() as block:
            @block.sync
            def _(sp):
                sp.dma_start(W13[:], a["w13"]).then_inc(ws_in, 16)
                sp.dma_start(W2s[:], a["w2s"]).then_inc(ws_in, 16)
        with nc.cleanup_on_exit():
            self_attention(nc, group("b_"), X, EMB, HID, RL, consts)
        first_mixture(nc, group("r_"), EMB, HID, RL, table0, done0, weight_kept, consts)
        middle(nc, group("m_"), X, EMB, HID, RL, csum, weight_kept, part_dram, consts)
        second_mixture(nc, None, (W13, W2s, ws_in, 32), X, EMB, HID, RL, table1, done1, out, consts)


def arrays_of(inputs):
    import numpy as np

    i = {k: np.asarray(v) for k, v in inputs.items()}
    order = np.array([(2 * (p % 8) + m) * HD + p // 8 for m in range(KC) for p in range(128)])

    def chunks(wt):
        return np.ascontiguousarray(wt.reshape(KC, 128, -1).transpose(1, 0, 2))

    def columns(v):
        return np.ascontiguousarray(v.reshape(-1, 128).T)

    win, bin_ = i["L0_xattn_in_proj_weight"], i["L0_xattn_in_proj_bias"]
    flat = lambda k: i["L0_ffn_" + k].reshape(D, D)
    W = i["L1_xattn_W"]
    up = np.stack([i["L1_ffn_W1"], i["L1_ffn_W3"]], axis=1)
    out = {
        "x": i["x"], "ctxT": i["ctx_1024"].reshape(B, S, KC, 128).transpose(0, 3, 2, 1),
        "gates": np.concatenate([i["g_xattn"], i["g_ffn"]]),
        "a_wq": chunks(win[0:D][order].T), "a_wk": chunks(win[D:2 * D][order].T), "a_wv": chunks(win[2 * D:].T),
        "a_wo": chunks(i["L0_xattn_out_proj_weight"].T), "a_qb": columns(bin_[0:D][order]), "a_kb": columns(bin_[D:2 * D][order]),
        "a_vb": bin_[2 * D:], "a_ob": i["L0_xattn_out_proj_bias"], "a_gate": i["g_xattn"][0:1],
        "a_lam": np.stack([i["L0_xattn_lambda_" + k] for k in ("q1", "k1", "q2", "k2")]),
        "b_wq": chunks(flat("Wq")[order].T), "b_wk": chunks(flat("Wk")[order].T), "b_wv": chunks(flat("Wv").T),
        "b_wr": chunks(i["L0_ffn_Wsw"].T), "b_qkb": columns(np.concatenate([i["L0_ffn_bq"].reshape(D)[order], i["L0_ffn_bk"].reshape(D)[order]])),
        "b_vb": i["L0_ffn_bv"].reshape(D), "b_rb": i["L0_ffn_bsw"],
        "r_we": i["L0_ffn_We"].reshape(E, D, KC, 128).transpose(3, 0, 2, 1), "r_be": i["L0_ffn_be"].reshape(E * D),
        "m_w1": chunks(W[:, 0:D].T), "m_w2": chunks(W[:, D:].T), "m_wr2": chunks(i["L1_ffn_Wr"]), "m_b1": i["L1_xattn_b"],
        "m_gamma": i["L0_ffn_gamma"], "m_beta": i["L0_ffn_beta"],
        "w13": up.reshape(E, 2, KC, 128, HID2).transpose(3, 0, 1, 2, 4),
        "w2s": i["L1_ffn_W2"].reshape(E, HID2 // 128, 128, D).transpose(2, 0, 1, 3),
    }
    return {k: np.ascontiguousarray(v) for k, v in out.items()}


def kernel(**inputs):
    import concourse.bacc as _bacc
    from concourse.bass_utils import run_bass_kernel_spmd as _run

    nc = _bacc.Bacc("TRN2", target_bir_lowering=False, num_devices=1)
    arrays = arrays_of(inputs)
    args = {k: nc.dram_tensor("in_" + k, v.shape, mybir.dt.from_np(v.dtype), kind="ExternalInput").ap() for k, v in arrays.items()}
    out = nc.dram_tensor("out_x", (B, T, D), F32, kind="ExternalOutput").ap()
    build(nc, args, out)
    r = _run(nc, [{"in_" + k: v for k, v in arrays.items()}], core_ids=[0])
    return r.results[0]["out_x"]
```

```python
from contextlib import ExitStack
import math

import concourse.bass as bass
from concourse import mybir

F32 = mybir.dt.float32
BF16 = mybir.dt.bfloat16
ALU = mybir.AluOpType
ACT = mybir.ActivationFunctionType
AX = mybir.AxisListType

B, T, D = 16, 100, 256
S = 361
H, HD = 16, 16
SUB = HD // 2
KC = D // 128
SC = 3
SP_ = SC * 128
SCALING = 1.0 / math.sqrt(SUB)
LAMBDA_INIT = 0.8 - 0.6 * math.exp(-0.3 * 0)
EPS = 1e-5
RING = 3
BRING = 4

K_PARTS = (0, 0, 0, 1, 1, 2)
Q_PARTS = (0, 1, 2, 0, 1, 0)
G = len(K_PARTS)
E = 8
CAP = int(1.2 * B * T / E)
HALF = CAP // 2
HID2 = D * 3 // 2
E1_BLOCKS = (2 * B * T + E * 127) // 128
ROWS = 16 * G


def batch(off, i=None, stride=3):
    return (i, off, stride)


def later(n, d):
    return (n[0], n[1] + d, n[2])


def count(n, per, extra):
    return n[1] * per + extra if n[0] is None else n[0] * (n[2] * per) + (n[1] * per + extra)


def slot(n, ring=3):
    return n[1] % ring


def uses(n, ring=None):
    ring = ring or n[2]
    return n[1] // ring if n[0] is None else n[0] * (n[2] // ring) + n[1] // ring


def uses_value(n, per, ring=None):
    return (uses(n, ring) + 1) * per


def exists(n, total=16):
    return n[0] is not None or 0 <= n[1] < total


def at(n, width=1):
    if n[0] is None:
        return slice(n[1] * width, n[1] * width + width)
    return bass.ds(n[0] * (n[2] * width) + n[1] * width, width)


def at_batch(tensor, n):
    return tensor[:, n[1], :] if n[0] is None else tensor[:, at(n), :].rearrange("p b d -> p (b d)")


def wait(eng, sem, value):
    if not isinstance(value, int) or value > 0:
        eng.wait_ge(sem, value)


def waits(eng, settled, *pairs):
    if all(isinstance(v, int) for _, v in pairs):
        for sem, value in pairs:
            wait(eng, sem, value)
        return
    values = [(sem, v if isinstance(v, int) else eng.snap(eng.to_reg(v))) for sem, v in pairs]
    eng.wait_ge(*settled)
    for sem, value in values:
        wait(eng, sem, value)


def schedule(eng, body, first, last, rolled=2, stride=3, turns=4):
    for n in range(first, rolled):
        body(batch(n, stride=stride))
    with eng.Fori(0, turns) as i:
        for u in range(stride):
            body(batch(rolled + u, i, stride))
    for n in range(rolled + stride * turns, last + 1):
        body(batch(n, stride=stride))


def cross_attention(nc, x, ctxT, w, X1, pooled, prefetch, prefetched, consts):
    with ExitStack() as ctx:
        sb = lambda name, shape, dt=F32: ctx.enter_context(nc.sbuf_tensor("a_" + name, shape, dt))
        ps = lambda name: ctx.enter_context(nc.psum_tensor("a_" + name, [128, 512], F32))
        sem = lambda name: nc.alloc_semaphore("a_" + name)
        ring = lambda name, shape, dt=F32: [sb(f"{name}{s}", shape, dt) for s in range(RING)]

        ident, neg_half = consts["ident"], consts["neg_half"]
        W2, b1, pooled_dram = pooled
        summed = sb("summed", [128, S])
        csum, part = sb("csum", [128, KC, B]), sb("part", [B, D])
        Wq, Wk, Wv, Wo = (sb(n_, [128, KC, D]) for n_ in ("Wq", "Wk", "Wv", "Wo"))
        qb, kb = sb("qb", [128, KC]), sb("kb", [128, KC])
        vb, ob = sb("vb", [128, KC]), sb("ob", [128, D])
        vbs, both = sb("vbs", [128, KC, T]), sb("both", [128, 1])
        lamv = sb("lamv", [128, 4, SUB])
        lamp = sb("lamp", [128, 2, SUB])
        lamd, lame, lam = sb("lamd", [128, 2]), sb("lame", [128, 2]), sb("lam", [128, 1])
        gate, tgate = sb("gate", [128, 1]), sb("tgate", [128, 1])
        coef = sb("coef", [128, 4, 4])

        xin = ring("xin", [T, D])
        ctxs = ring("ctx", [128, KC, S])
        Kst = ring("Kst", [ROWS + 2, H, SP_], BF16)
        Qst = ring("Qst", [ROWS + 2, H, 2 * T], BF16)
        V = ring("V", [128, SC, H, 32])
        mx = ring("mx", [T, 2 * H])
        xres = ring("xres", [T, D])
        stats, mv = sb("stats", [T, 6]), sb("mv", [T, 2])
        ve, rstd = sb("ve", [T, 1]), sb("rstd", [T, 1])
        xn, xnT = sb("xn", [T, D]), sb("xnT", [128, KC, T])
        qf = sb("qf", [128, KC, 2, T])
        kf = sb("kf", [128, KC, S])
        qrem, krem = sb("qrem", [128, KC, 2 * T]), sb("krem", [128, KC, S])
        qpart, kpart = sb("qpart", [128, 3, KC, 2 * T], BF16), sb("kpart", [128, 3, KC, S], BF16)
        mrow = [sb(f"mrow{a}", [H, 2, T], BF16) for a in range(2)]
        probs = [sb(f"probs{k}", [128, 4 * T]) for k in range(6)]
        O = sb("O", [128, 4, 2 * T])
        rec, rc = sb("rec", [T, 2, 4, 4]), sb("rc", [T, 2, 4, 4])
        numer = sb("numer", [T, 2, 4, 4, HD])
        attn, attnT = sb("attn", [T, D]), sb("attnT", [128, KC, T])

        pM, pE, pX = ([ps(f"p{c}{s}") for s in range(k)] for c, k in (("M", 3), ("E", 2), ("X", 2)))
        pA = ps("pA")

        weights_in, gates_in, consts_ok = sem("weights_in"), sem("gates_in"), sem("consts_ok")
        lam_prod, lam_dot, lam_exp, lam_ok, coef_ok = (sem(n_) for n_ in ("lam_prod", "lam_dot", "lam_exp", "lam_ok", "coef_ok"))
        tgate_ok, vbs_ok, bias_ps, ob_ok = (sem(n_) for n_ in ("tgate_ok", "vbs_ok", "bias_ps", "ob_ok"))
        ones_in, v_init = sem("ones_in"), sem("v_init")
        x_in = [sem(f"x_in{s}") for s in range(RING)]
        ctx_in = [sem(f"ctx_in{s}") for s in range(RING)]
        res_in = [sem(f"res_in{s}") for s in range(RING)]
        kst_in = [sem(f"kst_in{s}") for s in range(RING)]
        qst_in = [sem(f"qst_in{s}") for s in range(RING)]
        mrow_in = [[sem(f"mrow_in{a}{s}") for s in range(RING)] for a in range(2)]
        ln_steps, rstd_ok, xn_ok = sem("ln_steps"), sem("rstd_ok"), sem("xn_ok")
        csum_ok = sem("csum_ok")
        qsplit, ksplit = sem("qsplit"), sem("ksplit")
        m_filled, m_reduced = sem("m_filled"), sem("m_reduced")
        e_filled, e_done = sem("e_filled"), sem("e_done")
        av_done, o_ok = sem("av_done"), sem("o_ok")
        msplit = [sem(f"msplit{a}") for a in range(2)]
        f_steps = sem("f_steps")
        resb_ok = sem("resb_ok")
        part_ps, part_ok, part_out = sem("part_ps"), sem("part_ok"), sem("part_out")

        TURNS = [("f0", -1), ("f1", -1), ("p0", 2), ("p1", 2), ("p2", 2), ("f2", -1), ("p3", 2),
                 ("f3", -1), ("p4", 2), ("mA", 1), ("p5", 2), ("p6", 2), ("mB", 1)]
        NAMES = [u for u, _ in TURNS]
        filled = {u: sem("filled_" + u) for u in NAMES}
        taken = {u: sem("taken_" + u) for u in NAMES}
        bank = {u: pX[k % 2] for k, u in enumerate(NAMES)}

        def free_bank(eng, n, u):
            k = NAMES.index(u)
            before = [(n, *t) for t in TURNS[:k]][::-1] + [(later(n, -1), *t) for t in TURNS][::-1]
            for m, name, d in before:
                if bank[name] is bank[u] and exists(later(m, d)):
                    wait(eng, taken[name], count(later(m, d), 1, 1))
                    return

        def m_tiles(k):
            before = lambda k: 2 * k // 3 if k <= 6 else 4 + 28 * (k - 6) // 18
            return range(before(k), before(k + 1))

        def m_bank(n, j):
            return (32 * n[1] + j) % 3

        block = ctx.enter_context(nc.Block())

        @block.sync
        def _(sp):
            loaded = (weights_in, 16 * 7)
            sp.dma_start(xin[0][:], x[0:1]).then_inc(x_in[0], 16)
            for dst, name in ((Wq, "wq"), (qb, "qb"), (Wk, "wk"), (kb, "kb")):
                sp.dma_start(dst[:], w[name]).then_inc(weights_in, 16)
            sp.dma_start(ctxs[0][:], ctxT[0:1]).then_inc(ctx_in[0], 16)
            for dst, name in ((Wv, "wv"), (Wo, "wo"), (vb, "vb")):
                sp.dma_start(dst[:], w[name]).then_inc(weights_in, 16)
            sp.wait_ge(consts["made"], consts["made_value"])
            sp.wait_ge(consts_ok, RING)
            for s in range(RING):
                sp.dma_start(Kst[s][ROWS:ROWS + 2, :, 0:S], consts["onesb"][0:2 * H, :]).then_inc(ones_in, 16)

            def load(n):
                waits(sp, loaded, (xn_ok, count(n, 1, 1 - RING)))
                waits(sp, loaded, (filled["p6"], count(n, 1, 1 - RING)))
                waits(sp, loaded, (csum_ok, count(n, 2, 2 * (1 - RING))))
                sp.dma_start(xin[slot(n)][:], x[at(n)]).then_inc(x_in[slot(n)], 16)
                sp.dma_start(ctxs[slot(n)][:], ctxT[at(n)]).then_inc(ctx_in[slot(n)], 16)

            def body(n):
                nF, nM, nP, nL = later(n, -1), later(n, 1), later(n, 2), later(n, 3)
                if exists(nL):
                    load(nL)
                if exists(nF):
                    sp.dma_start(xres[slot(nF)][:], x[at(nF)]).then_inc(res_in[slot(nF)], 16)
                if exists(nP):
                    waits(sp, loaded, (e_filled, count(nP, 24, 24 * (1 - RING))))
                    stack(nP, Qst[slot(nP)], qpart, Q_PARTS, qsplit, qst_in, 2 * T)
                if exists(nM):
                    rows(nM, 0)
                if exists(nP):
                    stack(nP, Kst[slot(nP)], kpart, K_PARTS, ksplit, kst_in, S)
                if exists(nM):
                    rows(nM, 1)

            def stack(n, to, part, parts, steps, sent, width):
                for k in range(3):
                    waits(sp, loaded, (steps, count(n, 4, (1, 3, 4)[k])))
                    for g in range(G):
                        if parts[g] == k:
                            sp.dma_start(to[16 * g:16 * g + 16, :, 0:width], part[:, k]).then_inc(sent[slot(n)], 16)

            def rows(n, a):
                waits(sp, loaded, (taken["m" + "AB"[a]], count(n, 1, 1)))
                for r in range(2):
                    sp.dma_start(Qst[slot(n)][ROWS + r:ROWS + r + 1, 8 * a:8 * a + 8, :], mrow[a][:, r, :]).then_inc(mrow_in[a][slot(n)], 16)

            for n in (-2, -1, 0):
                body(batch(n))
            for dst, src in prefetch:
                sp.dma_start(dst, src).then_inc(prefetched, 16)
            schedule(sp, body, 1, B, rolled=1)
            sp.wait_ge(part_ok, 2)
            sp.dma_start(pooled_dram, part[:]).then_inc(part_out, 16)
            sp.wait_ge(part_out, 16)

        @block.gpsimd
        def _(pool):
            for s in range(RING):
                pool.memset(Kst[s][:, :, S:SP_], 0.0).then_inc(consts_ok, 1)
            started = (consts_ok, RING)
            pool.wait_ge(*started)

            def split(n, full, rem, part, steps):
                src = full[:].rearrange("p c s t -> p c (s t)") if full is qf else full[:]
                for k in range(2):
                    pool.wait_ge(steps, count(n, 4, 2 * k + 1))
                    pool.tensor_tensor(part[:, 2] if k else rem[:], rem[:] if k else src, part[:, k], ALU.subtract).then_inc(steps, 1)

            def body(n):
                nF, nP = later(n, -1), later(n, 2)
                if exists(nP):
                    pool.wait_ge(ln_steps, count(nP, 3, 3))
                    pool.tensor_tensor(rstd[:], ve[:], neg_half[0:T, :], ALU.pow).then_inc(rstd_ok, 1)
                if exists(nF):
                    if nF[0] is None and nF[1] == 0:
                        pool.wait_ge(ob_ok, 2)
                    pool.wait_ge(res_in[slot(nF)], uses_value(nF, 16))
                    pool.tensor_tensor(xres[slot(nF)][:], xres[slot(nF)][:], ob[0:T, :], ALU.add).then_inc(resb_ok, 1)
                if exists(nP):
                    split(nP, qf, qrem, qpart, qsplit)
                    split(nP, kf, krem, kpart, ksplit)

            schedule(pool, body, -2, B)

        AT = dict(f0=0, f1=2, p0=3, p1=5, p2=7, f2=8, p3=9, f3=11, p4=12, mA=15, p5=16, p6=18, mB=24)

        @block.tensor
        def _(pe):
            pe.wait_ge(weights_in, 16 * 7)

            def use(n, u):
                stage = later(n, dict(TURNS)[u])
                if not exists(stage):
                    return
                free_bank(pe, n, u)
                X = bank[u]
                if u == "p0":
                    pe.wait_ge(xn_ok, count(stage, 1, 1))
                    for c in range(KC):
                        mm = pe.transpose(X[:, T * c:T * (c + 1)], xn[:, 128 * c:128 * (c + 1)], ident[0:T, 0:T])
                elif u == "p1":
                    pe.wait_ge(taken["p0"], count(stage, 1, 1))
                    for m in range(KC):
                        for c in range(KC):
                            mm = pe.matmul(X[:, T * m:T * (m + 1)], Wq[:, c, 128 * m:128 * (m + 1)], xnT[:, c, :], start=(c == 0), stop=(c == KC - 1))
                elif u in ("p2", "p3"):
                    m = int(u[1]) - 2
                    pe.wait_ge(ctx_in[slot(stage)], uses_value(stage, 16))
                    for c in range(KC):
                        mm = pe.matmul(X[:, 0:S], Wk[:, c, 128 * m:128 * (m + 1)], ctxs[slot(stage)][:, c, :], start=(c == 0), stop=(c == KC - 1))
                elif u in ("p4", "p5", "p6"):
                    k = int(u[1]) - 4
                    r = min(128, S - 128 * k)
                    for c in range(KC):
                        mm = pe.matmul(X[0:r, 0:D], ctxs[slot(stage)][:, c, 128 * k:128 * k + r], Wv[:, c, :], start=(c == 0), stop=(c == KC - 1))
                elif u in ("mA", "mB"):
                    a = "AB".index(u[1])
                    pe.wait_ge(m_reduced, count(stage, 32, 16 * (a + 1)))
                    mm = pe.transpose(X[0:16, 0:T], mx[slot(stage)][:, 16 * a:16 * a + 16], ident[0:T, 0:T])
                elif u in ("f0", "f1"):
                    f = int(u[1])
                    pe.wait_ge(o_ok, count(stage, 4, 2 * f + 2))
                    for q in range(2):
                        for s in range(2):
                            k = 2 * q + s
                            mm = pe.transpose(X[0:T, 128 * k:128 * (k + 1)], O[:, 2 * f + q, T * s:T * (s + 1)], ident[:])
                elif u == "f2":
                    pe.wait_ge(f_steps, count(stage, 6, 6))
                    for c in range(KC):
                        mm = pe.transpose(X[:, T * c:T * (c + 1)], attn[:, 128 * c:128 * (c + 1)], ident[0:T, 0:T])
                elif u == "f3":
                    pe.wait_ge(taken["f2"], count(stage, 1, 1))
                    for c in range(KC):
                        mm = pe.matmul(X[0:T, 0:D], attnT[:, c, :], Wo[:, c, :], start=(c == 0), stop=(c == KC - 1))
                mm.then_inc(filled[u], 1)

            def e_tile(n, k):
                q, c, half = k // 6, k % 6 // 2, k % 2
                if n[0] is None and n[1] == k == 0:
                    pe.wait_ge(consts_ok, RING)
                    pe.wait_ge(ones_in, 16 * RING)
                    pe.wait_ge(ob_ok, 1)
                if k in (0, 12):
                    pe.wait_ge(mrow_in[k // 12][slot(n)], uses_value(n, 32))
                wait(pe, e_done, count(n, 24, k - 1))
                for j in range(2):
                    h = 4 * q + 2 * half + j
                    mm = pe.matmul(pE[k % 2][:, 2 * T * j:2 * T * (j + 1)], Kst[slot(n)][:, h, 128 * c:128 * (c + 1)],
                                   Qst[slot(n)][:, h, :], start=True, stop=True)
                mm.then_inc(e_filled, 1)

            def m_tile(n, j):
                if j == 0:
                    pe.wait_ge(qst_in[slot(n)], uses_value(n, 16 * G))
                    pe.wait_ge(kst_in[slot(n)], uses_value(n, 16 * G))
                wait(pe, m_reduced, count(n, 32, j - 2))
                pe.matmul(pM[m_bank(n, j)][0:T, 0:S], Qst[slot(n)][0:ROWS, j // 2, T * (j % 2):T * (j % 2 + 1)],
                          Kst[slot(n)][0:ROWS, j // 2, 0:S], start=True, stop=True).then_inc(m_filled, 1)

            def av(n, g):
                q, c = g // 3, g % 3
                if g == 0:
                    pe.wait_ge(taken["p6"], count(n, 1, 1))
                    if n[0] is None and n[1] == 0:
                        pe.wait_ge(v_init, 6)
                if c == 0:
                    wait(pe, o_ok, count(n, 4, q))
                pe.wait_ge(e_done, count(n, 24, 2 * g + 2))
                for j in range(4):
                    mm = pe.matmul(pA[32 * j:32 * j + 32, 0:2 * T], V[slot(n)][:, c, 4 * q + j, :],
                                   probs[(2 * g + j // 2) % 6][:, 2 * T * (j % 2):2 * T * (j % 2 + 1)],
                                   start=(c == 0), stop=(c == SC - 1))
                mm.then_inc(av_done, 1)

            def body(n):
                for k in range(24):
                    if exists(n):
                        e_tile(n, k)
                    if exists(later(n, 1)):
                        for j in m_tiles(k):
                            m_tile(later(n, 1), j)
                    if exists(n) and k % 2 and k >= 3:
                        av(n, k // 2 - 1)
                    for u in NAMES:
                        if AT[u] == k:
                            use(n, u)
                if exists(n):
                    av(n, 11)
                use(n, "mB")

            body(batch(-2))
            pe.wait_ge(vbs_ok, 1)
            for c in range(KC):
                mm = pe.matmul(pE[0][0:T, 0:D], vbs[:, c, :], Wo[:, c, :], start=(c == 0), stop=(c == KC - 1))
            mm.then_inc(bias_ps, 1)
            schedule(pe, body, -1, B)
            pe.wait_ge(csum_ok, 2 * B)
            pe.wait_ge(prefetched, 16 * len(prefetch))
            pe.wait_ge(m_reduced, 32 * B)
            for c in range(KC):
                mm = pe.matmul(pM[0][0:B, 0:D], csum[:, c, :], W2[:, c, :], start=(c == 0), stop=(c == KC - 1))
            mm.then_inc(part_ps, 1)

        @block.vector
        def _(dve):
            for s in range(RING):
                dve.memset(V[s][:], 0.0).then_inc(v_init, 1)
            dve.wait_ge(v_init, RING)
            for s in range(RING):
                dve.memset(V[s][:, 0:2, :, HD:HD + 1], 1.0).then_inc(v_init, 1)
                dve.memset(V[s][0:S - 256, 2, :, HD:HD + 1], 1.0)
            dve.memset(qf[:], 0.0)
            dve.wait_ge(gates_in, 16 * 3)
            dve.tensor_tensor(lamp[:], lamv[:, 0:4:2, :], lamv[:, 1:4:2, :], ALU.mult).then_inc(lam_prod, 1)
            dve.wait_ge(lam_prod, 1)
            dve.tensor_reduce(lamd[:], lamp[:], AX.X, ALU.add).then_inc(lam_dot, 1)
            dve.wait_ge(lam_exp, 1)
            dve.tensor_tensor(lam[:], lame[:, 1:2], lame[:, 0:1], ALU.subtract).then_inc(lam_ok, 1)
            dve.wait_ge(lam_ok, 1)
            dve.tensor_scalar(lam[:], lam[:], -LAMBDA_INIT, 1.0 - LAMBDA_INIT, ALU.add, ALU.mult).then_inc(lam_ok, 1)
            dve.memset(coef[:], 1.0 - LAMBDA_INIT).then_inc(coef_ok, 1)
            dve.wait_ge(lam_ok, 2)
            dve.wait_ge(coef_ok, 1)
            dve.tensor_scalar(coef[:, 1:4:2, :], coef[:, 1:4:2, :], 0.0, lam[:, 0:1], ALU.mult, ALU.add).then_inc(coef_ok, 1)
            dve.wait_ge(coef_ok, 2)
            loaded = (weights_in, 16 * 7)
            dve.wait_ge(*loaded)
            dve.tensor_scalar(both[:], lam[:], 1.0 - LAMBDA_INIT, None, ALU.add).then_inc(coef_ok, 1)
            dve.wait_ge(coef_ok, 3)
            dve.tensor_scalar(vbs[:], vb[:].unsqueeze(2).broadcast_to([128, KC, T]), both[:, 0:1], None, ALU.mult).then_inc(vbs_ok, 1)

            def norm(n):
                s = slot(n)
                dve.wait_ge(x_in[s], uses_value(n, 16))
                dve.bn_stats(stats[:], xin[s][:]).then_inc(ln_steps, 1)
                waits(dve, loaded, (ln_steps, count(n, 3, 1)))
                dve.bn_aggr(mv[:], stats[:]).then_inc(ln_steps, 1)
                dve.wait_ge(ln_steps, count(n, 3, 2))
                dve.tensor_scalar(ve[:], mv[:, 1:2], EPS, None, ALU.add).then_inc(ln_steps, 1)

            def norm_end(n):
                dve.wait_ge(rstd_ok, count(n, 1, 1))
                wait(dve, filled["p0"], count(n, 1, 0))
                dve.tensor_scalar(xn[:], xin[slot(n)][:], mv[:, 0:1], rstd[:, 0:1], ALU.subtract, ALU.mult).then_inc(xn_ok, 1)

            def take(n, u):
                stage = later(n, dict(TURNS)[u])
                if not exists(stage):
                    return
                X = bank[u]
                dve.wait_ge(filled[u], count(stage, 1, 1))
                if u == "p1":
                    wait(dve, qsplit, count(stage, 4, 0))
                    for s in range(2):
                        r = slice(64 * s, 64 * s + 64)
                        ins = dve.tensor_tensor(qf[r, :, s, :], X[r, 0:2 * T].rearrange("p (c t) -> p c t", c=KC),
                                                qb[r, :].unsqueeze(2).broadcast_to([64, KC, T]), ALU.add)
                    ins.then_inc(taken[u], 1)
                elif u in ("mA", "mB"):
                    a = "AB".index(u[1])
                    m = later(stage, -1)
                    if exists(m):
                        dve.wait_ge(mrow_in[a][slot(m)], uses_value(m, 32))
                    dve.tensor_scalar(mrow[a][:, 0, :], X[0:16, 0:T], -1.0, None, ALU.mult).then_inc(msplit[a], 1)
                    dve.wait_ge(msplit[a], count(stage, 1, 1))
                    dve.scalar_tensor_tensor(mrow[a][:, 1, :], X[0:16, 0:T], -1.0, mrow[a][:, 0, :], ALU.mult, ALU.subtract).then_inc(taken[u], 1)
                elif u in ("f0", "f1"):
                    f = int(u[1])
                    sums = X[0:T, :].rearrange("p (k j d) -> p k j d", k=4, j=4)
                    dve.reciprocal(rec[:, f], sums[:, :, :, HD]).then_inc(f_steps, 1)
                    dve.wait_ge(f_steps, count(stage, 6, 3 * f + 1))
                    dve.tensor_tensor(rc[:, f], rec[:, f], coef[0:T], ALU.mult).then_inc(f_steps, 1)
                    dve.wait_ge(f_steps, count(stage, 6, 3 * f + 2))
                    dve.tensor_tensor(numer[:, f], sums[:, :, :, 0:HD], rc[:, f].unsqueeze(3).broadcast_to([T, 4, 4, HD]), ALU.mult).then_inc(taken[u], 1)
                    dve.wait_ge(taken[u], count(stage, 1, 1))
                    two = numer[:, f].rearrange("p (q s) j d -> p q s (j d)", s=2)
                    dve.tensor_tensor(attn[:, 128 * f:128 * f + 128].rearrange("p (q x) -> p q x", q=2),
                                      two[:, :, 0], two[:, :, 1], ALU.add).then_inc(f_steps, 1)
                elif u == "f3":
                    dve.wait_ge(resb_ok, count(stage, 1, 1))
                    dve.scalar_tensor_tensor(at_batch(X1, stage), X[0:T, 0:D], tgate[0:T, 0:1], xres[slot(stage)][:], ALU.mult, ALU.add).then_inc(taken[u], 1)

            def body(n):
                nM, nP = later(n, 1), later(n, 2)
                if exists(nP):
                    norm(nP)
                for k in range(25):
                    for u in ("f0", "f1", "p1", "f3", "mA", "mB"):
                        if AT[u] == k - 1:
                            take(n, u)
                    if k == 1 and exists(nP):
                        norm_end(nP)
                    if k < 24 and exists(nM):
                        for j in m_tiles(k):
                            dve.wait_ge(m_filled, count(nM, 32, j + 1))
                            dve.tensor_reduce(mx[slot(nM)][:, j:j + 1], pM[m_bank(nM, j)][0:T, 0:S], AX.X, ALU.max).then_inc(m_reduced, 1)
                take(n, "mB")

            body(batch(-2))
            dve.wait_ge(bias_ps, 1)
            dve.tensor_tensor(ob[0:T], ob[0:T], pE[0][0:T, 0:D], ALU.add).then_inc(ob_ok, 1)
            dve.wait_ge(ob_ok, 1)
            dve.wait_ge(tgate_ok, 1)
            dve.tensor_scalar(ob[0:T], ob[0:T], tgate[0:T, 0:1], None, ALU.mult).then_inc(ob_ok, 1)
            schedule(dve, body, -1, B)
            dve.wait_ge(part_ps, 1)
            dve.wait_ge(prefetched, 16 * len(prefetch))
            dve.scalar_tensor_tensor(part[:], pM[0][0:B, 0:D], 1.0 / S, b1[0:B, :], ALU.mult, ALU.add).then_inc(part_ok, 1)
            dve.wait_ge(part_ok, 1)
            dve.tensor_scalar(part[:], part[:], consts["tgates"][0:B, 1:2], None, ALU.mult).then_inc(part_ok, 1)

        @block.scalar
        def _(act):
            act.dma_start(lamv[:].rearrange("p k d -> p (k d)"), w["lam"].partition_broadcast(128)).then_inc(gates_in, 16)
            act.dma_start(gate[:], w["gate"].partition_broadcast(128)).then_inc(gates_in, 16)
            act.dma_start(ob[:], w["ob"].partition_broadcast(128)).then_inc(gates_in, 16)
            act.wait_ge(lam_dot, 1)
            act.activation(lame[:], lamd[:], ACT.Exp).then_inc(lam_exp, 1)
            act.activation(tgate[:], gate[:], ACT.Tanh).then_inc(tgate_ok, 1)
            act.wait_ge(weights_in, 16 * 7)

            def take(n, u):
                stage = later(n, dict(TURNS)[u])
                if not exists(stage):
                    return
                X = bank[u]
                act.wait_ge(filled[u], count(stage, 1, 1))
                if u == "p0":
                    wait(act, filled["p1"], count(stage, 1, 0))
                    act.activation(xnT[:].rearrange("p c t -> p (c t)"), X[:, 0:KC * T], ACT.Copy).then_inc(taken[u], 1)
                elif u in ("p2", "p3"):
                    m = int(u[1]) - 2
                    wait(act, ksplit, count(stage, 4, 0))
                    ins = act.activation(kf[:, m, :], X[:, 0:S], ACT.Identity, bias=kb[:, m:m + 1])
                    ins.then_inc(taken[u], 1)
                elif u in ("p4", "p5", "p6"):
                    k = int(u[1]) - 4
                    r = min(128, S - 128 * k)
                    wait(act, av_done, count(stage, 12, 12 * (1 - RING)))
                    if stage[0] is None and stage[1] < RING:
                        act.wait_ge(v_init, RING)
                    act.activation(V[slot(stage)][0:r, k, :, 0:HD], X[0:r, 0:D].rearrange("p (h d) -> p h d", h=H), ACT.Copy).then_inc(taken[u], 1)
                elif u == "f2":
                    wait(act, filled["f3"], count(stage, 1, 0))
                    act.activation(attnT[:].rearrange("p c t -> p (c t)"), X[:, 0:KC * T], ACT.Copy).then_inc(taken[u], 1)

            started = (tgate_ok, 1)
            SPLIT_AT = {7: (qf, qrem, qpart, 0, qsplit, taken["p1"], qst_in), 9: (qf, qrem, qpart, 1, qsplit, taken["p1"], qst_in),
                        11: (kf, krem, kpart, 0, ksplit, taken["p3"], kst_in), 14: (kf, krem, kpart, 1, ksplit, taken["p3"], kst_in)}

            def split(n, full, rem, part, k, steps, ready, sent):
                m = later(n, -1)
                src = full[:].rearrange("p c s t -> p c (s t)") if full is qf else full[:]
                if k == 0:
                    act.wait_ge(ready, count(n, 1, 1))
                    if exists(m):
                        act.wait_ge(sent[slot(m)], uses_value(m, 16 * G))
                else:
                    act.wait_ge(steps, count(n, 4, 2))
                act.activation(part[:, k], rem[:] if k else src, ACT.Copy).then_inc(steps, 1)

            def sum_context(n):
                for c in range(KC):
                    waits(act, started, (ctx_in[slot(n)], uses_value(n, 16)), (csum_ok, count(n, 2, c)))
                    act.activation(summed[:], ctxs[slot(n)][:, c, :], ACT.Copy, accum_out=csum[:, c, at(n)]).then_inc(csum_ok, 1)

            def sums_out(n, q):
                act.wait_ge(av_done, count(n, 12, 3 * q + 3))
                wait(act, filled["f0" if q < 2 else "f1"], count(n, 1, 0))
                act.activation(O[:, q, :], pA[:, 0:2 * T], ACT.Copy).then_inc(o_ok, 1)

            def body(n):
                nP = later(n, 2)
                for k in range(24):
                    for u in ("p0", "p2", "p3", "f2", "p4", "p5", "p6"):
                        if AT[u] == k - 1:
                            take(n, u)
                    if exists(nP) and k in SPLIT_AT:
                        split(nP, *SPLIT_AT[k])
                    if exists(n):
                        if k >= 8 and k % 6 == 2:
                            sums_out(n, k // 6 - 1)
                        act.wait_ge(e_filled, count(n, 24, k + 1))
                        wait(act, av_done, count(n, 12, (k - 6) // 2 + 1))
                        act.activation(probs[k % 6][:], pE[k % 2][:, 0:4 * T], ACT.Exp, scale=SCALING).then_inc(e_done, 1)
                if exists(n):
                    sums_out(n, 3)
                if exists(later(n, 2)):
                    sum_context(later(n, 2))

            schedule(act, body, -2, B)
            act.wait_ge(csum_ok, 2 * B)


def zeroed(table, zero):
    rows = table.rearrange("(p k) d -> p (k d)", p=128)
    total, step = rows.shape[1], zero.shape[1]
    return [(rows[:, a:min(a + step, total)], zero[:, 0:min(step, total - a)]) for a in range(0, total, step)]


def constants(nc, ctx, gates):
    sb = lambda name, shape, dt=F32: ctx.enter_context(nc.sbuf_tensor("c_" + name, shape, dt))
    made = nc.alloc_semaphore("c_made")
    c = dict(onesb=sb("onesb", [3 * H, S], BF16), ident=sb("ident", [128, 128]), identb=sb("identb", [128, 128], BF16), neg_half=sb("neg_half", [128, 1]),
             far_s=sb("far_s", [T, 4 * T], BF16), far_t=sb("far_t", [T, 4 * T], BF16), behind=sb("behind", [T, T]),
             before=sb("before", [T, T]), ones=sb("ones", [T, T]), floor=sb("floor", [128, 1]),
             numbers=sb("numbers", [T, E1_BLOCKS]), zero=sb("zero", [128, 1024]), tgates=sb("tgates", [128, 4]))
    whole = sb("whole", [T, E1_BLOCKS], mybir.dt.int32)
    starts = dict(ident=0.0, identb=0.0, neg_half=-0.5, far_s=0.0, far_t=0.0, behind=1.0, before=1.0, ones=1.0, floor=0.0, zero=0.0, onesb=1.0)
    gates_in, gates_ok = nc.alloc_semaphore("c_gates_in"), nc.alloc_semaphore("c_gates_ok")
    c["made"], c["made_value"] = made, len(starts)
    FAR = -1.0e30
    with nc.Block() as block:
        @block.gpsimd
        def _(pool):
            for name, value in starts.items():
                pool.memset(c[name][:], value).then_inc(made, 1)
            pool.wait_ge(made, len(starts))
            four = lambda name: c[name][:].rearrange("p (h t) -> p h t", h=4)
            selects = [(c["ident"][:], [[-1, 128]], 1, 0, ALU.not_equal, 1.0),
                       (c["identb"][:], [[-1, 128]], 1, 0, ALU.not_equal, 1.0),
                       (four("far_s"), [[0, 4], [-1, T]], 1, 0, ALU.is_ge, FAR),
                       (four("far_t"), [[0, 4], [1, T]], -1, 0, ALU.is_ge, FAR),
                       (c["behind"][:], [[-1, T]], 1, 0, ALU.is_gt, 0.0),
                       (c["before"][:], [[1, T]], -1, 0, ALU.is_gt, 0.0),
                       (c["floor"][:], [[0, 1]], -1, T - 2, ALU.is_ge, -3.0e38)]
            for out, pattern, factor, base, compare, other in selects:
                pool.affine_select(out=out, in_=out, compare_op=compare, fill=other, base=base, pattern=pattern,
                                   channel_multiplier=factor).then_inc(made, 1)
            pool.iota(whole[:], pattern=[[1, E1_BLOCKS]], base=0, channel_multiplier=0).then_inc(made, 1)
            pool.wait_ge(made, len(starts) + len(selects) + 1)
            pool.tensor_copy(c["numbers"][:], whole[:]).then_inc(made, 1)
            pool.wait_ge(made, len(starts) + len(selects) + 2)

        @block.scalar
        def _(act):
            act.dma_start(c["tgates"][:], gates.partition_broadcast(128)).then_inc(gates_in, 16)
            act.wait_ge(gates_in, 16)
            act.activation(c["tgates"][:], c["tgates"][:], ACT.Tanh).then_inc(gates_ok, 1)
            act.wait_ge(gates_ok, 1)

    return c


def self_attention(nc, W, X1, EMB, HID, RL, consts):
    run = dict(rolled=2, stride=BRING, turns=2)
    bslot = lambda n: slot(n, BRING)
    with ExitStack() as ctx:
        sb = lambda name, shape, dt=F32: ctx.enter_context(nc.sbuf_tensor("b_" + name, shape, dt))
        ps = lambda name: ctx.enter_context(nc.psum_tensor("b_" + name, [128, 512], F32))
        sem = lambda name: nc.alloc_semaphore("b_" + name)
        ring = lambda name, shape, dt=F32: [sb(f"{name}{s}", shape, dt) for s in range(BRING)]

        ident, identb, neg_half = consts["ident"], consts["identb"], consts["neg_half"]
        far_s, far_t = consts["far_s"], consts["far_t"]
        behind, floor = consts["behind"], consts["floor"]
        Wq, Wk, Wv, Wr, qkb, vb, rb = (W[n_] for n_ in ("wq", "wk", "wv", "wr", "qkb", "vb", "rb"))

        Kst = ring("Kst", [ROWS + 3, H, T], BF16)
        Qst = ring("Qst", [ROWS + 3, H, T], BF16)
        V = ring("V", [T, H, 32])
        mxr = ring("mxr", [T, H])
        mx = ring("mx", [T, H])
        stats, mv = sb("stats", [T, 6]), sb("mv", [T, 2])
        ve, rstd = sb("ve", [T, 1]), sb("rstd", [T, 1])
        xn, xnT = sb("xn", [T, D]), sb("xnT", [128, KC, T])
        qk, rem = sb("qk", [128, 2 * KC, T]), sb("rem", [128, 2 * KC, T])
        parts = [sb(f"part{h}", [128, 3, 2 * KC, T], BF16) for h in range(2)]
        mrow, mrem = sb("mrow", [H, 3, T], BF16), sb("mrem", [H, T])
        probs = [sb(f"probs{k}", [T, 4 * T]) for k in range(4)]
        O = sb("O", [128, 4, T])
        expm = sb("expm", [T, H])
        later_sum, total = sb("later_sum", [T, H, HD + 1]), sb("total", [T, H, HD + 1])
        rec = sb("rec", [T, H])
        hid, hidT = sb("hid", [T, D]), sb("hidT", [128, KC, T])

        pM, pE, pA, pX = ([ps(f"p{c}{s}") for s in range(2)] for c in "MEAX")

        consts_ok, ones_in = sem("consts_ok"), sem("ones_in")
        qst_in = [sem(f"qst_in{s}") for s in range(BRING)]
        kst_in = [sem(f"kst_in{s}") for s in range(BRING)]
        mrow_in = [sem(f"mrow_in{s}") for s in range(BRING)]
        ln_steps, rstd_ok, xn_ok = sem("ln_steps"), sem("rstd_ok"), sem("xn_ok")
        split_steps = sem("split_steps")
        m_filled, m_reduced, m_floored, m_steps = sem("m_filled"), sem("m_reduced"), sem("m_floored"), sem("m_steps")
        e_filled, e_done, av_done, o_ok = sem("e_filled"), sem("e_done"), sem("av_done"), sem("o_ok")
        expm_ok, f_steps, hid_kept = sem("expm_ok"), sem("f_steps"), sem("hid_kept")

        TURNS = [("f1", -1), ("f0", -1), ("p0", 3), ("p1", 3), ("mA", 1), ("f2", -1), ("p2", 3), ("f3", -1)]
        NAMES = [u for u, _ in TURNS]
        filled = {u: sem("filled_" + u) for u in NAMES}
        taken = {u: sem("taken_" + u) for u in NAMES}
        bank = {u: pX[k % 2] for k, u in enumerate(NAMES)}

        def free_bank(eng, n, u):
            k = NAMES.index(u)
            before = [(n, *t) for t in TURNS[:k]][::-1] + [(later(n, -1), *t) for t in TURNS][::-1]
            for m, name, d in before:
                if bank[name] is bank[u] and exists(later(m, d)):
                    wait(eng, taken[name], count(later(m, d), 1, 1))
                    return

        block = ctx.enter_context(nc.Block())

        @block.sync
        def _(sp):
            loaded = (W["in"], W["in_value"])
            for s in range(BRING):
                sp.dma_start(Kst[s][ROWS:ROWS + 3, :, :], consts["onesb"][:, 0:T]).then_inc(ones_in, 16)

            def body(n):
                nM, nP = later(n, 1), later(n, 3)
                if exists(nM):
                    waits(sp, loaded, (m_steps, count(nM, 3, 3)))
                    for r in range(3):
                        sp.dma_start(Qst[bslot(nM)][ROWS + r:ROWS + r + 1, :, :], mrow[:, r, :]).then_inc(mrow_in[bslot(nM)], 16)
                if exists(nP):
                    for k in range(3):
                        waits(sp, loaded, (e_filled, count(nP, 4, 4 * (1 - BRING))), (split_steps, count(nP, 4, (1, 3, 4)[k])))
                        for to, of, first, sent in ((Qst, Q_PARTS, 0, qst_in), (Kst, K_PARTS, KC, kst_in)):
                            for g in range(G):
                                if of[g] == k:
                                    sp.dma_start(to[bslot(nP)][16 * g:16 * g + 16, :, :], parts[slot(nP, 2)][:, k, first:first + KC]).then_inc(sent[bslot(nP)], 16)

            schedule(sp, body, -3, B, **run)

        @block.gpsimd
        def _(pool):
            inits = [(V[s][:], 0.0) for s in range(BRING)]
            inits += [(V[s][:, :, HD:HD + 1], 1.0) for s in range(BRING)]
            for k, (out, value) in enumerate(inits):
                if k:
                    pool.wait_ge(consts_ok, k)
                pool.memset(out, value).then_inc(consts_ok, 1)
            started = (consts_ok, len(inits))
            pool.wait_ge(*started)

            def body(n):
                nF, nP = later(n, -1), later(n, 3)
                if exists(nP):
                    pool.wait_ge(ln_steps, count(nP, 3, 3))
                    pool.tensor_tensor(rstd[:], ve[:], neg_half[0:T, :], ALU.pow).then_inc(rstd_ok, 1)
                if exists(nF):
                    waits(pool, started, (f_steps, count(nF, 4, 4)))
                    pool.tensor_copy(at_batch(HID, nF), hid[:]).then_inc(hid_kept, 1)
                if exists(nP):
                    for k in range(2):
                        part = parts[slot(nP, 2)]
                        pool.wait_ge(split_steps, count(nP, 4, 2 * k + 1))
                        out = part[:, 2] if k else rem[:]
                        pool.tensor_tensor(out, rem[:] if k else qk[:], part[:, k], ALU.subtract).then_inc(split_steps, 1)

            schedule(pool, body, -3, B, **run)

        @block.tensor
        def _(pe):
            pe.wait_ge(W["in"], W["in_value"])
            pe.wait_ge(consts_ok, 2 * BRING)

            def use(n, u):
                stage = later(n, dict(TURNS)[u])
                if not exists(stage):
                    return
                free_bank(pe, n, u)
                X = bank[u]
                if u == "p0":
                    pe.wait_ge(xn_ok, count(stage, 1, 1))
                    for c in range(KC):
                        mm = pe.transpose(X[:, T * c:T * (c + 1)], xn[:, 128 * c:128 * (c + 1)], ident[0:T, 0:T])
                elif u == "p1":
                    pe.wait_ge(taken["p0"], count(stage, 1, 1))
                    for k, W in enumerate((Wq, Wk)):
                        for m in range(KC):
                            for c in range(KC):
                                mm = pe.matmul(X[:, T * (KC * k + m):T * (KC * k + m + 1)], W[:, c, 128 * m:128 * (m + 1)], xnT[:, c, :],
                                               start=(c == 0), stop=(c == KC - 1))
                elif u == "p2":
                    for c in range(KC):
                        mm = pe.matmul(X[0:T, 0:D], xnT[:, c, :], Wv[:, c, :], start=(c == 0), stop=(c == KC - 1))
                elif u == "mA":
                    pe.wait_ge(m_floored, count(stage, 1, 1))
                    mm = pe.transpose(X[0:H, 0:T], mx[bslot(stage)][:], ident[0:T, 0:T])
                elif u == "f0":
                    pe.wait_ge(o_ok, count(stage, 2, 2))
                    for q in range(4):
                        mm = pe.transpose(X[0:T, 128 * q:128 * (q + 1)], O[:, q, :], ident[:])
                elif u == "f1":
                    mm = pe.matmul(X[0:T, 0:H * (HD + 1)], behind[:], V[bslot(stage)][:, :, 0:HD + 1], start=True, stop=True)
                elif u == "f2":
                    pe.wait_ge(f_steps, count(stage, 4, 4))
                    for c in range(KC):
                        mm = pe.transpose(X[:, T * c:T * (c + 1)], hid[:, 128 * c:128 * (c + 1)], ident[0:T, 0:T])
                elif u == "f3":
                    pe.wait_ge(taken["f2"], count(stage, 1, 1))
                    for c in range(KC):
                        mm = pe.matmul(X[0:T, 0:8], hidT[:, c, :], Wr[:, c, :], start=(c == 0), stop=(c == KC - 1))
                mm.then_inc(filled[u], 1)

            def m_tile(n, k):
                if k == 0:
                    pe.wait_ge(qst_in[bslot(n)], uses_value(n, 16 * G))
                    pe.wait_ge(kst_in[bslot(n)], uses_value(n, 16 * G))
                wait(pe, m_reduced, count(n, 4, k - 1))
                pe.matmul(pM[k % 2][0:T, 0:4 * T], identb[0:T, 0:T], far_s[:], start=True, stop=True)
                for j in range(4):
                    mm = pe.matmul(pM[k % 2][0:T, T * j:T * (j + 1)], Qst[bslot(n)][0:ROWS, 4 * k + j, :],
                                   Kst[bslot(n)][0:ROWS, 4 * k + j, :], start=False, stop=True, skip_group_check=True)
                mm.then_inc(m_filled, 1)

            def e_tile(n, k):
                if n[0] is None and n[1] == k == 0:
                    pe.wait_ge(ones_in, 16 * BRING)
                if k == 0:
                    pe.wait_ge(mrow_in[bslot(n)], uses_value(n, 48))
                wait(pe, e_done, count(n, 4, k - 1))
                pe.matmul(pE[k % 2][0:T, 0:4 * T], identb[0:T, 0:T], far_t[:], start=True, stop=True)
                for j in range(4):
                    mm = pe.matmul(pE[k % 2][0:T, T * j:T * (j + 1)], Kst[bslot(n)][:, 4 * k + j, :],
                                   Qst[bslot(n)][:, 4 * k + j, :], start=False, stop=True, skip_group_check=True)
                mm.then_inc(e_filled, 1)

            def av(n, q):
                if q < 2:
                    wait(pe, o_ok, count(n, 2, q - 1))
                if q == 0:
                    pe.wait_ge(taken["p2"], count(n, 1, 1))
                pe.wait_ge(e_done, count(n, 4, q + 1))
                for j in range(4):
                    mm = pe.matmul(pA[q % 2][32 * j:32 * j + 32, T * (q // 2):T * (q // 2 + 1)], V[bslot(n)][:, 4 * q + j, :],
                                   probs[q][:, T * j:T * (j + 1)], start=True, stop=True)
                mm.then_inc(av_done, 1)

            def body(n):
                for step in ("m0 m1 f1 f0 m2 m3 p0 e0 p1 mA e1 f2 a0 p2 e2 a1 f3 e3 a2 a3").split():
                    k = int(step[1]) if step != "mA" else None
                    if step in NAMES:
                        use(n, step)
                    elif step[0] == "m":
                        if exists(later(n, 1)):
                            m_tile(later(n, 1), k)
                    elif exists(n):
                        (e_tile if step[0] == "e" else av)(n, k)

            schedule(pe, body, -3, B, **run)

        @block.vector
        def _(dve):
            loaded = (W["in"], W["in_value"])
            dve.wait_ge(*loaded)
            dve.wait_ge(consts_ok, 2 * BRING)

            def norm(n):
                dve.bn_stats(stats[:], at_batch(X1, n)).then_inc(ln_steps, 1)
                waits(dve, loaded, (ln_steps, count(n, 3, 1)))
                dve.bn_aggr(mv[:], stats[:]).then_inc(ln_steps, 1)
                dve.wait_ge(ln_steps, count(n, 3, 2))
                dve.tensor_scalar(ve[:], mv[:, 1:2], EPS, None, ALU.add).then_inc(ln_steps, 1)

            def norm_end(n):
                dve.wait_ge(rstd_ok, count(n, 1, 1))
                wait(dve, filled["p0"], count(n, 1, 0))
                dve.tensor_scalar(xn[:], at_batch(X1, n), mv[:, 0:1], rstd[:, 0:1], ALU.subtract, ALU.mult).then_inc(xn_ok, 1)
                dve.tensor_scalar(at_batch(EMB, n), at_batch(X1, n), mv[:, 0:1], rstd[:, 0:1], ALU.subtract, ALU.mult)

            def take(n, u):
                stage = later(n, dict(TURNS)[u])
                if not exists(stage):
                    return
                X = bank[u]
                dve.wait_ge(filled[u], count(stage, 1, 1))
                if u == "p1":
                    wait(dve, split_steps, count(stage, 4, 0))
                    dve.tensor_tensor(qk[:], X[:, 0:4 * T].rearrange("p (c t) -> p c t", t=T),
                                      qkb[:].unsqueeze(2).broadcast_to([128, 2 * KC, T]), ALU.add).then_inc(taken[u], 1)
                elif u == "p2":
                    wait(dve, av_done, count(stage, 4, 4 * (1 - BRING)))
                    wait(dve, filled["f1"], count(stage, 1, 1 - BRING))
                    dve.tensor_tensor(V[bslot(stage)][:, :, 0:HD], X[0:T, 0:D].rearrange("p (h d) -> p h d", h=H),
                                      vb[0:T, :].rearrange("p (h d) -> p h d", h=H), ALU.add).then_inc(taken[u], 1)
                elif u == "mA":
                    m = later(stage, -1)
                    if exists(m):
                        dve.wait_ge(mrow_in[bslot(m)], uses_value(m, 48))
                    dve.tensor_scalar(mrow[:, 0, :], X[0:H, 0:T], -1.0, None, ALU.mult).then_inc(m_steps, 1)
                    dve.wait_ge(m_steps, count(stage, 3, 1))
                    dve.scalar_tensor_tensor(mrem[:], X[0:H, 0:T], -1.0, mrow[:, 0, :], ALU.mult, ALU.subtract).then_inc(taken[u], 1)
                    waits(dve, loaded, (taken[u], count(stage, 1, 1)))
                    dve.tensor_copy(mrow[:, 1, :], mrem[:]).then_inc(m_steps, 1)
                    dve.wait_ge(m_steps, count(stage, 3, 2))
                    dve.tensor_tensor(mrow[:, 2, :], mrem[:], mrow[:, 1, :], ALU.subtract).then_inc(m_steps, 1)
                elif u == "f1":
                    dve.wait_ge(expm_ok, count(stage, 1, 1))
                    dve.tensor_tensor(later_sum[:], X[0:T, 0:H * (HD + 1)].rearrange("p (h d) -> p h d", h=H),
                                      expm[:].unsqueeze(2).broadcast_to([T, H, HD + 1]), ALU.mult).then_inc(taken[u], 1)
                elif u == "f0":
                    dve.wait_ge(taken["f1"], count(stage, 1, 1))
                    wait(dve, filled["f2"], count(stage, 1, 0))
                    wait(dve, hid_kept, count(stage, 1, 0))
                    dve.tensor_tensor(total[:], X[0:T, :].rearrange("p (h d) -> p h d", h=H)[:, :, 0:HD + 1],
                                      later_sum[:], ALU.add).then_inc(taken[u], 1)
                    dve.wait_ge(taken[u], count(stage, 1, 1))
                    dve.reciprocal(rec[:], total[:, :, HD]).then_inc(f_steps, 2)
                    dve.wait_ge(f_steps, count(stage, 4, 2))
                    dve.tensor_tensor(hid[:].rearrange("p (h d) -> p h d", h=H), total[:, :, 0:HD],
                                      rec[:].unsqueeze(2).broadcast_to([T, H, HD]), ALU.mult).then_inc(f_steps, 2)
                elif u == "f3":
                    dve.tensor_tensor(at_batch(RL, stage), X[0:T, 0:8], rb[0:T, :], ALU.add).then_inc(taken[u], 1)

            def body(n):
                nM, nP = later(n, 1), later(n, 3)

                def reduce(k):
                    if exists(nM):
                        dve.wait_ge(m_filled, count(nM, 4, k + 1))
                        dve.tensor_reduce(mxr[bslot(nM)][:, 4 * k:4 * k + 4], pM[k % 2][0:T, 0:4 * T].rearrange("p (h t) -> p h t", h=4),
                                          AX.X, ALU.max).then_inc(m_reduced, 1)

                if exists(nP):
                    norm(nP)
                reduce(0)
                if exists(nP):
                    norm_end(nP)
                reduce(1)
                take(n, "f1")
                take(n, "f0")
                reduce(2)
                reduce(3)
                if exists(nM):
                    dve.wait_ge(m_reduced, count(nM, 4, 4))
                    dve.tensor_scalar(mx[bslot(nM)][:], mxr[bslot(nM)][:], floor[0:T, 0:1], None, ALU.max).then_inc(m_floored, 1)
                take(n, "p1")
                take(n, "mA")
                take(n, "p2")
                take(n, "f3")

            schedule(dve, body, -3, B, **run)

        @block.scalar
        def _(act):
            def take(n, u):
                stage = later(n, dict(TURNS)[u])
                if not exists(stage):
                    return
                act.wait_ge(filled[u], count(stage, 1, 1))
                wait(act, filled["p2" if u == "p0" else "f3"], count(stage, 1, 0))
                out = xnT if u == "p0" else hidT
                act.activation(out[:].rearrange("p c t -> p (c t)"), bank[u][:, 0:KC * T], ACT.Copy).then_inc(taken[u], 1)

            def exp_tile(n, k):
                act.wait_ge(e_filled, count(n, 4, k + 1))
                wait(act, av_done, count(n, 4, k - 3))
                act.activation(probs[k][:], pE[k % 2][0:T, 0:4 * T], ACT.Exp, scale=D ** -0.5).then_inc(e_done, 1)

            def split(n, k):
                m, part = later(n, -2), parts[slot(n, 2)]
                if k == 0:
                    act.wait_ge(taken["p1"], count(n, 1, 1))
                    if exists(m):
                        act.wait_ge(qst_in[bslot(m)], uses_value(m, 16 * G))
                        act.wait_ge(kst_in[bslot(m)], uses_value(m, 16 * G))
                else:
                    act.wait_ge(split_steps, count(n, 4, 2))
                act.activation(part[:, k], rem[:] if k else qk[:], ACT.Copy).then_inc(split_steps, 1)

            def body(n):
                nF, nP = later(n, -1), later(n, 3)
                if exists(nF):
                    wait(act, taken["f1"], count(nF, 1, 0))
                    act.activation(expm[:], mx[bslot(nF)][:], ACT.Exp, scale=-D ** -0.5).then_inc(expm_ok, 1)
                take(n, "p0")
                if exists(n):
                    exp_tile(n, 0)
                if exists(nP):
                    split(nP, 0)
                if exists(n):
                    exp_tile(n, 1)
                if exists(nP):
                    split(nP, 1)
                take(n, "f2")
                if exists(n):
                    exp_tile(n, 2)
                    exp_tile(n, 3)
                    for a in range(2):
                        act.wait_ge(av_done, count(n, 4, a + 3))
                        wait(act, filled["f0"], count(n, 1, 0))
                        act.activation(O[:, a:4:2, :], pA[a][:, 0:2 * T].rearrange("p (q t) -> p q t", q=2), ACT.Copy).then_inc(o_ok, 1)

            schedule(act, body, -3, B, **run)


def chain(eng, sem):
    done = [0]

    def link(ins):
        done[0] += 1
        ins.then_inc(sem, 1)
        eng.wait_ge(sem, done[0])
    return link


def per_expert(t):
    return t.unsqueeze(2).broadcast_to([T, B, E])


def per_batch(t):
    return t.unsqueeze(1).broadcast_to([T, B, E])


def first_max(dve, link, logits, top, onehot, work, best, falling):
    link(dve.tensor_reduce(top[:], logits, AX.X, ALU.max))
    link(dve.tensor_tensor(work[:], logits, per_expert(top[:]), ALU.is_equal))
    link(dve.tensor_tensor(work[:], work[:], per_batch(falling[:]), ALU.mult))
    link(dve.tensor_reduce(best[:], work[:], AX.X, ALU.max))
    link(dve.tensor_tensor(onehot[:], work[:], per_expert(best[:]), ALU.is_equal))


def running_count(dve, link, totals, bufs):
    a, b = bufs
    link(dve.memset(a[:, 0:1, :], 0.0))
    link(dve.tensor_copy(a[:, 1:B, :], totals[:, 0:B - 1, :]))
    for d in (1, 2, 4, 8):
        link(dve.tensor_copy(b[:, 0:d, :], a[:, 0:d, :]))
        link(dve.tensor_tensor(b[:, d:B, :], a[:, d:B, :], a[:, 0:B - d, :], ALU.add))
        a, b = b, a


def first_mixture(nc, w, EMB, HID, RL, table, done_table, weight_kept, from_row, tables_zero, next_zero, next_zero_ok, consts):
    U32 = mybir.dt.uint32
    with ExitStack() as ctx:
        sb = lambda name, shape, dt=F32: ctx.enter_context(nc.sbuf_tensor("r_" + name, shape, dt))
        ps = lambda name: ctx.enter_context(nc.psum_tensor("r_" + name, [128, 512], F32))
        sem = lambda name: nc.alloc_semaphore("r_" + name)
        top, best = sb("top", [T, B]), sb("best", [T, B])
        falling, base = sb("falling", [T, E]), sb("base", [T, E])
        onehot, chosen, work, diff, expd = (sb(n_, [T, B, E]) for n_ in ("onehot", "chosen", "work", "diff", "expd"))
        counts = [sb(f"counts{k}", [T, B, E]) for k in range(2)]
        rank = sb("rank", [T, B, E])
        total, prob, kept, lost, row = (sb(n_, [T, B]) for n_ in ("total", "prob", "kept", "lost", "row"))
        to_row = sb("to_row", [T, B], U32)
        We, be = sb("We", [128, E, KC, D]), sb("be", [128, E, D])
        xs = [sb(f"xs{h}", [HALF, D]) for h in range(4)]
        xT = [sb(f"xT{h}", [128, KC, HALF]) for h in range(2)]
        ys = [sb(f"ys{h}", [HALF, D]) for h in range(2)]
        pR, pT, pY = ps("pR"), [ps(f"pT{h}") for h in range(2)], [ps(f"pY{h}") for h in range(2)]

        we_in, steps, onehot_ok, ranked, diff_ok, exp_ok = (sem(n_) for n_ in ("we_in", "steps", "onehot_ok", "ranked", "diff_ok", "exp_ok"))
        rows_ok, sent = sem("rows_ok"), sem("sent")
        xs_in = [sem(f"xs_in{h}") for h in range(4)]
        y_out = [sem(f"y_out{h}") for h in range(2)]
        turned, xT_ok, y_ok, ys_ok = sem("turned"), sem("xT_ok"), sem("y_ok"), sem("ys_ok")
        BLOCKS = 2 * E
        run = dict(first=-2, last=BLOCKS - 1, rolled=2, stride=4, turns=3)
        block = ctx.enter_context(nc.Block())

        @block.sync
        def _(sp):
            sp.dma_start(We[:], w["we"]).then_inc(we_in, 16)
            sp.dma_start(be[:].rearrange("p e d -> p (e d)"), w["be"].partition_broadcast(128)).then_inc(we_in, 16)
            for dst, src in next_zero:
                sp.dma_start(dst, src).then_inc(next_zero_ok, 16)
            sp.wait_ge(sent, 16 * B)
            ready = (sent, 16 * B)

            def body(n):
                nL = later(n, 2)
                if exists(nL, BLOCKS):
                    waits(sp, ready, (turned, count(nL, 1, -3)))
                    sp.dma_start(xs[slot(nL, 4)][:], table[at(nL, HALF), :]).then_inc(xs_in[slot(nL, 4)], 16)
                if exists(n, BLOCKS):
                    waits(sp, ready, (ys_ok, count(n, 1, 1)))
                    sp.dma_start(done_table[at(n, HALF), :], ys[slot(n, 2)][:]).then_inc(y_out[slot(n, 2)], 16)

            schedule(sp, body, **run)
            for h in range(2):
                sp.wait_ge(y_out[h], 16 * E)

        @block.scalar
        def _(act):
            act.wait_ge(diff_ok, 1)
            act.activation(expd[:], diff[:], ACT.Exp).then_inc(exp_ok, 1)

            def body(n):
                nL = later(n, 1)
                if exists(nL, BLOCKS):
                    act.wait_ge(turned, count(nL, 1, 1))
                    wait(act, y_ok, count(nL, 1, -1))
                    act.activation(xT[slot(nL, 2)][:].rearrange("p c t -> p (c t)"), pT[slot(nL, 2)][:, 0:KC * HALF], ACT.Copy).then_inc(xT_ok, 1)

            schedule(act, body, **run)

        @block.tensor
        def _(pe):
            pe.wait_ge(onehot_ok, 1)
            chosen_ = chosen[:].rearrange("p b e -> p (b e)")
            pe.matmul(pR[0:T, 0:B * E], consts["before"][:], chosen_, start=True, stop=True)
            pe.matmul(pR[0:T, B * E:2 * B * E], consts["ones"][:], chosen_, start=True, stop=True).then_inc(ranked, 1)
            pe.wait_ge(we_in, 32)

            def body(n):
                nL = later(n, 1)
                if exists(nL, BLOCKS):
                    pe.wait_ge(xs_in[slot(nL, 4)], uses_value(nL, 16))
                    wait(pe, xT_ok, count(nL, 1, -1))
                    for c in range(KC):
                        mm = pe.transpose(pT[slot(nL, 2)][:, HALF * c:HALF * (c + 1)], xs[slot(nL, 4)][:, 128 * c:128 * (c + 1)],
                                          consts["ident"][0:HALF, 0:HALF])
                    mm.then_inc(turned, 1)
                if exists(n, BLOCKS):
                    pe.wait_ge(xT_ok, count(n, 1, 1))
                    wait(pe, ys_ok, count(n, 1, -1))
                    e = uses(n, 2)
                    for c in range(KC):
                        mm = pe.matmul(pY[slot(n, 2)][0:HALF, 0:D], xT[slot(n, 2)][:, c, :],
                                       We[:].rearrange("p e c f -> p (e c f)")[:, bass.ds((e * KC + c) * D, D)], start=(c == 0), stop=(c == KC - 1))
                    mm.then_inc(y_ok, 1)

            schedule(pe, body, **run)

        @block.vector
        def _(dve):
            link = chain(dve, steps)
            numbers = consts["numbers"]
            link(dve.tensor_scalar(falling[:], numbers[:, 0:E], -1.0, float(E), ALU.mult, ALU.add))
            link(dve.tensor_scalar(base[:], numbers[:, 0:E], float(CAP), None, ALU.mult))
            first_max(dve, link, RL[:], top, onehot, work, best, falling)
            dve.tensor_tensor(diff[:], RL[:], per_expert(top[:]), ALU.subtract).then_inc(diff_ok, 1)
            dve.tensor_copy(chosen[:], onehot[:]).then_inc(onehot_ok, 1)
            dve.wait_ge(ranked, 1)
            ranks = pR[0:T, :].rearrange("p (k b e) -> p k b e", k=4, b=B)
            running_count(dve, link, ranks[:, 1], counts)
            link(dve.tensor_tensor(rank[:], ranks[:, 0], counts[0][:], ALU.add))
            link(dve.tensor_scalar(work[:], rank[:], float(CAP), None, ALU.is_lt))
            link(dve.tensor_tensor(work[:], work[:], onehot[:], ALU.mult))
            link(dve.tensor_reduce(kept[:], work[:], AX.X, ALU.add))
            link(dve.tensor_tensor(work[:], rank[:], per_batch(base[:]), ALU.add))
            link(dve.tensor_tensor(work[:], work[:], onehot[:], ALU.mult))
            link(dve.tensor_reduce(row[:], work[:], AX.X, ALU.add))
            link(dve.tensor_tensor(total[:], row[:], kept[:], ALU.mult))
            link(dve.tensor_copy(from_row[:], total[:]))
            link(dve.tensor_scalar(lost[:], kept[:], -float(4 * B * T), float(4 * B * T), ALU.mult, ALU.add))
            link(dve.tensor_tensor(row[:], row[:], lost[:], ALU.add))
            dve.tensor_copy(to_row[:], row[:]).then_inc(rows_ok, 1)
            dve.wait_ge(exp_ok, 1)
            link(dve.tensor_reduce(total[:], expd[:], AX.X, ALU.add))
            link(dve.reciprocal(prob[:], total[:]))
            link(dve.tensor_tensor(weight_kept[:], prob[:], kept[:], ALU.mult))
            link(dve.tensor_tensor(lost[:], prob[:], weight_kept[:], ALU.subtract))
            for b in range(B):
                dve.scalar_tensor_tensor(EMB[:, b, :], HID[:, b, :], lost[:, b:b + 1], EMB[:, b, :], ALU.mult, ALU.add)

            dve.wait_ge(we_in, 32)

            def body(n):
                if exists(n, BLOCKS):
                    dve.wait_ge(y_ok, count(n, 1, 1))
                    m = later(n, -2)
                    if exists(m, BLOCKS):
                        dve.wait_ge(y_out[slot(m, 2)], uses_value(m, 16, 2))
                    e = uses(n, 2)
                    dve.tensor_tensor(ys[slot(n, 2)][:], pY[slot(n, 2)][0:HALF, 0:D],
                                      be[0:HALF].rearrange("p e f -> p (e f)")[:, bass.ds(e * D, D)], ALU.add).then_inc(ys_ok, 1)

            schedule(dve, body, **run)

        @block.gpsimd
        def _(pool):
            pool.wait_ge(rows_ok, 1)
            pool.wait_ge(*tables_zero)
            for b in range(B):
                pool.indirect_dma_start(table, bass.IndirectOffsetOnAxis(ap=to_row[:, b:b + 1], axis=0), HID[:, b, :], None,
                                        bounds_check=E * CAP - 1, oob_is_err=False).then_inc(sent, 16)


def middle(nc, W, X, EMB, HID, RL, weight_kept, pooled_dram, done_table, from_row, loads, loads_in, consts):
    with ExitStack() as ctx:
        sb = lambda name, shape, dt=F32: ctx.enter_context(nc.sbuf_tensor("m_" + name, shape, dt))
        ps = lambda name: ctx.enter_context(nc.psum_tensor("m_" + name, [128, 512], F32))
        sem = lambda name: nc.alloc_semaphore("m_" + name)
        pair = lambda make, name, *shape: [make(f"{name}{h}", *shape) for h in range(2)]
        tg, neg_half, ident = consts["tgates"], consts["neg_half"], consts["ident"]
        gamma, beta, W1, Wr = (W[n_] for n_ in ("gamma", "beta", "w1", "wr2"))
        pooled = sb("pooled", [T, B, D])
        temp = pair(sb, "temp", [T, D])
        stats, mv, ve, rstd = ({k: pair(sb, name + k, [T, width]) for k in "ABD"}
                               for name, width in (("stats", 6), ("mv", 2), ("ve", 1), ("rstd", 1)))
        xn, xnT = ({k: pair(sb, name + k, shape) for k in "CR"} for name, shape in (("xn", [T, D]), ("xnT", [128, KC, T])))
        pT, pY = ({k: pair(ps, name + k) for k in "CR"} for name in ("pT", "pY"))

        gb_ok, part_in = sem("gb_ok"), sem("part_in")
        got = [sem(f"got{g}") for g in range(4)]
        shifted, x3_base, kept, logits_ok = (sem(n_) for n_ in ("shifted", "x3_base", "kept", "logits_ok"))
        steps = {k: sem("steps" + k) for k in "ABD"}
        STEPS = dict(A=4, B=5, D=4)
        rstd_ok = {k: sem("rstd_ok" + k) for k in "ABD"}
        xn_ok, turned, xnT_ok, mm_ok = ({k: sem(n_ + k) for k in "CR"} for n_ in ("xn_ok", "turned", "xnT_ok", "mm_ok"))
        OFFSET = dict(A=3, B=2, C=1, D=0, R=-1, L=-2)
        run = dict(first=-3, last=B + 1, rolled=4, stride=2, turns=4)
        block = ctx.enter_context(nc.Block())

        def at_stage(n, k):
            m = later(n, OFFSET[k])
            return m if exists(m) else None

        @block.sync
        def _(sp):
            sp.dma_start(pooled[:].rearrange("p b d -> p (b d)"), pooled_dram.rearrange("b d -> (b d)").partition_broadcast(T)).then_inc(part_in, 16)
            for g in range(4):
                sp.wait_ge(got[g], 16 * 4)
            for dst, src in loads:
                sp.dma_start(dst[:], src).then_inc(loads_in, 16)

        @block.gpsimd
        def _(pool):
            def fetch(g):
                for b in range(4 * g, 4 * g + 4):
                    pool.indirect_dma_start(HID[:, b, :], None, done_table, bass.IndirectOffsetOnAxis(ap=from_row[:, b:b + 1], axis=0)).then_inc(got[g], 16)

            fetch(0)
            pool.wait_ge(W["in"], W["in_value"])
            pool.tensor_scalar(gamma[:], gamma[:], tg[:, 2:3], None, ALU.mult).then_inc(gb_ok, 1)
            pool.tensor_scalar(beta[:], beta[:], tg[:, 2:3], None, ALU.mult).then_inc(gb_ok, 1)
            pool.wait_ge(gb_ok, 2)

            def power(n, k):
                m = at_stage(n, k)
                if m:
                    pool.wait_ge(steps[k], count(m, STEPS[k], STEPS[k]))
                    pool.tensor_tensor(rstd[k][slot(m, 2)][:], ve[k][slot(m, 2)][:], neg_half[0:T, :], ALU.pow).then_inc(rstd_ok[k], 1)

            def body(n):
                m = at_stage(n, "A")
                if m:
                    pool.tensor_tensor(at_batch(X, m), at_batch(X, m), beta[0:T, :], ALU.add).then_inc(shifted, 1)
                power(n, "A")
                power(n, "B")
                power(n, "D")
                m = at_stage(n, "C")
                if m:
                    if m[0] is None and m[1] == 0:
                        pool.wait_ge(part_in, 16)
                    pool.wait_ge(xn_ok["C"], count(m, 1, 1))
                    pool.tensor_tensor(at_batch(X, m), at_batch(X, m), at_batch(pooled, m), ALU.add).then_inc(x3_base, 1)

            for n in range(run["first"], run["rolled"]):
                body(batch(n))
                if n in (-3, -1, 1):
                    fetch((n + 5) // 2)
            schedule(pool, body, **dict(run, first=run["rolled"]))

        @block.tensor
        def _(pe):
            pe.wait_ge(W["in"], W["in_value"])
            def turn(n, k):
                m = at_stage(n, k)
                if m:
                    s = slot(m, 2)
                    pe.wait_ge(xn_ok[k], count(m, 1, 1))
                    wait(pe, xnT_ok[k], count(m, 1, -1))
                    for c in range(KC):
                        mm = pe.transpose(pT[k][s][:, T * c:T * (c + 1)], xn[k][s][:, 128 * c:128 * (c + 1)], ident[0:T, 0:T])
                    mm.then_inc(turned[k], 1)

            def multiply(n, k):
                m = at_stage(n, k)
                if m:
                    s = slot(m, 2)
                    W, width = dict(C=(W1, D), R=(Wr, E))[k]
                    pe.wait_ge(xnT_ok[k], count(m, 1, 1))
                    wait(pe, *((steps["D"], count(m, 4, -7)) if k == "C" else (logits_ok, count(m, 1, -1))))
                    for c in range(KC):
                        mm = pe.matmul(pY[k][s][0:T, 0:width], xnT[k][s][:, c, :], W[:, c, :], start=(c == 0), stop=(c == KC - 1))
                    mm.then_inc(mm_ok[k], 1)

            def body(n):
                turn(n, "C")
                turn(n, "R")
                multiply(n, "C")
                multiply(n, "R")

            schedule(pe, body, **run)

        @block.scalar
        def _(act):
            ready = (W["in"], W["in_value"])
            act.wait_ge(*ready)

            def turned_rows(n, k):
                m = at_stage(n, k)
                if m:
                    s = slot(m, 2)
                    act.wait_ge(turned[k], count(m, 1, 1))
                    wait(act, mm_ok[k], count(m, 1, -1))
                    act.activation(xnT[k][s][:].rearrange("p c t -> p (c t)"), pT[k][s][:, 0:KC * T], ACT.Copy).then_inc(xnT_ok[k], 1)

            def body(n):
                turned_rows(n, "C")
                turned_rows(n, "R")
                m = at_stage(n, "R")
                if m:
                    waits(act, ready, (xn_ok["R"], count(m, 1, 1)))
                    act.activation(at_batch(EMB, m), xn["R"][slot(m, 2)][:], ACT.Copy).then_inc(kept, 1)

            schedule(act, body, **run)

        @block.vector
        def _(dve):
            ready = (W["in"], W["in_value"])
            dve.wait_ge(*ready)
            dve.wait_ge(gb_ok, 2)

            def step(n, k, before, ins):
                if before:
                    waits(dve, ready, (steps[k], count(n, STEPS[k], before)))
                ins().then_inc(steps[k], 1)

            def sums(n, k):
                m = at_stage(n, k)
                if not m:
                    return
                s = slot(m, 2)
                if k == "A":
                    if m[0] is None and m[1] in (0, 4):
                        dve.wait_ge(got[m[1] // 4], 16 * 4)
                    weight = weight_kept[:, at(m)]
                    step(m, k, 0, lambda: dve.scalar_tensor_tensor(at_batch(EMB, m), at_batch(HID, m), weight, at_batch(EMB, m), ALU.mult, ALU.add))
                elif k == "B":
                    dve.wait_ge(rstd_ok["A"], count(m, 1, 1))
                    step(m, k, 0, lambda: dve.scalar_tensor_tensor(temp[s][:], at_batch(EMB, m), mv["A"][s][:, 0:1], gamma[0:T, :], ALU.subtract, ALU.mult))
                else:
                    dve.wait_ge(mm_ok["C"], count(m, 1, 1))
                    dve.wait_ge(x3_base, count(m, 1, 1))
                    step(m, k, 0, lambda: dve.scalar_tensor_tensor(at_batch(X, m), pY["C"][s][0:T, 0:D], tg[0:T, 1:2], at_batch(X, m), ALU.mult, ALU.add))

            def normed_sum(n):
                m = at_stage(n, "B")
                if m:
                    s = slot(m, 2)
                    dve.wait_ge(shifted, count(m, 1, 1))
                    step(m, "B", 1, lambda: dve.scalar_tensor_tensor(at_batch(X, m), temp[s][:], rstd["A"][s][:, 0:1], at_batch(X, m), ALU.mult, ALU.add))

            def statistics(n, k, part):
                m = at_stage(n, k)
                if not m:
                    return
                s, before = slot(m, 2), STEPS[k] - 3 + part
                rows = at_batch(EMB if k == "A" else X, m)
                step(m, k, before, (lambda: dve.bn_stats(stats[k][s][:], rows), lambda: dve.bn_aggr(mv[k][s][:], stats[k][s][:]),
                                    lambda: dve.tensor_scalar(ve[k][s][:], mv[k][s][:, 1:2], EPS, None, ALU.add))[part])

            def normalise(n, k):
                m = at_stage(n, k)
                if m:
                    s, of = slot(m, 2), "B" if k == "C" else "D"
                    dve.wait_ge(rstd_ok[of], count(m, 1, 1))
                    wait(dve, turned[k], count(m, 1, -1))
                    if k == "R":
                        wait(dve, kept, count(m, 1, -1))
                    dve.tensor_scalar(xn[k][s][:], at_batch(X, m), mv[of][s][:, 0:1], rstd[of][s][:, 0:1], ALU.subtract, ALU.mult).then_inc(xn_ok[k], 1)

            def body(n):
                sums(n, "A")
                sums(n, "B")
                statistics(n, "A", 0)
                normed_sum(n)
                sums(n, "D")
                normalise(n, "C")
                statistics(n, "A", 1)
                statistics(n, "B", 0)
                statistics(n, "D", 0)
                statistics(n, "A", 2)
                normalise(n, "R")
                statistics(n, "B", 1)
                statistics(n, "D", 1)
                statistics(n, "B", 2)
                statistics(n, "D", 2)
                m = at_stage(n, "L")
                if m:
                    waits(dve, ready, (mm_ok["R"], count(m, 1, 1)))
                    dve.tensor_copy(at_batch(RL, m), pY["R"][slot(m, 2)][0:T, 0:E]).then_inc(logits_ok, 1)

            for n in range(run["first"], run["rolled"]):
                body(batch(n))
            for g in (2, 3):
                dve.wait_ge(got[g], 16 * 4)
            schedule(dve, body, **dict(run, first=run["rolled"]))


def second_mixture(nc, Ws, X, EMB, HID, RL, table, done_table, tables_zero, out, consts):
    U32, I32 = mybir.dt.uint32, mybir.dt.int32
    W13, W2s, ws_in, ws_value = Ws
    with ExitStack() as ctx:
        sb = lambda name, shape, dt=F32: ctx.enter_context(nc.sbuf_tensor("t_" + name, shape, dt))
        ps = lambda name: ctx.enter_context(nc.psum_tensor("t_" + name, [128, 512], F32))
        sem = lambda name: nc.alloc_semaphore("t_" + name)
        NB, HC = E1_BLOCKS, HID2 // 128
        SIZES = (B * T + 127) // 128
        top = [sb(f"top{k}", [T, B]) for k in range(2)]
        best, falling = sb("best", [T, B]), sb("falling", [T, E])
        onehot = [sb(f"onehot{k}", [T, B, E]) for k in range(2)]
        work, masked, both, rank = (sb(n_, [T, B, E]) for n_ in ("work", "masked", "both", "rank"))
        counts = [sb(f"counts{k}", [T, B, E]) for k in range(2)]
        limits, over = sb("limits", [T, SIZES]), sb("over", [T, E, SIZES])
        sizes, nblocks, base = sb("sizes", [T, E]), sb("nblocks", [T, E]), sb("base", [T, E])
        ends = [sb(f"ends{k}", [T, E]) for k in range(2)]
        ended, idf, ids = sb("ended", [T, NB, E]), sb("idf", [T, NB]), sb("ids", [T, NB], I32)
        gap, ratio = sb("gap", [T, B]), sb("ratio", [T, B])
        factor = [sb(f"factor{k}", [T, B]) for k in range(2)]
        row = [sb(f"row{k}", [T, B]) for k in range(2)]
        rows = [sb(f"rows{k}", [T, B], U32) for k in range(2)]
        xs = [sb(f"xs{h}", [128, D]) for h in range(4)]
        xT = [sb(f"xT{h}", [128, KC, 128]) for h in range(2)]
        silu = [sb(f"silu{h}", [128, HID2]) for h in range(2)]
        act_ = [sb(f"act{h}", [128, HID2]) for h in range(2)]
        aT = [sb(f"aT{h}", [128, HC, 128]) for h in range(2)]
        ys = [sb(f"ys{h}", [128, D]) for h in range(2)]
        pT, pH, pG, pY = ([ps(f"p{c}{h}") for h in range(2)] for c in "THGY")

        steps, gap_ok, ratio_ok, both_ok, ranked, ids_ok, rows_ok = (sem(n_) for n_ in ("steps", "gap_ok", "ratio_ok", "both_ok", "ranked", "ids_ok", "rows_ok"))
        sent, summed, out_done = sem("sent"), sem("summed"), sem("out_done")
        got = [sem(f"got{g}") for g in range(4)]
        xs_in = [sem(f"xs_in{h}") for h in range(4)]
        y_out = [sem(f"y_out{h}") for h in range(2)]
        turned, xT_ok, h_ok, g_ok, silu_ok, act_ok = (sem(n_) for n_ in ("turned", "xT_ok", "h_ok", "g_ok", "silu_ok", "act_ok"))
        aturned, aT_ok, y_ok, ys_ok = (sem(n_) for n_ in ("aturned", "aT_ok", "y_ok", "ys_ok"))
        run = dict(first=-2, last=NB, rolled=2, stride=4, turns=(NB - 4) // 4)
        block = ctx.enter_context(nc.Block())

        @block.sync
        def _(sp):
            sp.wait_ge(sent, 16 * 2 * B)
            ready = (sent, 16 * 2 * B)

            def body(n):
                nL, nY = later(n, 2), later(n, -1)
                if exists(nL, NB):
                    waits(sp, ready, (turned, count(nL, 1, -3)))
                    sp.dma_start(xs[slot(nL, 4)][:], table[at(nL, 128), :]).then_inc(xs_in[slot(nL, 4)], 16)
                if exists(nY, NB):
                    waits(sp, ready, (ys_ok, count(nY, 1, 1)))
                    sp.dma_start(done_table[at(nY, 128), :], ys[slot(nY, 2)][:]).then_inc(y_out[slot(nY, 2)], 16)

            schedule(sp, body, **run)
            for b in range(B):
                sp.wait_ge(summed, 2 * (b + 1))
                sp.dma_start(out[b], X[:, b, :]).then_inc(out_done, 16)
            sp.wait_ge(out_done, 16 * B)

        @block.gpsimd
        def _(pool):
            pool.wait_ge(rows_ok, 2)
            pool.wait_ge(*tables_zero)
            for b in range(B):
                for k in range(2):
                    pool.indirect_dma_start(table, bass.IndirectOffsetOnAxis(ap=rows[k][:, b:b + 1], axis=0), EMB[:, b, :], None,
                                            bounds_check=NB * 128 - 1, oob_is_err=False).then_inc(sent, 16)
            pool.wait_ge(sent, 16 * 2 * B)
            for h in range(2):
                pool.wait_ge(y_out[h], 16 * NB // 2)
            for b in range(B):
                for k, to in enumerate((HID, EMB)):
                    pool.indirect_dma_start(to[:, b, :], None, done_table, bass.IndirectOffsetOnAxis(ap=rows[k][:, b:b + 1], axis=0)).then_inc(got[b // 4], 16)

        @block.tensor
        def _(pe):
            pe.wait_ge(both_ok, 1)
            chosen = both[:].rearrange("p b e -> p (b e)")
            pe.matmul(pY[0][0:T, 0:B * E], consts["before"][:], chosen, start=True, stop=True)
            pe.matmul(pY[0][0:T, B * E:2 * B * E], consts["ones"][:], chosen, start=True, stop=True).then_inc(ranked, 1)
            pe.wait_ge(ids_ok, 1)
            pe.wait_ge(ws_in, ws_value)
            up, down = W13[:].rearrange("p e k c f -> p (e k c f)"), W2s[:].rearrange("p e c f -> p (e c f)")

            def expert(n):
                return pe.value_load(ids[0:1, at(n)], min_val=0, max_val=E - 1)

            def body(n):
                nL, nY = later(n, 1), later(n, -1)
                if exists(nY, NB):
                    s = slot(nY, 2)
                    pe.wait_ge(act_ok, count(nY, 1, 1))
                    pe.wait_ge(xT_ok, count(nY, 1, 1))
                    for c in range(HC):
                        mm = pe.transpose(pT[s][:, 128 * c:128 * (c + 1)], act_[s][:, 128 * c:128 * (c + 1)], consts["ident"][:])
                    mm.then_inc(aturned, 1)
                if exists(n, NB):
                    s = slot(n, 2)
                    e = expert(n)
                    pe.wait_ge(xT_ok, count(n, 1, 1))
                    wait(pe, act_ok, count(n, 1, -1))
                    for k, (P, ok) in enumerate(((pH[s], h_ok), (pG[s], g_ok))):
                        for c in range(KC):
                            mm = pe.matmul(P[:, 0:HID2], xT[s][:, c, :], up[:, bass.ds(e * (2 * KC * HID2) + (k * KC + c) * HID2, HID2)],
                                           start=(c == 0), stop=(c == KC - 1))
                        mm.then_inc(ok, 1)
                if exists(nY, NB):
                    s = slot(nY, 2)
                    e = expert(nY)
                    pe.wait_ge(aT_ok, count(nY, 1, 1))
                    wait(pe, ys_ok, count(nY, 1, -1))
                    for c in range(HC):
                        mm = pe.matmul(pY[s][:, 0:D], aT[s][:, c, :], down[:, bass.ds(e * (HC * D) + c * D, D)], start=(c == 0), stop=(c == HC - 1))
                    mm.then_inc(y_ok, 1)
                if exists(nL, NB):
                    pe.wait_ge(xs_in[slot(nL, 4)], uses_value(nL, 16))
                    wait(pe, aT_ok, count(nL, 1, -1))
                    for c in range(KC):
                        mm = pe.transpose(pT[slot(nL, 2)][:, 128 * c:128 * (c + 1)], xs[slot(nL, 4)][:, 128 * c:128 * (c + 1)], consts["ident"][:])
                    mm.then_inc(turned, 1)

            schedule(pe, body, **run)

        @block.scalar
        def _(act):
            act.wait_ge(gap_ok, 1)
            act.activation(ratio[:], gap[:], ACT.Exp).then_inc(ratio_ok, 1)

            def body(n):
                nL, nY = later(n, 1), later(n, -1)
                if exists(nY, NB):
                    s = slot(nY, 2)
                    act.wait_ge(aturned, count(nY, 1, 1))
                    wait(act, y_ok, count(nY, 1, -1))
                    act.activation(aT[s][:].rearrange("p c t -> p (c t)"), pT[s][:, 0:HC * 128], ACT.Copy).then_inc(aT_ok, 1)
                if exists(n, NB):
                    s = slot(n, 2)
                    act.wait_ge(h_ok, count(n, 1, 1))
                    wait(act, act_ok, count(n, 1, -1))
                    act.activation(silu[s][:], pH[s][:, 0:HID2], ACT.Silu).then_inc(silu_ok, 1)
                if exists(nL, NB):
                    s = slot(nL, 2)
                    act.wait_ge(turned, count(nL, 1, 1))
                    wait(act, g_ok, count(nL, 1, -1))
                    act.activation(xT[s][:].rearrange("p c t -> p (c t)"), pT[s][:, 0:KC * 128], ACT.Copy).then_inc(xT_ok, 1)

            schedule(act, body, **run)

        @block.vector
        def _(dve):
            link = chain(dve, steps)
            numbers = consts["numbers"]
            link(dve.tensor_scalar(falling[:], numbers[:, 0:E], -1.0, float(E), ALU.mult, ALU.add))
            first_max(dve, link, RL[:], top[0], onehot[0], work, best, falling)
            link(dve.scalar_tensor_tensor(masked[:], onehot[0][:], -3.0e38, RL[:], ALU.mult, ALU.add))
            first_max(dve, link, masked[:], top[1], onehot[1], work, best, falling)
            dve.tensor_tensor(both[:], onehot[0][:], onehot[1][:], ALU.add).then_inc(both_ok, 1)
            dve.tensor_tensor(gap[:], top[1][:], top[0][:], ALU.subtract).then_inc(gap_ok, 1)
            dve.wait_ge(ratio_ok, 1)
            link(dve.tensor_scalar(work[:, :, 0], ratio[:], 1.0, None, ALU.add))
            link(dve.reciprocal(factor[0][:], work[:, :, 0]))
            link(dve.tensor_scalar(factor[0][:], factor[0][:], consts["tgates"][0:T, 3:4], None, ALU.mult))
            link(dve.tensor_tensor(factor[1][:], factor[0][:], ratio[:], ALU.mult))
            dve.wait_ge(ranked, 1)
            ranks = pY[0][0:T, :].rearrange("p (k b e) -> p k b e", k=4, b=B)
            running_count(dve, link, ranks[:, 1], counts)
            link(dve.tensor_tensor(rank[:], ranks[:, 0], counts[0][:], ALU.add))
            link(dve.tensor_tensor(sizes[:], ranks[:, 1, B - 1], counts[0][:, B - 1], ALU.add))
            link(dve.tensor_scalar(limits[:], numbers[:, 0:SIZES], 128.0, None, ALU.mult))
            link(dve.tensor_tensor(over[:], sizes[:].unsqueeze(2).broadcast_to([T, E, SIZES]), limits[:].unsqueeze(1).broadcast_to([T, E, SIZES]), ALU.is_gt))
            link(dve.tensor_reduce(nblocks[:], over[:], AX.X, ALU.add))
            a, b_ = nblocks, ends[0]
            for d in (1, 2, 4):
                link(dve.tensor_copy(b_[:, 0:d], a[:, 0:d]))
                link(dve.tensor_tensor(b_[:, d:E], a[:, d:E], a[:, 0:E - d], ALU.add))
                a, b_ = b_, ends[1] if b_ is ends[0] else ends[0]
            end = a
            link(dve.tensor_tensor(base[:], end[:], nblocks[:], ALU.subtract))
            link(dve.tensor_scalar(base[:], base[:], 128.0, None, ALU.mult))
            link(dve.tensor_tensor(rank[:], rank[:], per_batch(base[:]), ALU.add))
            for k in range(2):
                link(dve.tensor_tensor(work[:], rank[:], onehot[k][:], ALU.mult))
                link(dve.tensor_reduce(row[k][:], work[:], AX.X, ALU.add))
                dve.tensor_copy(rows[k][:], row[k][:]).then_inc(rows_ok, 1)
            link(dve.tensor_tensor(ended[:], end[:].unsqueeze(1).broadcast_to([T, NB, E]), numbers[:, 0:NB].unsqueeze(2).broadcast_to([T, NB, E]), ALU.is_le))
            link(dve.tensor_reduce(idf[:], ended[:], AX.X, ALU.add))
            link(dve.tensor_scalar(idf[:], idf[:], float(E - 1), None, ALU.min))
            dve.tensor_copy(ids[:], idf[:]).then_inc(ids_ok, 1)
            ready = (rows_ok, 2)

            def body(n):
                nY = later(n, -1)
                if exists(n, NB):
                    s = slot(n, 2)
                    dve.wait_ge(silu_ok, count(n, 1, 1))
                    dve.wait_ge(g_ok, count(n, 1, 1))
                    wait(dve, aturned, count(n, 1, -1))
                    dve.tensor_tensor(act_[s][:], silu[s][:], pG[s][:, 0:HID2], ALU.mult).then_inc(act_ok, 1)
                if exists(nY, NB):
                    s, m = slot(nY, 2), later(nY, -2)
                    pairs = [(y_ok, count(nY, 1, 1))]
                    if m[0] is not None or m[1] >= 0:
                        pairs.append((y_out[slot(m, 2)], uses_value(m, 16, 2)))
                    waits(dve, ready, *pairs)
                    dve.tensor_copy(ys[s][:], pY[s][:, 0:D]).then_inc(ys_ok, 1)

            schedule(dve, body, **run)
            for b in range(B):
                dve.wait_ge(got[b // 4], 16 * 2 * 4)
                for k, y in enumerate((HID, EMB)):
                    if k:
                        dve.wait_ge(summed, 2 * b + 1)
                    dve.scalar_tensor_tensor(X[:, b, :], y[:, b, :], factor[k][:, b:b + 1], X[:, b, :], ALU.mult, ALU.add).then_inc(summed, 1)


def build(nc, a, out):
    with ExitStack() as ctx:
        sb = lambda name, shape, dt=F32: ctx.enter_context(nc.sbuf_tensor(name, shape, dt))
        dram = lambda name, shape: nc.dram_tensor(name, shape, F32, kind="Internal").ap()
        table0, done0 = dram("table0", [E * CAP, D]), dram("done0", [E * CAP, D])
        table1, done1 = dram("table1", [E1_BLOCKS * 128, D]), dram("done1", [E1_BLOCKS * 128, D])
        pooled_dram = dram("pooled_context", [B, D])
        X, EMB, HID = sb("X", [T, B, D]), sb("EMB", [T, B, D]), sb("HID", [T, B, D])
        RL, weight_kept = sb("RL", [T, B, E]), sb("weight_kept", [T, B])
        from_row = sb("from_row", [T, B], mybir.dt.uint32)
        W = {name: sb(name, shape) for name, shape in dict(
            b_wq=[128, KC, D], b_wk=[128, KC, D], b_wv=[128, KC, D], b_wr=[128, KC, E], b_qkb=[128, 2 * KC], b_vb=[128, D],
            b_rb=[128, E], m_w1=[128, KC, D], m_w2=[128, KC, D], m_wr2=[128, KC, E], m_b1=[128, D], m_gamma=[128, D], m_beta=[128, D]).items()}
        prefetch = [(t[:], a[name] if len(a[name].shape) > 1 else a[name].partition_broadcast(128)) for name, t in W.items()]
        prefetched = nc.alloc_semaphore("prefetched")
        consts = constants(nc, ctx, a["gates"])
        prefetch += zeroed(table0, consts["zero"])
        group = lambda prefix, of=a: {k[len(prefix):]: v for k, v in of.items() if k.startswith(prefix)}
        loaded = {"in": prefetched, "in_value": 16 * len(prefetch)}
        with nc.cleanup_on_exit():
            cross_attention(nc, a["x"], a["ctxT"], group("a_"), X, (W["m_w2"], W["m_b1"], pooled_dram), prefetch, prefetched, consts)
        with nc.cleanup_on_exit():
            self_attention(nc, dict(group("b_", W), **loaded), X, EMB, HID, RL, consts)
        W13, W2s = sb("W13", [128, E, 2, KC, HID2]), sb("W2s", [128, E, HID2 // 128, D])
        ws_in, table1_zero = nc.alloc_semaphore("ws_in"), nc.alloc_semaphore("table1_zero")
        first_mixture(nc, group("r_"), EMB, HID, RL, table0, done0, weight_kept, from_row, (prefetched, 16 * len(prefetch)), zeroed(table1, consts["zero"]), table1_zero, consts)
        middle(nc, dict(group("m_", W), **loaded), X, EMB, HID, RL, weight_kept, pooled_dram, done0, from_row,
               ((W13, a["w13"]), (W2s, a["w2s"])), ws_in, consts)
        second_mixture(nc, (W13, W2s, ws_in, 32), X, EMB, HID, RL, table1, done1, (table1_zero, 16 * len(zeroed(table1, consts["zero"]))), out, consts)


def arrays_of(inputs):
    import numpy as np

    i = {k: np.asarray(v) for k, v in inputs.items()}
    order = np.array([(2 * (p % 8) + m) * HD + p // 8 for m in range(KC) for p in range(128)])

    def chunks(wt):
        return np.ascontiguousarray(wt.reshape(KC, 128, -1).transpose(1, 0, 2))

    def columns(v):
        return np.ascontiguousarray(v.reshape(-1, 128).T)

    win, bin_ = i["L0_xattn_in_proj_weight"], i["L0_xattn_in_proj_bias"]
    flat = lambda k: i["L0_ffn_" + k].reshape(D, D)
    W = i["L1_xattn_W"]
    up = np.stack([i["L1_ffn_W1"], i["L1_ffn_W3"]], axis=1)
    out = {
        "x": i["x"], "ctxT": i["ctx_1024"].reshape(B, S, KC, 128).transpose(0, 3, 2, 1),
        "gates": np.concatenate([i["g_xattn"], i["g_ffn"]]),
        "a_wq": chunks(win[0:D][order].T), "a_wk": chunks(win[D:2 * D][order].T), "a_wv": chunks(win[2 * D:].T),
        "a_wo": chunks(i["L0_xattn_out_proj_weight"].T), "a_qb": columns(bin_[0:D][order]), "a_kb": columns(bin_[D:2 * D][order]),
        "a_vb": columns(bin_[2 * D:]), "a_ob": i["L0_xattn_out_proj_bias"], "a_gate": i["g_xattn"][0:1],
        "a_lam": np.stack([i["L0_xattn_lambda_" + k] for k in ("q1", "k1", "q2", "k2")]).reshape(-1),
        "b_wq": chunks(flat("Wq")[order].T), "b_wk": chunks(flat("Wk")[order].T), "b_wv": chunks(flat("Wv").T),
        "b_wr": chunks(i["L0_ffn_Wsw"].T), "b_qkb": columns(np.concatenate([i["L0_ffn_bq"].reshape(D)[order], i["L0_ffn_bk"].reshape(D)[order]])),
        "b_vb": i["L0_ffn_bv"].reshape(D), "b_rb": i["L0_ffn_bsw"],
        "r_we": i["L0_ffn_We"].reshape(E, D, KC, 128).transpose(3, 0, 2, 1), "r_be": i["L0_ffn_be"].reshape(E * D),
        "m_w1": chunks(W[:, 0:D].T), "m_w2": chunks(W[:, D:].T), "m_wr2": chunks(i["L1_ffn_Wr"]), "m_b1": i["L1_xattn_b"],
        "m_gamma": i["L0_ffn_gamma"], "m_beta": i["L0_ffn_beta"],
        "w13": up.reshape(E, 2, KC, 128, HID2).transpose(3, 0, 1, 2, 4),
        "w2s": i["L1_ffn_W2"].reshape(E, HID2 // 128, 128, D).transpose(2, 0, 1, 3),
    }
    return {k: np.ascontiguousarray(v) for k, v in out.items()}


def kernel(**inputs):
    import concourse.bacc as _bacc
    from concourse.bass_utils import run_bass_kernel_spmd as _run

    nc = _bacc.Bacc("TRN2", target_bir_lowering=False, num_devices=1)
    arrays = arrays_of(inputs)
    args = {k: nc.dram_tensor("in_" + k, v.shape, mybir.dt.from_np(v.dtype), kind="ExternalInput").ap() for k, v in arrays.items()}
    out = nc.dram_tensor("out_x", (B, T, D), F32, kind="ExternalOutput").ap()
    build(nc, args, out)
    r = _run(nc, [{"in_" + k: v for k, v in arrays.items()}], core_ids=[0])
    return r.results[0]["out_x"]
```

```python
from contextlib import ExitStack
import math

import concourse.bass as bass
from concourse import mybir

F32 = mybir.dt.float32
BF16 = mybir.dt.bfloat16
ALU = mybir.AluOpType
ACT = mybir.ActivationFunctionType
AX = mybir.AxisListType

B, T, D = 16, 100, 256
S = 361
H, HD = 16, 16
SUB = HD // 2
KC = D // 128
SC = 3
SP_ = SC * 128
SCALING = 1.0 / math.sqrt(SUB)
LAMBDA_INIT = 0.8 - 0.6 * math.exp(-0.3 * 0)
EPS = 1e-5
RING = 3
BRING = 4

K_PARTS = (0, 0, 0, 1, 1, 2)
Q_PARTS = (0, 1, 2, 0, 1, 0)
G = len(K_PARTS)
E = 8
CAP = int(1.2 * B * T / E)
HALF = CAP // 2
HID2 = D * 3 // 2
E1_BLOCKS = (2 * B * T + E * 127) // 128
ROWS = 16 * G


def batch(off, i=None, stride=3):
    return (i, off, stride)


def later(n, d):
    return (n[0], n[1] + d, n[2])


def count(n, per, extra):
    return n[1] * per + extra if n[0] is None else n[0] * (n[2] * per) + (n[1] * per + extra)


def slot(n, ring=3):
    return n[1] % ring


def uses(n, ring=None):
    ring = ring or n[2]
    return n[1] // ring if n[0] is None else n[0] * (n[2] // ring) + n[1] // ring


def uses_value(n, per, ring=None):
    return (uses(n, ring) + 1) * per


def exists(n, total=16):
    return n[0] is not None or 0 <= n[1] < total


def at(n, width=1):
    if n[0] is None:
        return slice(n[1] * width, n[1] * width + width)
    return bass.ds(n[0] * (n[2] * width) + n[1] * width, width)


def at_batch(tensor, n):
    return tensor[:, n[1], :] if n[0] is None else tensor[:, at(n), :].rearrange("p b d -> p (b d)")


def wait(eng, sem, value):
    if not isinstance(value, int) or value > 0:
        eng.wait_ge(sem, value)


def waits(eng, settled, *pairs):
    if all(isinstance(v, int) for _, v in pairs):
        for sem, value in pairs:
            wait(eng, sem, value)
        return
    values = [(sem, v if isinstance(v, int) else eng.snap(eng.to_reg(v))) for sem, v in pairs]
    eng.wait_ge(*settled)
    for sem, value in values:
        wait(eng, sem, value)


def schedule(eng, body, first, last, rolled=2, stride=3, turns=4):
    for n in range(first, rolled):
        body(batch(n, stride=stride))
    with eng.Fori(0, turns) as i:
        for u in range(stride):
            body(batch(rolled + u, i, stride))
    for n in range(rolled + stride * turns, last + 1):
        body(batch(n, stride=stride))


def cross_attention(nc, x, ctxT, w, X1, pooled, prefetch, prefetched, zeros, zeros_out, consts):
    with ExitStack() as ctx:
        sb = lambda name, shape, dt=F32: ctx.enter_context(nc.sbuf_tensor("a_" + name, shape, dt))
        ps = lambda name: ctx.enter_context(nc.psum_tensor("a_" + name, [128, 512], F32))
        sem = lambda name: nc.alloc_semaphore("a_" + name)
        ring = lambda name, shape, dt=F32: [sb(f"{name}{s}", shape, dt) for s in range(RING)]

        ident, neg_half = consts["ident"], consts["neg_half"]
        W2, b1, pooled_dram = pooled
        summed = sb("summed", [128, S])
        csum, part = sb("csum", [128, KC, B]), sb("part", [B, D])
        Wq, Wk, Wv, Wo = (sb(n_, [128, KC, D]) for n_ in ("Wq", "Wk", "Wv", "Wo"))
        qb, kb = sb("qb", [128, KC]), sb("kb", [128, KC])
        vb, ob = sb("vb", [128, KC]), sb("ob", [128, D])
        vbs, both = sb("vbs", [128, KC, T]), sb("both", [128, 1])
        lamv = sb("lamv", [128, 4, SUB])
        lamp = sb("lamp", [128, 2, SUB])
        lamd, lame, lam = sb("lamd", [128, 2]), sb("lame", [128, 2]), sb("lam", [128, 1])
        gate, tgate = sb("gate", [128, 1]), sb("tgate", [128, 1])
        coef = sb("coef", [128, 4, 4])

        xin = ring("xin", [T, D])
        ctxs = ring("ctx", [128, KC, S])
        Kst = ring("Kst", [ROWS + 2, H, SP_], BF16)
        Qst = ring("Qst", [ROWS + 2, H, 2 * T], BF16)
        V = ring("V", [128, SC, H, 32])
        mx = ring("mx", [T, 2 * H])
        xres = ring("xres", [T, D])
        stats, mv = sb("stats", [T, 6]), sb("mv", [T, 2])
        ve, rstd = sb("ve", [T, 1]), sb("rstd", [T, 1])
        xn, xnT = sb("xn", [T, D]), sb("xnT", [128, KC, T])
        qf = sb("qf", [128, KC, 2, T])
        kf = sb("kf", [128, KC, S])
        qrem, krem = sb("qrem", [128, KC, 2 * T]), sb("krem", [128, KC, S])
        qpart, kpart = sb("qpart", [128, 3, KC, 2 * T], BF16), sb("kpart", [128, 3, KC, S], BF16)
        mrow = [sb(f"mrow{a}", [H, 2, T], BF16) for a in range(2)]
        probs = [sb(f"probs{k}", [128, 4 * T]) for k in range(6)]
        O = sb("O", [128, 4, 2 * T])
        rec, rc = sb("rec", [T, 2, 4, 4]), sb("rc", [T, 2, 4, 4])
        numer = sb("numer", [T, 2, 4, 4, HD])
        attn, attnT = sb("attn", [T, D]), sb("attnT", [128, KC, T])

        pM, pE, pX = ([ps(f"p{c}{s}") for s in range(k)] for c, k in (("M", 3), ("E", 2), ("X", 2)))
        pA = ps("pA")

        weights_in, gates_in, consts_ok = sem("weights_in"), sem("gates_in"), sem("consts_ok")
        lam_prod, lam_dot, lam_exp, lam_ok, coef_ok = (sem(n_) for n_ in ("lam_prod", "lam_dot", "lam_exp", "lam_ok", "coef_ok"))
        tgate_ok, vbs_ok, bias_ps, ob_ok = (sem(n_) for n_ in ("tgate_ok", "vbs_ok", "bias_ps", "ob_ok"))
        ones_in, v_init = sem("ones_in"), sem("v_init")
        x_in = [sem(f"x_in{s}") for s in range(RING)]
        ctx_in = [sem(f"ctx_in{s}") for s in range(RING)]
        res_in = [sem(f"res_in{s}") for s in range(RING)]
        kst_in = [sem(f"kst_in{s}") for s in range(RING)]
        qst_in = [sem(f"qst_in{s}") for s in range(RING)]
        mrow_in = [[sem(f"mrow_in{a}{s}") for s in range(RING)] for a in range(2)]
        ln_steps, rstd_ok, xn_ok = sem("ln_steps"), sem("rstd_ok"), sem("xn_ok")
        csum_ok = sem("csum_ok")
        qsplit, ksplit = sem("qsplit"), sem("ksplit")
        m_filled, m_reduced = sem("m_filled"), sem("m_reduced")
        e_filled, e_done = sem("e_filled"), sem("e_done")
        av_done, o_ok = sem("av_done"), sem("o_ok")
        msplit = [sem(f"msplit{a}") for a in range(2)]
        f_steps = sem("f_steps")
        resb_ok = sem("resb_ok")
        part_ps, part_ok, part_out = sem("part_ps"), sem("part_ok"), sem("part_out")

        TURNS = [("f0", -1), ("f1", -1), ("p0", 2), ("p1", 2), ("p2", 2), ("f2", -1), ("p3", 2),
                 ("f3", -1), ("p4", 2), ("mA", 1), ("p5", 2), ("p6", 2), ("mB", 1)]
        NAMES = [u for u, _ in TURNS]
        filled = {u: sem("filled_" + u) for u in NAMES}
        taken = {u: sem("taken_" + u) for u in NAMES}
        bank = {u: pX[k % 2] for k, u in enumerate(NAMES)}

        def free_bank(eng, n, u):
            k = NAMES.index(u)
            before = [(n, *t) for t in TURNS[:k]][::-1] + [(later(n, -1), *t) for t in TURNS][::-1]
            for m, name, d in before:
                if bank[name] is bank[u] and exists(later(m, d)):
                    wait(eng, taken[name], count(later(m, d), 1, 1))
                    return

        def m_tiles(k):
            before = lambda k: 2 * k // 3 if k <= 6 else 4 + 28 * (k - 6) // 18
            return range(before(k), before(k + 1))

        def m_bank(n, j):
            return (32 * n[1] + j) % 3

        block = ctx.enter_context(nc.Block())

        @block.sync
        def _(sp):
            loaded = (weights_in, 16 * 7)
            sp.dma_start(xin[0][:], x[0:1]).then_inc(x_in[0], 16)
            for dst, name in ((Wq, "wq"), (qb, "qb"), (Wk, "wk"), (kb, "kb")):
                sp.dma_start(dst[:], w[name]).then_inc(weights_in, 16)
            sp.dma_start(ctxs[0][:], ctxT[0:1]).then_inc(ctx_in[0], 16)
            for dst, name in ((Wv, "wv"), (Wo, "wo"), (vb, "vb")):
                sp.dma_start(dst[:], w[name]).then_inc(weights_in, 16)
            sp.wait_ge(consts["made"], consts["made_value"])
            sp.wait_ge(consts_ok, RING)
            for s in range(RING):
                sp.dma_start(Kst[s][ROWS:ROWS + 2, :, 0:S], consts["onesb"][0:2 * H, :]).then_inc(ones_in, 16)

            def load(n):
                waits(sp, loaded, (xn_ok, count(n, 1, 1 - RING)))
                waits(sp, loaded, (filled["p6"], count(n, 1, 1 - RING)))
                waits(sp, loaded, (csum_ok, count(n, 2, 2 * (1 - RING))))
                sp.dma_start(xin[slot(n)][:], x[at(n)]).then_inc(x_in[slot(n)], 16)
                sp.dma_start(ctxs[slot(n)][:], ctxT[at(n)]).then_inc(ctx_in[slot(n)], 16)

            def body(n):
                nF, nM, nP, nL = later(n, -1), later(n, 1), later(n, 2), later(n, 3)
                if exists(nL):
                    load(nL)
                if exists(nF):
                    sp.dma_start(xres[slot(nF)][:], x[at(nF)]).then_inc(res_in[slot(nF)], 16)
                if exists(nP):
                    waits(sp, loaded, (e_filled, count(nP, 24, 24 * (1 - RING))))
                    stack(nP, Qst[slot(nP)], qpart, Q_PARTS, qsplit, qst_in, 2 * T)
                if exists(nM):
                    rows(nM, 0)
                if exists(nP):
                    stack(nP, Kst[slot(nP)], kpart, K_PARTS, ksplit, kst_in, S)
                if exists(nM):
                    rows(nM, 1)

            def stack(n, to, part, parts, steps, sent, width):
                for k in range(3):
                    waits(sp, loaded, (steps, count(n, 4, (1, 3, 4)[k])))
                    for g in range(G):
                        if parts[g] == k:
                            sp.dma_start(to[16 * g:16 * g + 16, :, 0:width], part[:, k]).then_inc(sent[slot(n)], 16)

            def rows(n, a):
                waits(sp, loaded, (taken["m" + "AB"[a]], count(n, 1, 1)))
                for r in range(2):
                    sp.dma_start(Qst[slot(n)][ROWS + r:ROWS + r + 1, 8 * a:8 * a + 8, :], mrow[a][:, r, :]).then_inc(mrow_in[a][slot(n)], 16)

            for n in (-2, -1, 0):
                body(batch(n))
            for dst, src in prefetch:
                sp.dma_start(dst, src).then_inc(prefetched, 16)
            schedule(sp, body, 1, B, rolled=1)
            for dst, src in zeros:
                sp.dma_start(dst, src).then_inc(zeros_out, 16)
            sp.wait_ge(part_ok, 2)
            sp.dma_start(pooled_dram, part[:]).then_inc(part_out, 16)
            sp.wait_ge(part_out, 16)

        @block.gpsimd
        def _(pool):
            consts["fill"](pool)
            for s in range(RING):
                pool.memset(Kst[s][:, :, S:SP_], 0.0).then_inc(consts_ok, 1)
            started = (consts_ok, RING)
            pool.wait_ge(*started)

            def split(n, full, rem, part, steps):
                src = full[:].rearrange("p c s t -> p c (s t)") if full is qf else full[:]
                for k in range(2):
                    pool.wait_ge(steps, count(n, 4, 2 * k + 1))
                    pool.tensor_tensor(part[:, 2] if k else rem[:], rem[:] if k else src, part[:, k], ALU.subtract).then_inc(steps, 1)

            def body(n):
                nF, nP = later(n, -1), later(n, 2)
                if exists(nP):
                    pool.wait_ge(ln_steps, count(nP, 3, 3))
                    pool.tensor_tensor(rstd[:], ve[:], neg_half[0:T, :], ALU.pow).then_inc(rstd_ok, 1)
                if exists(nF):
                    if nF[0] is None and nF[1] == 0:
                        pool.wait_ge(ob_ok, 2)
                    pool.wait_ge(res_in[slot(nF)], uses_value(nF, 16))
                    pool.tensor_tensor(xres[slot(nF)][:], xres[slot(nF)][:], ob[0:T, :], ALU.add).then_inc(resb_ok, 1)
                if exists(nP):
                    split(nP, qf, qrem, qpart, qsplit)
                    split(nP, kf, krem, kpart, ksplit)

            schedule(pool, body, -2, B)

        AT = dict(f0=0, f1=2, p0=3, p1=5, p2=7, f2=8, p3=9, f3=11, p4=12, mA=15, p5=16, p6=18, mB=24)

        @block.tensor
        def _(pe):
            pe.wait_ge(consts["made"], consts["made_value"])
            pe.wait_ge(weights_in, 16 * 7)

            def use(n, u):
                stage = later(n, dict(TURNS)[u])
                if not exists(stage):
                    return
                free_bank(pe, n, u)
                X = bank[u]
                if u == "p0":
                    pe.wait_ge(xn_ok, count(stage, 1, 1))
                    for c in range(KC):
                        mm = pe.transpose(X[:, T * c:T * (c + 1)], xn[:, 128 * c:128 * (c + 1)], ident[0:T, 0:T])
                elif u == "p1":
                    pe.wait_ge(taken["p0"], count(stage, 1, 1))
                    for m in range(KC):
                        for c in range(KC):
                            mm = pe.matmul(X[:, T * m:T * (m + 1)], Wq[:, c, 128 * m:128 * (m + 1)], xnT[:, c, :], start=(c == 0), stop=(c == KC - 1))
                elif u in ("p2", "p3"):
                    m = int(u[1]) - 2
                    pe.wait_ge(ctx_in[slot(stage)], uses_value(stage, 16))
                    for c in range(KC):
                        mm = pe.matmul(X[:, 0:S], Wk[:, c, 128 * m:128 * (m + 1)], ctxs[slot(stage)][:, c, :], start=(c == 0), stop=(c == KC - 1))
                elif u in ("p4", "p5", "p6"):
                    k = int(u[1]) - 4
                    r = min(128, S - 128 * k)
                    for c in range(KC):
                        mm = pe.matmul(X[0:r, 0:D], ctxs[slot(stage)][:, c, 128 * k:128 * k + r], Wv[:, c, :], start=(c == 0), stop=(c == KC - 1))
                elif u in ("mA", "mB"):
                    a = "AB".index(u[1])
                    pe.wait_ge(m_reduced, count(stage, 32, 16 * (a + 1)))
                    mm = pe.transpose(X[0:16, 0:T], mx[slot(stage)][:, 16 * a:16 * a + 16], ident[0:T, 0:T])
                elif u in ("f0", "f1"):
                    f = int(u[1])
                    pe.wait_ge(o_ok, count(stage, 4, 2 * f + 2))
                    for q in range(2):
                        for s in range(2):
                            k = 2 * q + s
                            mm = pe.transpose(X[0:T, 128 * k:128 * (k + 1)], O[:, 2 * f + q, T * s:T * (s + 1)], ident[:])
                elif u == "f2":
                    pe.wait_ge(f_steps, count(stage, 6, 6))
                    for c in range(KC):
                        mm = pe.transpose(X[:, T * c:T * (c + 1)], attn[:, 128 * c:128 * (c + 1)], ident[0:T, 0:T])
                elif u == "f3":
                    pe.wait_ge(taken["f2"], count(stage, 1, 1))
                    for c in range(KC):
                        mm = pe.matmul(X[0:T, 0:D], attnT[:, c, :], Wo[:, c, :], start=(c == 0), stop=(c == KC - 1))
                mm.then_inc(filled[u], 1)

            def e_tile(n, k):
                q, c, half = k // 6, k % 6 // 2, k % 2
                if n[0] is None and n[1] == k == 0:
                    pe.wait_ge(consts_ok, RING)
                    pe.wait_ge(ones_in, 16 * RING)
                    pe.wait_ge(ob_ok, 1)
                if k in (0, 12):
                    pe.wait_ge(mrow_in[k // 12][slot(n)], uses_value(n, 32))
                wait(pe, e_done, count(n, 24, k - 1))
                for j in range(2):
                    h = 4 * q + 2 * half + j
                    mm = pe.matmul(pE[k % 2][:, 2 * T * j:2 * T * (j + 1)], Kst[slot(n)][:, h, 128 * c:128 * (c + 1)],
                                   Qst[slot(n)][:, h, :], start=True, stop=True)
                mm.then_inc(e_filled, 1)

            def m_tile(n, j):
                if j == 0:
                    pe.wait_ge(qst_in[slot(n)], uses_value(n, 16 * G))
                    pe.wait_ge(kst_in[slot(n)], uses_value(n, 16 * G))
                wait(pe, m_reduced, count(n, 32, j - 2))
                pe.matmul(pM[m_bank(n, j)][0:T, 0:S], Qst[slot(n)][0:ROWS, j // 2, T * (j % 2):T * (j % 2 + 1)],
                          Kst[slot(n)][0:ROWS, j // 2, 0:S], start=True, stop=True).then_inc(m_filled, 1)

            def av(n, g):
                q, c = g // 3, g % 3
                if g == 0:
                    pe.wait_ge(taken["p6"], count(n, 1, 1))
                    if n[0] is None and n[1] == 0:
                        pe.wait_ge(v_init, 6)
                if c == 0:
                    wait(pe, o_ok, count(n, 4, q))
                pe.wait_ge(e_done, count(n, 24, 2 * g + 2))
                for j in range(4):
                    mm = pe.matmul(pA[32 * j:32 * j + 32, 0:2 * T], V[slot(n)][:, c, 4 * q + j, :],
                                   probs[(2 * g + j // 2) % 6][:, 2 * T * (j % 2):2 * T * (j % 2 + 1)],
                                   start=(c == 0), stop=(c == SC - 1))
                mm.then_inc(av_done, 1)

            def body(n):
                for k in range(24):
                    if exists(n):
                        e_tile(n, k)
                    if exists(later(n, 1)):
                        for j in m_tiles(k):
                            m_tile(later(n, 1), j)
                    if exists(n) and k % 2 and k >= 3:
                        av(n, k // 2 - 1)
                    for u in NAMES:
                        if AT[u] == k:
                            use(n, u)
                if exists(n):
                    av(n, 11)
                use(n, "mB")

            body(batch(-2))
            pe.wait_ge(vbs_ok, 1)
            for c in range(KC):
                mm = pe.matmul(pE[0][0:T, 0:D], vbs[:, c, :], Wo[:, c, :], start=(c == 0), stop=(c == KC - 1))
            mm.then_inc(bias_ps, 1)
            schedule(pe, body, -1, B)
            pe.wait_ge(csum_ok, 2 * B)
            pe.wait_ge(prefetched, 16 * len(prefetch))
            pe.wait_ge(m_reduced, 32 * B)
            for c in range(KC):
                mm = pe.matmul(pM[0][0:B, 0:D], csum[:, c, :], W2[:, c, :], start=(c == 0), stop=(c == KC - 1))
            mm.then_inc(part_ps, 1)

        @block.vector
        def _(dve):
            for s in range(RING):
                dve.memset(V[s][:], 0.0).then_inc(v_init, 1)
            dve.wait_ge(v_init, RING)
            for s in range(RING):
                dve.memset(V[s][:, 0:2, :, HD:HD + 1], 1.0).then_inc(v_init, 1)
                dve.memset(V[s][0:S - 256, 2, :, HD:HD + 1], 1.0)
            dve.memset(qf[:], 0.0)
            dve.wait_ge(gates_in, 16 * 3)
            dve.tensor_tensor(lamp[:], lamv[:, 0:4:2, :], lamv[:, 1:4:2, :], ALU.mult).then_inc(lam_prod, 1)
            dve.wait_ge(lam_prod, 1)
            dve.tensor_reduce(lamd[:], lamp[:], AX.X, ALU.add).then_inc(lam_dot, 1)
            dve.wait_ge(lam_exp, 1)
            dve.tensor_tensor(lam[:], lame[:, 1:2], lame[:, 0:1], ALU.subtract).then_inc(lam_ok, 1)
            dve.wait_ge(lam_ok, 1)
            dve.tensor_scalar(lam[:], lam[:], -LAMBDA_INIT, 1.0 - LAMBDA_INIT, ALU.add, ALU.mult).then_inc(lam_ok, 1)
            dve.memset(coef[:], 1.0 - LAMBDA_INIT).then_inc(coef_ok, 1)
            dve.wait_ge(lam_ok, 2)
            dve.wait_ge(coef_ok, 1)
            dve.tensor_scalar(coef[:, 1:4:2, :], coef[:, 1:4:2, :], 0.0, lam[:, 0:1], ALU.mult, ALU.add).then_inc(coef_ok, 1)
            dve.wait_ge(coef_ok, 2)
            loaded = (weights_in, 16 * 7)
            dve.wait_ge(*loaded)
            dve.tensor_scalar(both[:], lam[:], 1.0 - LAMBDA_INIT, None, ALU.add).then_inc(coef_ok, 1)
            dve.wait_ge(coef_ok, 3)
            dve.tensor_scalar(vbs[:], vb[:].unsqueeze(2).broadcast_to([128, KC, T]), both[:, 0:1], None, ALU.mult).then_inc(vbs_ok, 1)

            def norm(n):
                s = slot(n)
                dve.wait_ge(x_in[s], uses_value(n, 16))
                dve.bn_stats(stats[:], xin[s][:]).then_inc(ln_steps, 1)
                waits(dve, loaded, (ln_steps, count(n, 3, 1)))
                dve.bn_aggr(mv[:], stats[:]).then_inc(ln_steps, 1)
                dve.wait_ge(ln_steps, count(n, 3, 2))
                dve.tensor_scalar(ve[:], mv[:, 1:2], EPS, None, ALU.add).then_inc(ln_steps, 1)

            def norm_end(n):
                dve.wait_ge(rstd_ok, count(n, 1, 1))
                wait(dve, filled["p0"], count(n, 1, 0))
                dve.tensor_scalar(xn[:], xin[slot(n)][:], mv[:, 0:1], rstd[:, 0:1], ALU.subtract, ALU.mult).then_inc(xn_ok, 1)

            def take(n, u):
                stage = later(n, dict(TURNS)[u])
                if not exists(stage):
                    return
                X = bank[u]
                dve.wait_ge(filled[u], count(stage, 1, 1))
                if u == "p1":
                    wait(dve, qsplit, count(stage, 4, 0))
                    for s in range(2):
                        r = slice(64 * s, 64 * s + 64)
                        ins = dve.tensor_tensor(qf[r, :, s, :], X[r, 0:2 * T].rearrange("p (c t) -> p c t", c=KC),
                                                qb[r, :].unsqueeze(2).broadcast_to([64, KC, T]), ALU.add)
                    ins.then_inc(taken[u], 1)
                elif u in ("mA", "mB"):
                    a = "AB".index(u[1])
                    m = later(stage, -1)
                    if exists(m):
                        dve.wait_ge(mrow_in[a][slot(m)], uses_value(m, 32))
                    dve.tensor_scalar(mrow[a][:, 0, :], X[0:16, 0:T], -1.0, None, ALU.mult).then_inc(msplit[a], 1)
                    dve.wait_ge(msplit[a], count(stage, 1, 1))
                    dve.scalar_tensor_tensor(mrow[a][:, 1, :], X[0:16, 0:T], -1.0, mrow[a][:, 0, :], ALU.mult, ALU.subtract).then_inc(taken[u], 1)
                elif u in ("f0", "f1"):
                    f = int(u[1])
                    sums = X[0:T, :].rearrange("p (k j d) -> p k j d", k=4, j=4)
                    dve.reciprocal(rec[:, f], sums[:, :, :, HD]).then_inc(f_steps, 1)
                    dve.wait_ge(f_steps, count(stage, 6, 3 * f + 1))
                    dve.tensor_tensor(rc[:, f], rec[:, f], coef[0:T], ALU.mult).then_inc(f_steps, 1)
                    dve.wait_ge(f_steps, count(stage, 6, 3 * f + 2))
                    dve.tensor_tensor(numer[:, f], sums[:, :, :, 0:HD], rc[:, f].unsqueeze(3).broadcast_to([T, 4, 4, HD]), ALU.mult).then_inc(taken[u], 1)
                    dve.wait_ge(taken[u], count(stage, 1, 1))
                    two = numer[:, f].rearrange("p (q s) j d -> p q s (j d)", s=2)
                    dve.tensor_tensor(attn[:, 128 * f:128 * f + 128].rearrange("p (q x) -> p q x", q=2),
                                      two[:, :, 0], two[:, :, 1], ALU.add).then_inc(f_steps, 1)
                elif u == "f3":
                    dve.wait_ge(resb_ok, count(stage, 1, 1))
                    dve.scalar_tensor_tensor(at_batch(X1, stage), X[0:T, 0:D], tgate[0:T, 0:1], xres[slot(stage)][:], ALU.mult, ALU.add).then_inc(taken[u], 1)

            def body(n):
                nM, nP = later(n, 1), later(n, 2)
                if exists(nP):
                    norm(nP)
                for k in range(25):
                    for u in ("f0", "f1", "p1", "f3", "mA", "mB"):
                        if AT[u] == k - 1:
                            take(n, u)
                    if k == 1 and exists(nP):
                        norm_end(nP)
                    if k < 24 and exists(nM):
                        for j in m_tiles(k):
                            dve.wait_ge(m_filled, count(nM, 32, j + 1))
                            dve.tensor_reduce(mx[slot(nM)][:, j:j + 1], pM[m_bank(nM, j)][0:T, 0:S], AX.X, ALU.max).then_inc(m_reduced, 1)
                take(n, "mB")

            body(batch(-2))
            dve.wait_ge(bias_ps, 1)
            dve.tensor_tensor(ob[0:T], ob[0:T], pE[0][0:T, 0:D], ALU.add).then_inc(ob_ok, 1)
            dve.wait_ge(ob_ok, 1)
            dve.wait_ge(tgate_ok, 1)
            dve.tensor_scalar(ob[0:T], ob[0:T], tgate[0:T, 0:1], None, ALU.mult).then_inc(ob_ok, 1)
            schedule(dve, body, -1, B)
            dve.wait_ge(part_ps, 1)
            dve.wait_ge(prefetched, 16 * len(prefetch))
            dve.wait_ge(consts["gates_ok"], 1)
            dve.scalar_tensor_tensor(part[:], pM[0][0:B, 0:D], 1.0 / S, b1[0:B, :], ALU.mult, ALU.add).then_inc(part_ok, 1)
            dve.wait_ge(part_ok, 1)
            dve.tensor_scalar(part[:], part[:], consts["tgates"][0:B, 1:2], None, ALU.mult).then_inc(part_ok, 1)

        @block.scalar
        def _(act):
            act.dma_start(lamv[:].rearrange("p k d -> p (k d)"), w["lam"].partition_broadcast(128)).then_inc(gates_in, 16)
            act.dma_start(gate[:], w["gate"].partition_broadcast(128)).then_inc(gates_in, 16)
            act.dma_start(ob[:], w["ob"].partition_broadcast(128)).then_inc(gates_in, 16)
            act.wait_ge(lam_dot, 1)
            act.activation(lame[:], lamd[:], ACT.Exp).then_inc(lam_exp, 1)
            act.activation(tgate[:], gate[:], ACT.Tanh).then_inc(tgate_ok, 1)
            consts["open_gates"](act)
            act.wait_ge(weights_in, 16 * 7)

            def take(n, u):
                stage = later(n, dict(TURNS)[u])
                if not exists(stage):
                    return
                X = bank[u]
                act.wait_ge(filled[u], count(stage, 1, 1))
                if u == "p0":
                    wait(act, filled["p1"], count(stage, 1, 0))
                    act.activation(xnT[:].rearrange("p c t -> p (c t)"), X[:, 0:KC * T], ACT.Copy).then_inc(taken[u], 1)
                elif u in ("p2", "p3"):
                    m = int(u[1]) - 2
                    wait(act, ksplit, count(stage, 4, 0))
                    ins = act.activation(kf[:, m, :], X[:, 0:S], ACT.Identity, bias=kb[:, m:m + 1])
                    ins.then_inc(taken[u], 1)
                elif u in ("p4", "p5", "p6"):
                    k = int(u[1]) - 4
                    r = min(128, S - 128 * k)
                    wait(act, av_done, count(stage, 12, 12 * (1 - RING)))
                    if stage[0] is None and stage[1] < RING:
                        act.wait_ge(v_init, RING)
                    act.activation(V[slot(stage)][0:r, k, :, 0:HD], X[0:r, 0:D].rearrange("p (h d) -> p h d", h=H), ACT.Copy).then_inc(taken[u], 1)
                elif u == "f2":
                    wait(act, filled["f3"], count(stage, 1, 0))
                    act.activation(attnT[:].rearrange("p c t -> p (c t)"), X[:, 0:KC * T], ACT.Copy).then_inc(taken[u], 1)

            started = (tgate_ok, 1)
            SPLIT_AT = {7: (qf, qrem, qpart, 0, qsplit, taken["p1"], qst_in), 9: (qf, qrem, qpart, 1, qsplit, taken["p1"], qst_in),
                        11: (kf, krem, kpart, 0, ksplit, taken["p3"], kst_in), 14: (kf, krem, kpart, 1, ksplit, taken["p3"], kst_in)}

            def split(n, full, rem, part, k, steps, ready, sent):
                m = later(n, -1)
                src = full[:].rearrange("p c s t -> p c (s t)") if full is qf else full[:]
                if k == 0:
                    act.wait_ge(ready, count(n, 1, 1))
                    if exists(m):
                        act.wait_ge(sent[slot(m)], uses_value(m, 16 * G))
                else:
                    act.wait_ge(steps, count(n, 4, 2))
                act.activation(part[:, k], rem[:] if k else src, ACT.Copy).then_inc(steps, 1)

            def sum_context(n):
                for c in range(KC):
                    waits(act, started, (ctx_in[slot(n)], uses_value(n, 16)), (csum_ok, count(n, 2, c)))
                    act.activation(summed[:], ctxs[slot(n)][:, c, :], ACT.Copy, accum_out=csum[:, c, at(n)]).then_inc(csum_ok, 1)

            def sums_out(n, q):
                act.wait_ge(av_done, count(n, 12, 3 * q + 3))
                wait(act, filled["f0" if q < 2 else "f1"], count(n, 1, 0))
                act.activation(O[:, q, :], pA[:, 0:2 * T], ACT.Copy).then_inc(o_ok, 1)

            def body(n):
                nP = later(n, 2)
                for k in range(24):
                    for u in ("p0", "p2", "p3", "f2", "p4", "p5", "p6"):
                        if AT[u] == k - 1:
                            take(n, u)
                    if exists(nP) and k in SPLIT_AT:
                        split(nP, *SPLIT_AT[k])
                    if exists(n):
                        if k >= 8 and k % 6 == 2:
                            sums_out(n, k // 6 - 1)
                        act.wait_ge(e_filled, count(n, 24, k + 1))
                        wait(act, av_done, count(n, 12, (k - 6) // 2 + 1))
                        act.activation(probs[k % 6][:], pE[k % 2][:, 0:4 * T], ACT.Exp, scale=SCALING).then_inc(e_done, 1)
                if exists(n):
                    sums_out(n, 3)
                if exists(later(n, 2)):
                    sum_context(later(n, 2))

            schedule(act, body, -2, B)
            act.wait_ge(csum_ok, 2 * B)


def zeroed(table, zero):
    rows = table.rearrange("(p k) d -> p (k d)", p=128)
    total, step = rows.shape[1], zero.shape[1]
    return [(rows[:, a:min(a + step, total)], zero[:, 0:min(step, total - a)]) for a in range(0, total, step)]


def constants(nc, ctx, gates):
    sb = lambda name, shape, dt=F32: ctx.enter_context(nc.sbuf_tensor("c_" + name, shape, dt))
    made = nc.alloc_semaphore("c_made")
    c = dict(onesb=sb("onesb", [3 * H, S], BF16), ident=sb("ident", [128, 128]), identb=sb("identb", [128, 128], BF16), neg_half=sb("neg_half", [128, 1]),
             far_s=sb("far_s", [T, 4 * T], BF16), far_t=sb("far_t", [T, 4 * T], BF16), behind=sb("behind", [T, T]),
             before=sb("before", [T, T], BF16), ones=sb("ones", [T, T], BF16), floor=sb("floor", [128, 1]),
             numbers=sb("numbers", [T, 128]), token=sb("token", [T, B]), behind_rows=sb("behind_rows", [128, 1]), zero=sb("zero", [128, 1024]), tgates=sb("tgates", [128, 4]))
    whole = sb("whole", [T, 128], mybir.dt.int32)
    whole_token, whole_behind = sb("whole_token", [T, B], mybir.dt.int32), sb("whole_behind", [128, 1], mybir.dt.int32)
    starts = dict(ident=0.0, identb=0.0, neg_half=-0.5, far_s=0.0, far_t=0.0, behind=1.0, before=1.0, ones=1.0, floor=0.0, zero=0.0, onesb=1.0)
    gates_in, gates_ok = nc.alloc_semaphore("c_gates_in"), nc.alloc_semaphore("c_gates_ok")
    FAR = -1.0e30

    def fill(pool):
        for name, value in starts.items():
            pool.memset(c[name][:], value).then_inc(made, 1)
        pool.wait_ge(made, len(starts))
        four = lambda name: c[name][:].rearrange("p (h t) -> p h t", h=4)
        selects = [(c["ident"][:], [[-1, 128]], 1, 0, ALU.not_equal, 1.0),
                   (c["identb"][:], [[-1, 128]], 1, 0, ALU.not_equal, 1.0),
                   (four("far_s"), [[0, 4], [-1, T]], 1, 0, ALU.is_ge, FAR),
                   (four("far_t"), [[0, 4], [1, T]], -1, 0, ALU.is_ge, FAR),
                   (c["behind"][:], [[-1, T]], 1, 0, ALU.is_gt, 0.0),
                   (c["before"][:], [[1, T]], -1, 0, ALU.is_gt, 0.0),
                   (c["floor"][:], [[0, 1]], -1, T - 2, ALU.is_ge, -3.0e38)]
        for out, pattern, factor, base, compare, other in selects:
            pool.affine_select(out=out, in_=out, compare_op=compare, fill=other, base=base, pattern=pattern,
                               channel_multiplier=factor).then_inc(made, 1)
        iotas = [(whole, "numbers", [[1, 128]], 0, 0), (whole_token, "token", [[T, B]], 1, 1),
                 (whole_behind, "behind_rows", [[0, 1]], B * T + 1, 1)]
        for out, _, pattern, base, factor in iotas:
            pool.iota(out[:], pattern=pattern, base=base, channel_multiplier=factor).then_inc(made, 1)
        pool.wait_ge(made, len(starts) + len(selects) + len(iotas))
        for out, name, *_ in iotas:
            pool.tensor_copy(c[name][:], out[:]).then_inc(made, 1)
        pool.wait_ge(made, len(starts) + len(selects) + 2 * len(iotas))

    def open_gates(act):
        act.dma_start(c["tgates"][:], gates.partition_broadcast(128)).then_inc(gates_in, 16)
        act.wait_ge(gates_in, 16)
        act.activation(c["tgates"][:], c["tgates"][:], ACT.Tanh).then_inc(gates_ok, 1)
        act.wait_ge(gates_ok, 1)

    c["fill"], c["open_gates"], c["gates_ok"] = fill, open_gates, gates_ok
    c["made"], c["made_value"] = made, len(starts) + 7 + 2 * 3
    return c


def self_attention(nc, W, X1, EMB, HID, RL, loads, loads_in, consts):
    run = dict(rolled=2, stride=BRING, turns=2)
    bslot = lambda n: slot(n, BRING)
    with ExitStack() as ctx:
        sb = lambda name, shape, dt=F32: ctx.enter_context(nc.sbuf_tensor("b_" + name, shape, dt))
        ps = lambda name: ctx.enter_context(nc.psum_tensor("b_" + name, [128, 512], F32))
        sem = lambda name: nc.alloc_semaphore("b_" + name)
        ring = lambda name, shape, dt=F32: [sb(f"{name}{s}", shape, dt) for s in range(BRING)]

        ident, identb, neg_half = consts["ident"], consts["identb"], consts["neg_half"]
        far_s, far_t = consts["far_s"], consts["far_t"]
        behind, floor = consts["behind"], consts["floor"]
        Wq, Wk, Wv, Wr, qkb, vb, rb = (W[n_] for n_ in ("wq", "wk", "wv", "wr", "qkb", "vb", "rb"))

        Kst = ring("Kst", [ROWS + 3, H, T], BF16)
        Qst = ring("Qst", [ROWS + 3, H, T], BF16)
        V = ring("V", [T, H, 32])
        mxr = ring("mxr", [T, H])
        mx = ring("mx", [T, H])
        stats, mv = sb("stats", [T, 6]), sb("mv", [T, 2])
        ve, rstd = sb("ve", [T, 1]), sb("rstd", [T, 1])
        xn, xnT = sb("xn", [T, D]), sb("xnT", [128, KC, T])
        qks, rem = [sb(f"qk{h}", [128, 2 * KC, T]) for h in range(2)], sb("rem", [128, 2 * KC, T])
        parts = [sb(f"part{h}", [128, 3, 2 * KC, T], BF16) for h in range(2)]
        mpart, mrem, mrow = sb("mpart", [T, 3, H], BF16), sb("mrem", [T, H]), sb("mrow", [3 * H, T], BF16)
        probs = [sb(f"probs{k}", [T, 4 * T]) for k in range(4)]
        O = sb("O", [128, 4, T])
        expm = sb("expm", [T, H])
        later_sum, total = sb("later_sum", [T, H, HD + 1]), sb("total", [T, H, HD + 1])
        rec = sb("rec", [T, H])
        hid, hidT = sb("hid", [T, D]), sb("hidT", [128, KC, T])

        pM, pE, pA, pX = ([ps(f"p{c}{s}") for s in range(2)] for c in "MEAX")

        consts_ok, ones_in = sem("consts_ok"), sem("ones_in")
        qst_in = [sem(f"qst_in{s}") for s in range(BRING)]
        kst_in = [sem(f"kst_in{s}") for s in range(BRING)]
        mrow_in = [sem(f"mrow_in{s}") for s in range(BRING)]
        ln_steps, rstd_ok, xn_ok = sem("ln_steps"), sem("rstd_ok"), sem("xn_ok")
        split_steps = sem("split_steps")
        m_filled, m_reduced, m_floored, m_steps = sem("m_filled"), sem("m_reduced"), sem("m_floored"), sem("m_steps")
        e_filled, e_done, av_done, o_ok = sem("e_filled"), sem("e_done"), sem("av_done"), sem("o_ok")
        expm_ok, f_steps, hid_kept = sem("expm_ok"), sem("f_steps"), sem("hid_kept")

        TURNS = [("p0", 3), ("f1", -1), ("f0", -1), ("p1", 3), ("f2", -1), ("mA", 1), ("p2", 3), ("f3", -1)]
        NAMES = [u for u, _ in TURNS]
        filled = {u: sem("filled_" + u) for u in NAMES}
        taken = {u: sem("taken_" + u) for u in NAMES}
        bank = {u: pX[k % 2] for k, u in enumerate(NAMES)}

        def free_bank(eng, n, u):
            k = NAMES.index(u)
            before = [(n, *t) for t in TURNS[:k]][::-1] + [(later(n, -1), *t) for t in TURNS][::-1]
            for m, name, d in before:
                if bank[name] is bank[u] and exists(later(m, d)):
                    wait(eng, taken[name], count(later(m, d), 1, 1))
                    return

        block = ctx.enter_context(nc.Block())

        @block.sync
        def _(sp):
            loaded = (W["in"], W["in_value"])
            for s in range(BRING):
                sp.dma_start(Kst[s][ROWS:ROWS + 3, :, :], consts["onesb"][:, 0:T]).then_inc(ones_in, 16)

            def send_maxima(n):
                waits(sp, loaded, (taken["mA"], count(n, 1, 1)))
                sp.dma_start(Qst[bslot(n)][ROWS:ROWS + 3, :, :], mrow[:]).then_inc(mrow_in[bslot(n)], 16)

            def body(n):
                nM, nP = later(n, 1), later(n, 3)
                for k in range(3):
                    if exists(nP):
                        waits(sp, loaded, (e_filled, count(nP, 4, 4 * (1 - BRING))), (split_steps, count(nP, 4, (1, 3, 4)[k])))
                        for to, of, first, sent in ((Qst, Q_PARTS, 0, qst_in), (Kst, K_PARTS, KC, kst_in)):
                            for g in range(G):
                                if of[g] == k:
                                    sp.dma_start(to[bslot(nP)][16 * g:16 * g + 16, :, :], parts[slot(nP, 2)][:, k, first:first + KC]).then_inc(sent[bslot(nP)], 16)
                    if k == 0 and exists(nM):
                        send_maxima(nM)

            rest = run["rolled"] + run["stride"] * run["turns"]
            schedule(sp, body, -3, rest - 1, **run)
            for n in range(rest, B + 1):
                body(batch(n))
                for dst, src in loads[2 * (n - rest):2 * (n - rest) + 2]:
                    sp.dma_start(dst, src).then_inc(loads_in, 16)

        @block.gpsimd
        def _(pool):
            inits = [(V[s][:], 0.0) for s in range(BRING)]
            inits += [(V[s][:, :, HD:HD + 1], 1.0) for s in range(BRING)]
            for k, (out, value) in enumerate(inits):
                if k:
                    pool.wait_ge(consts_ok, k)
                pool.memset(out, value).then_inc(consts_ok, 1)
            started = (consts_ok, len(inits))
            pool.wait_ge(*started)

            def deviation(n):
                pool.wait_ge(ln_steps, count(n, 3, 3))
                pool.tensor_tensor(rstd[:], ve[:], neg_half[0:T, :], ALU.pow).then_inc(rstd_ok, 1)

            def body(n):
                nF, nP = later(n, -1), later(n, 3)
                if exists(nF):
                    waits(pool, started, (f_steps, count(nF, 4, 4)))
                    pool.tensor_copy(at_batch(HID, nF), hid[:]).then_inc(hid_kept, 1)
                if exists(nP):
                    for k in range(2):
                        part, qk = parts[slot(nP, 2)], qks[slot(nP, 2)]
                        pool.wait_ge(split_steps, count(nP, 4, 2 * k + 1))
                        out = part[:, 2] if k else rem[:]
                        pool.tensor_tensor(out, rem[:] if k else qk[:], part[:, k], ALU.subtract).then_inc(split_steps, 1)

                if exists(later(n, 4)):
                    deviation(later(n, 4))

            deviation(batch(0))
            schedule(pool, body, -3, B, **run)

        @block.tensor
        def _(pe):
            pe.wait_ge(W["in"], W["in_value"])
            pe.wait_ge(consts_ok, 2 * BRING)

            def use(n, u):
                stage = later(n, dict(TURNS)[u])
                if not exists(stage):
                    return
                free_bank(pe, n, u)
                X = bank[u]
                if u == "p0":
                    pe.wait_ge(xn_ok, count(stage, 1, 1))
                    for c in range(KC):
                        mm = pe.transpose(X[:, T * c:T * (c + 1)], xn[:, 128 * c:128 * (c + 1)], ident[0:T, 0:T])
                elif u == "p1":
                    pe.wait_ge(taken["p0"], count(stage, 1, 1))
                    for k, W in enumerate((Wq, Wk)):
                        for m in range(KC):
                            for c in range(KC):
                                mm = pe.matmul(X[:, T * (KC * k + m):T * (KC * k + m + 1)], W[:, c, 128 * m:128 * (m + 1)], xnT[:, c, :],
                                               start=(c == 0), stop=(c == KC - 1))
                elif u == "p2":
                    for c in range(KC):
                        mm = pe.matmul(X[0:T, 0:D], xnT[:, c, :], Wv[:, c, :], start=(c == 0), stop=(c == KC - 1))
                elif u == "mA":
                    pe.wait_ge(m_steps, count(stage, 4, 4))
                    mm = pe.matmul(X[0:3 * H, 0:T], mpart[:].rearrange("t r h -> t (r h)"), identb[0:T, 0:T], start=True, stop=True)
                elif u == "f0":
                    pe.wait_ge(o_ok, count(stage, 2, 2))
                    for q in range(4):
                        mm = pe.transpose(X[0:T, 128 * q:128 * (q + 1)], O[:, q, :], ident[:])
                elif u == "f1":
                    mm = pe.matmul(X[0:T, 0:H * (HD + 1)], behind[:], V[bslot(stage)][:, :, 0:HD + 1], start=True, stop=True)
                elif u == "f2":
                    pe.wait_ge(f_steps, count(stage, 4, 4))
                    for c in range(KC):
                        mm = pe.transpose(X[:, T * c:T * (c + 1)], hid[:, 128 * c:128 * (c + 1)], ident[0:T, 0:T])
                elif u == "f3":
                    pe.wait_ge(taken["f2"], count(stage, 1, 1))
                    for c in range(KC):
                        mm = pe.matmul(X[0:T, 0:8], hidT[:, c, :], Wr[:, c, :], start=(c == 0), stop=(c == KC - 1))
                mm.then_inc(filled[u], 1)

            def m_tile(n, k):
                if k == 0:
                    pe.wait_ge(qst_in[bslot(n)], uses_value(n, 16 * G))
                    pe.wait_ge(kst_in[bslot(n)], uses_value(n, 16 * G))
                wait(pe, m_reduced, count(n, 4, k - 1))
                pe.matmul(pM[k % 2][0:T, 0:4 * T], identb[0:T, 0:T], far_s[:], start=True, stop=True)
                for j in range(4):
                    mm = pe.matmul(pM[k % 2][0:T, T * j:T * (j + 1)], Qst[bslot(n)][0:ROWS, 4 * k + j, :],
                                   Kst[bslot(n)][0:ROWS, 4 * k + j, :], start=False, stop=True, skip_group_check=True)
                mm.then_inc(m_filled, 1)

            def e_tile(n, k):
                if n[0] is None and n[1] == k == 0:
                    pe.wait_ge(ones_in, 16 * BRING)
                if k == 0:
                    pe.wait_ge(mrow_in[bslot(n)], uses_value(n, 16))
                wait(pe, e_done, count(n, 4, k - 1))
                pe.matmul(pE[k % 2][0:T, 0:4 * T], identb[0:T, 0:T], far_t[:], start=True, stop=True)
                for j in range(4):
                    mm = pe.matmul(pE[k % 2][0:T, T * j:T * (j + 1)], Kst[bslot(n)][:, 4 * k + j, :],
                                   Qst[bslot(n)][:, 4 * k + j, :], start=False, stop=True, skip_group_check=True)
                mm.then_inc(e_filled, 1)

            def av(n, q):
                if q < 2:
                    wait(pe, o_ok, count(n, 2, q - 1))
                if q == 0:
                    pe.wait_ge(taken["p2"], count(n, 1, 1))
                pe.wait_ge(e_done, count(n, 4, q + 1))
                for j in range(4):
                    mm = pe.matmul(pA[q % 2][32 * j:32 * j + 32, T * (q // 2):T * (q // 2 + 1)], V[bslot(n)][:, 4 * q + j, :],
                                   probs[q][:, T * j:T * (j + 1)], start=True, stop=True)
                mm.then_inc(av_done, 1)

            def body(n):
                for step in ("m0 p0 m1 f1 f0 p1 m2 m3 e0 f2 e1 a0 e2 mA p2 a1 e3 f3 a2 a3").split():
                    k = int(step[1]) if step != "mA" else None
                    if step in NAMES:
                        use(n, step)
                    elif step[0] == "m":
                        if exists(later(n, 1)):
                            m_tile(later(n, 1), k)
                    elif exists(n):
                        (e_tile if step[0] == "e" else av)(n, k)

            schedule(pe, body, -3, B, **run)

        @block.vector
        def _(dve):
            loaded = (W["in"], W["in_value"])
            dve.wait_ge(*loaded)
            dve.wait_ge(consts_ok, 2 * BRING)

            def norm(n):
                dve.bn_stats(stats[:], at_batch(X1, n)).then_inc(ln_steps, 1)
                waits(dve, loaded, (ln_steps, count(n, 3, 1)))
                dve.bn_aggr(mv[:], stats[:]).then_inc(ln_steps, 1)
                dve.wait_ge(ln_steps, count(n, 3, 2))
                dve.tensor_scalar(ve[:], mv[:, 1:2], EPS, None, ALU.add).then_inc(ln_steps, 1)

            def norm_end(n):
                dve.wait_ge(rstd_ok, count(n, 1, 1))
                wait(dve, filled["p0"], count(n, 1, 0))
                dve.tensor_scalar(xn[:], at_batch(X1, n), mv[:, 0:1], rstd[:, 0:1], ALU.subtract, ALU.mult).then_inc(xn_ok, 1)
                dve.tensor_scalar(at_batch(EMB, n), at_batch(X1, n), mv[:, 0:1], rstd[:, 0:1], ALU.subtract, ALU.mult)

            def take(n, u):
                stage = later(n, dict(TURNS)[u])
                if not exists(stage):
                    return
                X = bank[u]
                dve.wait_ge(filled[u], count(stage, 1, 1))
                if u == "p1":
                    wait(dve, split_steps, count(stage, 4, -4))
                    dve.tensor_tensor(qks[slot(stage, 2)][:], X[:, 0:4 * T].rearrange("p (c t) -> p c t", t=T),
                                      qkb[:].unsqueeze(2).broadcast_to([128, 2 * KC, T]), ALU.add).then_inc(taken[u], 1)
                elif u == "p2":
                    wait(dve, av_done, count(stage, 4, 4 * (1 - BRING)))
                    wait(dve, filled["f1"], count(stage, 1, 1 - BRING))
                    dve.tensor_tensor(V[bslot(stage)][:, :, 0:HD], X[0:T, 0:D].rearrange("p (h d) -> p h d", h=H),
                                      vb[0:T, :].rearrange("p (h d) -> p h d", h=H), ALU.add).then_inc(taken[u], 1)
                elif u == "f1":
                    dve.wait_ge(expm_ok, count(stage, 1, 1))
                    dve.tensor_tensor(later_sum[:], X[0:T, 0:H * (HD + 1)].rearrange("p (h d) -> p h d", h=H),
                                      expm[:].unsqueeze(2).broadcast_to([T, H, HD + 1]), ALU.mult).then_inc(taken[u], 1)
                elif u == "f0":
                    dve.wait_ge(taken["f1"], count(stage, 1, 1))
                    wait(dve, filled["f2"], count(stage, 1, 0))
                    wait(dve, hid_kept, count(stage, 1, 0))
                    dve.tensor_tensor(total[:], X[0:T, :].rearrange("p (h d) -> p h d", h=H)[:, :, 0:HD + 1],
                                      later_sum[:], ALU.add).then_inc(taken[u], 1)
                    dve.wait_ge(taken[u], count(stage, 1, 1))
                    dve.reciprocal(rec[:], total[:, :, HD]).then_inc(f_steps, 2)
                    dve.wait_ge(f_steps, count(stage, 4, 2))
                    dve.tensor_tensor(hid[:].rearrange("p (h d) -> p h d", h=H), total[:, :, 0:HD],
                                      rec[:].unsqueeze(2).broadcast_to([T, H, HD]), ALU.mult).then_inc(f_steps, 2)
                elif u == "f3":
                    dve.tensor_tensor(at_batch(RL, stage), X[0:T, 0:8], rb[0:T, :], ALU.add).then_inc(taken[u], 1)

            def body(n):
                nM, nP = later(n, 1), later(n, 3)

                def reduce(k):
                    if exists(nM):
                        dve.wait_ge(m_filled, count(nM, 4, k + 1))
                        dve.tensor_reduce(mxr[bslot(nM)][:, 4 * k:4 * k + 4], pM[k % 2][0:T, 0:4 * T].rearrange("p (h t) -> p h t", h=4),
                                          AX.X, ALU.max).then_inc(m_reduced, 1)

                if exists(nP):
                    norm_end(nP)
                reduce(0)
                reduce(1)
                take(n, "f1")
                take(n, "f0")
                take(n, "p1")
                reduce(2)
                reduce(3)
                if exists(nM):
                    dve.wait_ge(m_reduced, count(nM, 4, 4))
                    dve.tensor_scalar(mx[bslot(nM)][:], mxr[bslot(nM)][:], floor[0:T, 0:1], None, ALU.max).then_inc(m_floored, 1)
                    dve.wait_ge(m_floored, count(nM, 1, 1))
                if exists(nM):
                    wait(dve, filled["mA"], count(nM, 1, 0))
                    largest = mx[bslot(nM)]
                    dve.tensor_scalar(mpart[:, 0, :], largest[:], -1.0, None, ALU.mult).then_inc(m_steps, 1)
                    dve.wait_ge(m_steps, count(nM, 4, 1))
                    dve.scalar_tensor_tensor(mrem[:], largest[:], -1.0, mpart[:, 0, :], ALU.mult, ALU.subtract).then_inc(m_steps, 1)
                    dve.wait_ge(m_steps, count(nM, 4, 2))
                    dve.tensor_scalar(mpart[:, 1, :], mrem[:], 1.0, None, ALU.mult).then_inc(m_steps, 1)
                    dve.wait_ge(m_steps, count(nM, 4, 3))
                    dve.tensor_tensor(mpart[:, 2, :], mrem[:], mpart[:, 1, :], ALU.subtract).then_inc(m_steps, 1)
                if exists(later(n, 4)):
                    norm(later(n, 4))
                take(n, "p2")
                take(n, "f3")

            norm(batch(0))
            schedule(dve, body, -3, B, **run)

        @block.scalar
        def _(act):
            def take(n, u):
                stage = later(n, dict(TURNS)[u])
                if not exists(stage):
                    return
                act.wait_ge(filled[u], count(stage, 1, 1))
                if u == "mA":
                    m = later(stage, -1)
                    if exists(m):
                        act.wait_ge(mrow_in[bslot(m)], uses_value(m, 16))
                    act.activation(mrow[:], bank[u][0:3 * H, 0:T], ACT.Copy).then_inc(taken[u], 1)
                    return
                wait(act, filled["p2" if u == "p0" else "f3"], count(stage, 1, 0))
                out = xnT if u == "p0" else hidT
                act.activation(out[:].rearrange("p c t -> p (c t)"), bank[u][:, 0:KC * T], ACT.Copy).then_inc(taken[u], 1)

            def exp_tile(n, k):
                act.wait_ge(e_filled, count(n, 4, k + 1))
                wait(act, av_done, count(n, 4, k - 3))
                act.activation(probs[k][:], pE[k % 2][0:T, 0:4 * T], ACT.Exp, scale=D ** -0.5).then_inc(e_done, 1)

            def split(n, k):
                m, part, qk = later(n, -2), parts[slot(n, 2)], qks[slot(n, 2)]
                if k == 0:
                    act.wait_ge(taken["p1"], count(n, 1, 1))
                    if exists(m):
                        act.wait_ge(qst_in[bslot(m)], uses_value(m, 16 * G))
                        act.wait_ge(kst_in[bslot(m)], uses_value(m, 16 * G))
                else:
                    act.wait_ge(split_steps, count(n, 4, 2))
                act.activation(part[:, k], rem[:] if k else qk[:], ACT.Copy).then_inc(split_steps, 1)

            def body(n):
                nF, nP = later(n, -1), later(n, 3)
                if exists(nF):
                    wait(act, taken["f1"], count(nF, 1, 0))
                    act.activation(expm[:], mx[bslot(nF)][:], ACT.Exp, scale=-D ** -0.5).then_inc(expm_ok, 1)
                take(n, "p0")
                if exists(nP):
                    split(nP, 0)
                if exists(n):
                    exp_tile(n, 0)
                take(n, "f2")
                if exists(nP):
                    split(nP, 1)
                if exists(n):
                    exp_tile(n, 1)
                take(n, "mA")
                if exists(n):
                    exp_tile(n, 2)
                    exp_tile(n, 3)
                    for a in range(2):
                        act.wait_ge(av_done, count(n, 4, a + 3))
                        wait(act, filled["f0"], count(n, 1, 0))
                        act.activation(O[:, a:4:2, :], pA[a][:, 0:2 * T].rearrange("p (q t) -> p q t", q=2), ACT.Copy).then_inc(o_ok, 1)

            schedule(act, body, -3, B, **run)


def chain(eng, sem):
    done = [0]

    def link(ins):
        done[0] += 1
        ins.then_inc(sem, 1)
        eng.wait_ge(sem, done[0])
    return link


def per_expert(t):
    return t.unsqueeze(2).broadcast_to([T, B, E])


def per_batch(t):
    return t.unsqueeze(1).broadcast_to([T, B, E])


def first_max(dve, link, logits, top, onehot, work, best, falling):
    link(dve.tensor_reduce(top[:], logits, AX.X, ALU.max))
    link(dve.tensor_tensor(work[:], logits, per_expert(top[:]), ALU.is_equal))
    link(dve.tensor_tensor(work[:], work[:], per_batch(falling[:]), ALU.mult))
    link(dve.tensor_reduce(best[:], work[:], AX.X, ALU.max))
    link(dve.tensor_tensor(onehot[:], work[:], per_expert(best[:]), ALU.is_equal))


def count_before(pe, P, chosen, consts):
    flat = chosen[:].rearrange("p b e -> p (b e)")
    end = (B + 1) * E
    pe.matmul(P[0:T, 0:end], consts["before"][:], flat, start=True, stop=True)
    for d in range(1, B + 1):
        mm = pe.matmul(P[0:T, d * E:end], consts["ones"][:], flat[:, 0:end - d * E], start=False, stop=True, skip_group_check=True)
    return mm


def first_mixture(nc, We, be, weights_in, EMB, HID, RL, table, done_table, weight_kept, from_row, tables_zero, consts):
    U32 = mybir.dt.uint32
    with ExitStack() as ctx:
        sb = lambda name, shape, dt=F32: ctx.enter_context(nc.sbuf_tensor("r_" + name, shape, dt))
        ps = lambda name: ctx.enter_context(nc.psum_tensor("r_" + name, [128, 512], F32))
        sem = lambda name: nc.alloc_semaphore("r_" + name)
        top, best = sb("top", [T, B]), sb("best", [T, B])
        falling, base = sb("falling", [T, E]), sb("base", [T, E])
        onehot, work, diff, expd = (sb(n_, [T, B, E]) for n_ in ("onehot", "work", "diff", "expd"))
        chosen = sb("chosen", [T, B + 1, E], BF16)
        total, prob, kept, lost, row = (sb(n_, [T, B]) for n_ in ("total", "prob", "kept", "lost", "row"))
        to_row = sb("to_row", [T, B], U32)
        xs = [sb(f"xs{h}", [HALF, D]) for h in range(4)]
        xT = [sb(f"xT{h}", [128, KC, HALF]) for h in range(2)]
        ys = [sb(f"ys{h}", [HALF, D]) for h in range(2)]
        pR, pT, pY = ps("pR"), [ps(f"pT{h}") for h in range(2)], [ps(f"pY{h}") for h in range(2)]

        steps, onehot_ok, ranked, diff_ok, exp_ok = (sem(n_) for n_ in ("steps", "onehot_ok", "ranked", "diff_ok", "exp_ok"))
        rows_ok, sent = sem("rows_ok"), sem("sent")
        xs_in = [sem(f"xs_in{h}") for h in range(4)]
        y_out = [sem(f"y_out{h}") for h in range(2)]
        turned, xT_ok, y_ok, ys_ok = sem("turned"), sem("xT_ok"), sem("y_ok"), sem("ys_ok")
        BLOCKS = 2 * E
        run = dict(first=-2, last=BLOCKS, rolled=2, stride=4, turns=3)
        block = ctx.enter_context(nc.Block())

        @block.sync
        def _(sp):
            sp.wait_ge(sent, 16 * B)
            ready = (sent, 16 * B)

            def body(n):
                nL = later(n, 2)
                if exists(nL, BLOCKS):
                    waits(sp, ready, (turned, count(nL, 1, -3)))
                    sp.dma_start(xs[slot(nL, 4)][:], table[at(nL, HALF), :]).then_inc(xs_in[slot(nL, 4)], 16)

            schedule(sp, body, **run)
            for h in range(2):
                sp.wait_ge(y_out[h], 16 * E)

        @block.scalar
        def _(act):
            act.wait_ge(diff_ok, 1)
            act.activation(expd[:], diff[:], ACT.Exp).then_inc(exp_ok, 1)

            def body(n):
                nL = later(n, 1)
                if exists(nL, BLOCKS):
                    act.wait_ge(turned, count(nL, 1, 1))
                    wait(act, y_ok, count(nL, 1, -1))
                    act.activation(xT[slot(nL, 2)][:].rearrange("p c t -> p (c t)"), pT[slot(nL, 2)][:, 0:KC * HALF], ACT.Copy).then_inc(xT_ok, 1)
                nY = later(n, -1)
                if exists(nY, BLOCKS):
                    waits(act, (exp_ok, 1), (ys_ok, count(nY, 1, 1)))
                    act.dma_start(done_table[at(nY, HALF), :], ys[slot(nY, 2)][:]).then_inc(y_out[slot(nY, 2)], 16)

            schedule(act, body, **run)

        @block.tensor
        def _(pe):
            pe.wait_ge(onehot_ok, 1)
            count_before(pe, pR, chosen, consts).then_inc(ranked, 1)
            pe.wait_ge(*weights_in)

            def body(n):
                nL = later(n, 1)
                if exists(nL, BLOCKS):
                    pe.wait_ge(xs_in[slot(nL, 4)], uses_value(nL, 16))
                    wait(pe, xT_ok, count(nL, 1, -1))
                    for c in range(KC):
                        mm = pe.transpose(pT[slot(nL, 2)][:, HALF * c:HALF * (c + 1)], xs[slot(nL, 4)][:, 128 * c:128 * (c + 1)],
                                          consts["ident"][0:HALF, 0:HALF])
                    mm.then_inc(turned, 1)
                if exists(n, BLOCKS):
                    pe.wait_ge(xT_ok, count(n, 1, 1))
                    wait(pe, ys_ok, count(n, 1, -1))
                    e = uses(n, 2)
                    for c in range(KC):
                        mm = pe.matmul(pY[slot(n, 2)][0:HALF, 0:D], xT[slot(n, 2)][:, c, :],
                                       We[:].rearrange("p e c f -> p (e c f)")[:, bass.ds((e * KC + c) * D, D)], start=(c == 0), stop=(c == KC - 1))
                    mm.then_inc(y_ok, 1)

            schedule(pe, body, **run)

        @block.vector
        def _(dve):
            link = chain(dve, steps)
            numbers = consts["numbers"]
            link(dve.tensor_scalar(falling[:], numbers[:, 0:E], -1.0, float(E), ALU.mult, ALU.add))
            link(dve.tensor_scalar(base[:], numbers[:, 0:E], float(CAP), None, ALU.mult))
            link(dve.memset(chosen[:, B, :], 0.0))
            first_max(dve, link, RL[:], top, onehot, work, best, falling)
            dve.tensor_copy(chosen[:, 0:B, :], onehot[:]).then_inc(onehot_ok, 1)
            dve.tensor_tensor(diff[:], RL[:], per_expert(top[:]), ALU.subtract).then_inc(diff_ok, 1)
            dve.wait_ge(ranked, 1)
            rank = pR[0:T, 0:B * E].rearrange("p (b e) -> p b e", b=B)
            link(dve.tensor_scalar(work[:], rank, float(CAP), None, ALU.is_lt))
            link(dve.tensor_tensor(work[:], work[:], onehot[:], ALU.mult))
            link(dve.tensor_reduce(kept[:], work[:], AX.X, ALU.add))
            link(dve.tensor_tensor(work[:], rank, per_batch(base[:]), ALU.add))
            link(dve.tensor_tensor(work[:], work[:], onehot[:], ALU.mult))
            link(dve.tensor_reduce(row[:], work[:], AX.X, ALU.add))
            link(dve.tensor_tensor(total[:], row[:], kept[:], ALU.mult))
            link(dve.tensor_copy(from_row[:], total[:]))
            link(dve.tensor_scalar(lost[:], kept[:], -float(4 * B * T), float(4 * B * T), ALU.mult, ALU.add))
            link(dve.tensor_tensor(row[:], row[:], lost[:], ALU.add))
            dve.tensor_copy(to_row[:], row[:]).then_inc(rows_ok, 1)
            dve.wait_ge(exp_ok, 1)
            link(dve.tensor_reduce(total[:], expd[:], AX.X, ALU.add))
            link(dve.reciprocal(prob[:], total[:]))
            link(dve.tensor_tensor(weight_kept[:], prob[:], kept[:], ALU.mult))
            link(dve.tensor_tensor(lost[:], prob[:], weight_kept[:], ALU.subtract))
            for b in range(B):
                dve.scalar_tensor_tensor(EMB[:, b, :], HID[:, b, :], lost[:, b:b + 1], EMB[:, b, :], ALU.mult, ALU.add)

            dve.wait_ge(*weights_in)

            def body(n):
                if exists(n, BLOCKS):
                    dve.wait_ge(y_ok, count(n, 1, 1))
                    m = later(n, -2)
                    if exists(m, BLOCKS):
                        dve.wait_ge(y_out[slot(m, 2)], uses_value(m, 16, 2))
                    e = uses(n, 2)
                    dve.tensor_tensor(ys[slot(n, 2)][:], pY[slot(n, 2)][0:HALF, 0:D],
                                      be[0:HALF].rearrange("p e f -> p (e f)")[:, bass.ds(e * D, D)], ALU.add).then_inc(ys_ok, 1)

            schedule(dve, body, **run)

        @block.gpsimd
        def _(pool):
            pool.wait_ge(rows_ok, 1)
            pool.wait_ge(*tables_zero)
            for b in range(B):
                pool.indirect_dma_start(table, bass.IndirectOffsetOnAxis(ap=to_row[:, b:b + 1], axis=0), HID[:, b, :], None,
                                        bounds_check=E * CAP - 1, oob_is_err=False).then_inc(sent, 16)


def middle(nc, W, X, EMB, HID, RL, weight_kept, pooled_dram, done_table, from_row, loads, loads_in, consts):
    with ExitStack() as ctx:
        sb = lambda name, shape, dt=F32: ctx.enter_context(nc.sbuf_tensor("m_" + name, shape, dt))
        ps = lambda name: ctx.enter_context(nc.psum_tensor("m_" + name, [128, 512], F32))
        sem = lambda name: nc.alloc_semaphore("m_" + name)
        pair = lambda make, name, *shape: [make(f"{name}{h}", *shape) for h in range(2)]
        tg, neg_half, ident = consts["tgates"], consts["neg_half"], consts["ident"]
        gamma, beta, W1, Wr = (W[n_] for n_ in ("gamma", "beta", "w1", "wr2"))
        pooled = sb("pooled", [T, B, D])
        temp = pair(sb, "temp", [T, D])
        stats, mv, ve, rstd = ({k: pair(sb, name + k, [T, width]) for k in "ABD"}
                               for name, width in (("stats", 6), ("mv", 2), ("ve", 1), ("rstd", 1)))
        xn, xnT = ({k: pair(sb, name + k, shape) for k in "CR"} for name, shape in (("xn", [T, D]), ("xnT", [128, KC, T])))
        pT, pY = ({k: pair(ps, name + k) for k in "CR"} for name in ("pT", "pY"))

        gb_ok, part_in = sem("gb_ok"), sem("part_in")
        got = [sem(f"got{g}") for g in range(4)]
        shifted, x3_base, kept, logits_ok = (sem(n_) for n_ in ("shifted", "x3_base", "kept", "logits_ok"))
        steps = {k: sem("steps" + k) for k in "ABD"}
        STEPS = dict(A=4, B=5, D=4)
        rstd_ok = {k: sem("rstd_ok" + k) for k in "ABD"}
        xn_ok, turned, xnT_ok, mm_ok = ({k: sem(n_ + k) for k in "CR"} for n_ in ("xn_ok", "turned", "xnT_ok", "mm_ok"))
        OFFSET = dict(A=3, B=2, C=1, D=0, R=-1, L=-2)
        run = dict(first=-3, last=B + 1, rolled=4, stride=2, turns=4)
        block = ctx.enter_context(nc.Block())

        def at_stage(n, k):
            m = later(n, OFFSET[k])
            return m if exists(m) else None

        @block.sync
        def _(sp):
            sp.dma_start(pooled[:].rearrange("p b d -> p (b d)"), pooled_dram.rearrange("b d -> (b d)").partition_broadcast(T)).then_inc(part_in, 16)
            for g in range(4):
                sp.wait_ge(got[g], 16 * 4)
            for dst, src in loads:
                sp.dma_start(dst[:], src).then_inc(loads_in, 16)

        @block.gpsimd
        def _(pool):
            def fetch(g):
                for b in range(4 * g, 4 * g + 4):
                    pool.indirect_dma_start(HID[:, b, :], None, done_table, bass.IndirectOffsetOnAxis(ap=from_row[:, b:b + 1], axis=0)).then_inc(got[g], 16)

            fetch(0)
            pool.wait_ge(W["in"], W["in_value"])
            pool.tensor_scalar(gamma[:], gamma[:], tg[:, 2:3], None, ALU.mult).then_inc(gb_ok, 1)
            pool.tensor_scalar(beta[:], beta[:], tg[:, 2:3], None, ALU.mult).then_inc(gb_ok, 1)
            pool.wait_ge(gb_ok, 2)

            def power(n, k):
                m = at_stage(n, k)
                if m:
                    pool.wait_ge(steps[k], count(m, STEPS[k], STEPS[k]))
                    pool.tensor_tensor(rstd[k][slot(m, 2)][:], ve[k][slot(m, 2)][:], neg_half[0:T, :], ALU.pow).then_inc(rstd_ok[k], 1)

            def body(n):
                m = at_stage(n, "A")
                if m:
                    pool.tensor_tensor(at_batch(X, m), at_batch(X, m), beta[0:T, :], ALU.add).then_inc(shifted, 1)
                power(n, "A")
                power(n, "B")
                power(n, "D")
                m = at_stage(n, "C")
                if m:
                    if m[0] is None and m[1] == 0:
                        pool.wait_ge(part_in, 16)
                    pool.wait_ge(xn_ok["C"], count(m, 1, 1))
                    pool.tensor_tensor(at_batch(X, m), at_batch(X, m), at_batch(pooled, m), ALU.add).then_inc(x3_base, 1)

            for n in range(run["first"], run["rolled"]):
                body(batch(n))
                if n in (-3, -1, 1):
                    fetch((n + 5) // 2)
            schedule(pool, body, **dict(run, first=run["rolled"]))

        @block.tensor
        def _(pe):
            pe.wait_ge(W["in"], W["in_value"])
            def turn(n, k):
                m = at_stage(n, k)
                if m:
                    s = slot(m, 2)
                    pe.wait_ge(xn_ok[k], count(m, 1, 1))
                    wait(pe, xnT_ok[k], count(m, 1, -1))
                    for c in range(KC):
                        mm = pe.transpose(pT[k][s][:, T * c:T * (c + 1)], xn[k][s][:, 128 * c:128 * (c + 1)], ident[0:T, 0:T])
                    mm.then_inc(turned[k], 1)

            def multiply(n, k):
                m = at_stage(n, k)
                if m:
                    s = slot(m, 2)
                    W, width = dict(C=(W1, D), R=(Wr, E))[k]
                    pe.wait_ge(xnT_ok[k], count(m, 1, 1))
                    wait(pe, *((steps["D"], count(m, 4, -7)) if k == "C" else (logits_ok, count(m, 1, -1))))
                    for c in range(KC):
                        mm = pe.matmul(pY[k][s][0:T, 0:width], xnT[k][s][:, c, :], W[:, c, :], start=(c == 0), stop=(c == KC - 1))
                    mm.then_inc(mm_ok[k], 1)

            def body(n):
                turn(n, "C")
                turn(n, "R")
                multiply(n, "C")
                multiply(n, "R")

            schedule(pe, body, **run)

        @block.scalar
        def _(act):
            ready = (W["in"], W["in_value"])
            act.wait_ge(*ready)

            def turned_rows(n, k):
                m = at_stage(n, k)
                if m:
                    s = slot(m, 2)
                    act.wait_ge(turned[k], count(m, 1, 1))
                    wait(act, mm_ok[k], count(m, 1, -1))
                    act.activation(xnT[k][s][:].rearrange("p c t -> p (c t)"), pT[k][s][:, 0:KC * T], ACT.Copy).then_inc(xnT_ok[k], 1)

            def body(n):
                turned_rows(n, "C")
                turned_rows(n, "R")
                m = at_stage(n, "R")
                if m:
                    waits(act, ready, (xn_ok["R"], count(m, 1, 1)))
                    act.activation(at_batch(EMB, m), xn["R"][slot(m, 2)][:], ACT.Copy).then_inc(kept, 1)

            schedule(act, body, **run)

        @block.vector
        def _(dve):
            ready = (W["in"], W["in_value"])
            dve.wait_ge(*ready)
            dve.wait_ge(gb_ok, 2)

            def step(n, k, before, ins):
                if before:
                    waits(dve, ready, (steps[k], count(n, STEPS[k], before)))
                ins().then_inc(steps[k], 1)

            def sums(n, k):
                m = at_stage(n, k)
                if not m:
                    return
                s = slot(m, 2)
                if k == "A":
                    if m[0] is None and m[1] in (0, 4):
                        dve.wait_ge(got[m[1] // 4], 16 * 4)
                    weight = weight_kept[:, at(m)]
                    step(m, k, 0, lambda: dve.scalar_tensor_tensor(at_batch(EMB, m), at_batch(HID, m), weight, at_batch(EMB, m), ALU.mult, ALU.add))
                elif k == "B":
                    dve.wait_ge(rstd_ok["A"], count(m, 1, 1))
                    step(m, k, 0, lambda: dve.scalar_tensor_tensor(temp[s][:], at_batch(EMB, m), mv["A"][s][:, 0:1], gamma[0:T, :], ALU.subtract, ALU.mult))
                else:
                    dve.wait_ge(mm_ok["C"], count(m, 1, 1))
                    dve.wait_ge(x3_base, count(m, 1, 1))
                    step(m, k, 0, lambda: dve.scalar_tensor_tensor(at_batch(X, m), pY["C"][s][0:T, 0:D], tg[0:T, 1:2], at_batch(X, m), ALU.mult, ALU.add))

            def normed_sum(n):
                m = at_stage(n, "B")
                if m:
                    s = slot(m, 2)
                    dve.wait_ge(shifted, count(m, 1, 1))
                    step(m, "B", 1, lambda: dve.scalar_tensor_tensor(at_batch(X, m), temp[s][:], rstd["A"][s][:, 0:1], at_batch(X, m), ALU.mult, ALU.add))

            def statistics(n, k, part):
                m = at_stage(n, k)
                if not m:
                    return
                s, before = slot(m, 2), STEPS[k] - 3 + part
                rows = at_batch(EMB if k == "A" else X, m)
                step(m, k, before, (lambda: dve.bn_stats(stats[k][s][:], rows), lambda: dve.bn_aggr(mv[k][s][:], stats[k][s][:]),
                                    lambda: dve.tensor_scalar(ve[k][s][:], mv[k][s][:, 1:2], EPS, None, ALU.add))[part])

            def normalise(n, k):
                m = at_stage(n, k)
                if m:
                    s, of = slot(m, 2), "B" if k == "C" else "D"
                    dve.wait_ge(rstd_ok[of], count(m, 1, 1))
                    wait(dve, turned[k], count(m, 1, -1))
                    if k == "R":
                        wait(dve, kept, count(m, 1, -1))
                    dve.tensor_scalar(xn[k][s][:], at_batch(X, m), mv[of][s][:, 0:1], rstd[of][s][:, 0:1], ALU.subtract, ALU.mult).then_inc(xn_ok[k], 1)

            def body(n):
                sums(n, "A")
                sums(n, "B")
                statistics(n, "A", 0)
                normed_sum(n)
                sums(n, "D")
                normalise(n, "C")
                statistics(n, "A", 1)
                statistics(n, "B", 0)
                statistics(n, "D", 0)
                statistics(n, "A", 2)
                normalise(n, "R")
                statistics(n, "B", 1)
                statistics(n, "D", 1)
                statistics(n, "B", 2)
                statistics(n, "D", 2)
                m = at_stage(n, "L")
                if m:
                    waits(dve, ready, (mm_ok["R"], count(m, 1, 1)))
                    dve.tensor_copy(at_batch(RL, m), pY["R"][slot(m, 2)][0:T, 0:E]).then_inc(logits_ok, 1)

            for n in range(run["first"], run["rolled"]):
                body(batch(n))
            for g in (2, 3):
                dve.wait_ge(got[g], 16 * 4)
            schedule(dve, body, **dict(run, first=run["rolled"]))


def second_mixture(nc, Ws, X, EMB, HID, RL, source, total, out, consts):
    U32, I32 = mybir.dt.uint32, mybir.dt.int32
    W13, W2s, ws_in, ws_value = Ws
    with ExitStack() as ctx:
        sb = lambda name, shape, dt=F32: ctx.enter_context(nc.sbuf_tensor("t_" + name, shape, dt))
        ps = lambda name: ctx.enter_context(nc.psum_tensor("t_" + name, [128, 512], F32))
        sem = lambda name: nc.alloc_semaphore("t_" + name)
        NB, HC = E1_BLOCKS, HID2 // 128
        PART = 4
        SIZES = (B * T + 127) // 128
        top = [sb(f"top{k}", [T, B]) for k in range(2)]
        best, falling = sb("best", [T, B]), sb("falling", [T, E])
        onehot = [sb(f"onehot{k}", [T, B, E]) for k in range(2)]
        work, masked, rank = (sb(n_, [T, B, E]) for n_ in ("work", "masked", "rank"))
        both = sb("both", [T, B + 1, E], BF16)
        limits, over = sb("limits", [T, SIZES]), sb("over", [T, E, SIZES])
        sizes, nblocks, base = sb("sizes", [T, E]), sb("nblocks", [T, E]), sb("base", [T, E])
        ends = [sb(f"ends{k}", [T, E]) for k in range(2)]
        ended, idf, ids = sb("ended", [T, NB, E]), sb("idf", [T, NB]), sb("ids", [T, NB], I32)
        gap, ratio = sb("gap", [T, B]), sb("ratio", [T, B])
        factor, cell = (([sb(f"{n_}{k}", [T, B]) for k in range(2)]) for n_ in ("factor", "cell"))
        edges, places = sb("edges", [T, NB + 1]), sb("places", [T, 128])
        reached, in_block = sb("reached", [T, B, NB + 1]), sb("in_block", [T, B, NB])
        passed = sb("passed", [T, B])
        worth = [sb(f"worth{k}", [T, B, 2, NB]) for k in range(2)]
        at_place = [HID[:, :, 128 * k:128 * (k + 1)] for k in range(2)]
        no_token, token_row, row_factor = (sb(n_, [128, NB]) for n_ in ("no_token", "token_row", "row_factor"))
        fetched_row = [sb(f"fetched_row{h}", [128, 1], U32) for h in range(2)]
        row = [sb(f"row{k}", [T, B]) for k in range(2)]
        xs = [sb(f"xs{h}", [128, D]) for h in range(4)]
        xT = [sb(f"xT{h}", [128, KC, 128]) for h in range(2)]
        silu = [sb(f"silu{h}", [128, HID2]) for h in range(2)]
        act_ = [sb(f"act{h}", [128, HID2]) for h in range(2)]
        aT = [sb(f"aT{h}", [128, HC, 128]) for h in range(2)]
        ys = [sb(f"ys{h}", [128, D]) for h in range(2)]
        to_row = [sb(f"to_row{h}", [128, 1], U32) for h in range(2)]
        pT, pH, pG, pY = ([ps(f"p{c}{h}") for h in range(2)] for c in "THGY")

        steps, gap_ok, ratio_ok, both_ok, ranked, ids_ok, placed, turned_round, fetch_ok = (
            sem(n_) for n_ in ("steps", "gap_ok", "ratio_ok", "both_ok", "ranked", "ids_ok", "placed", "turned_round", "fetch_ok"))
        source_in, total_in, out_done = sem("source_in"), sem("total_in"), sem("out_done")
        xs_in = [sem(f"xs_in{h}") for h in range(4)]
        added = [sem(f"added{h}") for h in range(2)]
        turned, xT_ok, h_ok, g_ok, silu_ok, act_ok = (sem(n_) for n_ in ("turned", "xT_ok", "h_ok", "g_ok", "silu_ok", "act_ok"))
        aturned, aT_ok, y_ok, ys_ok = (sem(n_) for n_ in ("aturned", "aT_ok", "y_ok", "ys_ok"))
        run = dict(first=-2, last=NB, rolled=2, stride=4, turns=(NB - 4) // 4)
        block = ctx.enter_context(nc.Block())

        @block.sync
        def _(sp):
            for dst, src, done in ((source, EMB, source_in), (total, X, total_in)):
                sp.dma_start(dst[0:B * T].rearrange("(b t) d -> t b d", b=B), src[:]).then_inc(done, 16)
                sp.dma_start(dst[B * T:B * T + 128], consts["zero"][:, 0:D]).then_inc(done, 16)
            for h in range(2):
                sp.wait_ge(added[h], 16 * NB // 2)
            rows = lambda t: t.rearrange("(p k) d -> p (k d)", p=64)
            sp.dma_start(rows(out.rearrange("b t d -> (b t) d")), rows(total[0:B * T])).then_inc(out_done, 16)
            sp.wait_ge(out_done, 16)

        @block.gpsimd
        def _(pool):
            pool.wait_ge(source_in, 32)
            pool.wait_ge(total_in, 32)
            ready = (total_in, 32)

            def body(n):
                nL = later(n, 2)
                if exists(nL, NB):
                    waits(pool, ready, (fetch_ok, count(nL, 1, 1)), (turned, count(nL, 1, -3)))
                    pool.indirect_dma_start(xs[slot(nL, 4)][:], None, source, bass.IndirectOffsetOnAxis(ap=fetched_row[slot(nL, 2)][:], axis=0)).then_inc(xs_in[slot(nL, 4)], 16)
                nY = later(n, -1)
                if exists(nY, NB):
                    s, m = slot(nY, 2), later(nY, -1)
                    pairs = [(ys_ok, count(nY, 1, 1))]
                    if exists(m, NB):
                        pairs.append((added[slot(m, 2)], uses_value(m, 16, 2)))
                    waits(pool, ready, *pairs)
                    pool.indirect_dma_start(total, bass.IndirectOffsetOnAxis(ap=to_row[s][:], axis=0), ys[s][:], None,
                                            bounds_check=B * T + 127, oob_is_err=True, compute_op=ALU.add).then_inc(added[s], 16)

            schedule(pool, body, **run)

        @block.tensor
        def _(pe):
            pe.wait_ge(both_ok, 1)
            count_before(pe, pY[0], both, consts).then_inc(ranked, 1)
            for k in range(2):
                for b in range(B):
                    if b % PART == 0:
                        pe.wait_ge(placed, (B // PART) * k + b // PART + 1)
                    mm = pe.matmul(pG[0][:, 0:2 * NB], at_place[k][:, b, :], worth[k][:, b].rearrange("p c n -> p (c n)"),
                                   start=(k == 0 and b == 0), stop=(k == 1 and b == B - 1))
            mm.then_inc(turned_round, 1)
            pe.wait_ge(ids_ok, 1)
            pe.wait_ge(ws_in, ws_value)
            up, down = W13[:].rearrange("p e k c f -> p (e k c f)"), W2s[:].rearrange("p e c f -> p (e c f)")

            def expert(n):
                return pe.value_load(ids[0:1, at(n)], min_val=0, max_val=E - 1)

            def body(n):
                nL, nY = later(n, 1), later(n, -1)
                expert_n, expert_y = (expert(m) if exists(m, NB) else None for m in (n, nY))
                if exists(nY, NB):
                    s = slot(nY, 2)
                    pe.wait_ge(act_ok, count(nY, 1, 1))
                    pe.wait_ge(xT_ok, count(nY, 1, 1))
                    for c in range(HC):
                        mm = pe.transpose(pT[s][:, 128 * c:128 * (c + 1)], act_[s][:, 128 * c:128 * (c + 1)], consts["ident"][:])
                    mm.then_inc(aturned, 1)
                if exists(n, NB):
                    s = slot(n, 2)
                    pe.wait_ge(xT_ok, count(n, 1, 1))
                    wait(pe, act_ok, count(n, 1, -1))
                    for k, (P, ok) in enumerate(((pH[s], h_ok), (pG[s], g_ok))):
                        for c in range(KC):
                            mm = pe.matmul(P[:, 0:HID2], xT[s][:, c, :], up[:, bass.ds(expert_n * (2 * KC * HID2) + (k * KC + c) * HID2, HID2)],
                                           start=(c == 0), stop=(c == KC - 1))
                        mm.then_inc(ok, 1)
                if exists(nL, NB):
                    pe.wait_ge(xs_in[slot(nL, 4)], uses_value(nL, 16))
                    wait(pe, aT_ok, count(nL, 1, -1))
                    for c in range(KC):
                        mm = pe.transpose(pT[slot(nL, 2)][:, 128 * c:128 * (c + 1)], xs[slot(nL, 4)][:, 128 * c:128 * (c + 1)], consts["ident"][:])
                    mm.then_inc(turned, 1)
                if exists(nY, NB):
                    s = slot(nY, 2)
                    pe.wait_ge(aT_ok, count(nY, 1, 1))
                    wait(pe, ys_ok, count(nY, 1, -1))
                    for c in range(HC):
                        mm = pe.matmul(pY[s][:, 0:D], aT[s][:, c, :], down[:, bass.ds(expert_y * (HC * D) + c * D, D)], start=(c == 0), stop=(c == HC - 1))
                    mm.then_inc(y_ok, 1)

            schedule(pe, body, **run)

        @block.scalar
        def _(act):
            act.wait_ge(gap_ok, 1)
            act.activation(ratio[:], gap[:], ACT.Exp).then_inc(ratio_ok, 1)

            def body(n):
                nL, nY = later(n, 1), later(n, -1)
                if exists(nY, NB):
                    s = slot(nY, 2)
                    act.wait_ge(aturned, count(nY, 1, 1))
                    wait(act, y_ok, count(nY, 1, -1))
                    act.activation(aT[s][:].rearrange("p c t -> p (c t)"), pT[s][:, 0:HC * 128], ACT.Copy).then_inc(aT_ok, 1)
                if exists(n, NB):
                    s = slot(n, 2)
                    act.wait_ge(h_ok, count(n, 1, 1))
                    wait(act, act_ok, count(n, 1, -1))
                    act.activation(silu[s][:], pH[s][:, 0:HID2], ACT.Silu).then_inc(silu_ok, 1)
                if exists(nL, NB):
                    s = slot(nL, 2)
                    act.wait_ge(turned, count(nL, 1, 1))
                    wait(act, g_ok, count(nL, 1, -1))
                    act.activation(xT[s][:].rearrange("p c t -> p (c t)"), pT[s][:, 0:KC * 128], ACT.Copy).then_inc(xT_ok, 1)

            schedule(act, body, **run)

        @block.vector
        def _(dve):
            link = chain(dve, steps)
            numbers = consts["numbers"]
            link(dve.tensor_scalar(falling[:], numbers[:, 0:E], -1.0, float(E), ALU.mult, ALU.add))
            link(dve.memset(both[:, B, :], 0.0))
            link(dve.tensor_scalar(limits[:], numbers[:, 0:SIZES], 128.0, None, ALU.mult))
            link(dve.tensor_scalar(edges[:], numbers[:, 0:NB + 1], 128.0, None, ALU.mult))
            link(dve.tensor_scalar(places[:], numbers[:], -128.0, None, ALU.add))
            first_max(dve, link, RL[:], top[0], onehot[0], work, best, falling)
            link(dve.scalar_tensor_tensor(masked[:], onehot[0][:], -3.0e38, RL[:], ALU.mult, ALU.add))
            first_max(dve, link, masked[:], top[1], onehot[1], work, best, falling)
            dve.tensor_tensor(both[:, 0:B, :], onehot[0][:], onehot[1][:], ALU.add).then_inc(both_ok, 1)
            dve.tensor_tensor(gap[:], top[1][:], top[0][:], ALU.subtract).then_inc(gap_ok, 1)
            dve.wait_ge(ratio_ok, 1)
            link(dve.tensor_scalar(work[:, :, 0], ratio[:], 1.0, None, ALU.add))
            link(dve.reciprocal(best[:], work[:, :, 0]))
            link(dve.tensor_scalar(factor[0][:], best[:], consts["tgates"][0:T, 3:4], None, ALU.mult))
            link(dve.tensor_tensor(factor[1][:], factor[0][:], ratio[:], ALU.mult))
            dve.wait_ge(ranked, 1)
            before = pY[0][0:T, 0:B * E].rearrange("p (b e) -> p b e", b=B)
            link(dve.tensor_copy(sizes[:], pY[0][0:T, B * E:(B + 1) * E]))
            link(dve.tensor_tensor(over[:], sizes[:].unsqueeze(2).broadcast_to([T, E, SIZES]), limits[:].unsqueeze(1).broadcast_to([T, E, SIZES]), ALU.is_gt))
            link(dve.tensor_reduce(nblocks[:], over[:], AX.X, ALU.add))
            a, b_ = nblocks, ends[0]
            for d in (1, 2, 4):
                link(dve.tensor_copy(b_[:, 0:d], a[:, 0:d]))
                link(dve.tensor_tensor(b_[:, d:E], a[:, d:E], a[:, 0:E - d], ALU.add))
                a, b_ = b_, ends[1] if b_ is ends[0] else ends[0]
            end = a
            link(dve.tensor_tensor(base[:], end[:], nblocks[:], ALU.subtract))
            link(dve.tensor_scalar(base[:], base[:], 128.0, None, ALU.mult))
            link(dve.tensor_tensor(rank[:], before, per_batch(base[:]), ALU.add))
            for k in range(2):
                link(dve.tensor_tensor(work[:], rank[:], onehot[k][:], ALU.mult))
                link(dve.tensor_reduce(row[k][:], work[:], AX.X, ALU.add))
                link(dve.tensor_tensor(reached[:], row[k][:].unsqueeze(2).broadcast_to([T, B, NB + 1]), edges[:].unsqueeze(1).broadcast_to([T, B, NB + 1]), ALU.is_ge))
                link(dve.tensor_reduce(passed[:], reached[:], AX.X, ALU.add))
                link(dve.scalar_tensor_tensor(cell[k][:], passed[:], -128.0, row[k][:], ALU.mult, ALU.add))
                link(dve.tensor_tensor(in_block[:], reached[:, :, 0:NB], reached[:, :, 1:NB + 1], ALU.subtract))
                for c, value in enumerate((consts["token"], factor[k])):
                    link(dve.tensor_tensor(worth[k][:, :, c, :], in_block[:], value[:].unsqueeze(2).broadcast_to([T, B, NB]), ALU.mult))
                for b in range(0, B, PART):
                    dve.tensor_tensor(at_place[k][:, b:b + PART, :], cell[k][:, b:b + PART].unsqueeze(2).broadcast_to([T, PART, 128]),
                                      places[:].unsqueeze(1).broadcast_to([T, PART, 128]), ALU.is_equal).then_inc(placed, 1)
            link(dve.tensor_tensor(ended[:], end[:].unsqueeze(1).broadcast_to([T, NB, E]), numbers[:, 0:NB].unsqueeze(2).broadcast_to([T, NB, E]), ALU.is_le))
            link(dve.tensor_reduce(idf[:], ended[:], AX.X, ALU.add))
            link(dve.tensor_scalar(idf[:], idf[:], float(E - 1), None, ALU.min))
            link(dve.tensor_copy(ids[:], idf[:]))
            dve.wait_ge(turned_round, 1)
            link(dve.tensor_scalar(no_token[:], pG[0][:, 0:NB], 0.0, consts["behind_rows"][:, 0:1], ALU.is_equal, ALU.mult))
            link(dve.scalar_tensor_tensor(token_row[:], pG[0][:, 0:NB], -1.0, no_token[:], ALU.add, ALU.add))
            dve.tensor_copy(row_factor[:], pG[0][:, NB:2 * NB]).then_inc(ids_ok, 1)
            ready = (turned_round, 1)
            dve.wait_ge(ids_ok, 1)

            def fetch(m):
                pairs = [(xs_in[slot(later(m, -2), 4)], uses_value(later(m, -2), 16))] if exists(later(m, -2), NB) else []
                waits(dve, ready, *pairs)
                dve.tensor_copy(fetched_row[slot(m, 2)][:], token_row[:, at(m)]).then_inc(fetch_ok, 1)

            def body(n):
                nL, nY = later(n, 2), later(n, -1)
                if exists(nL, NB):
                    fetch(nL)
                if exists(n, NB):
                    s = slot(n, 2)
                    dve.wait_ge(silu_ok, count(n, 1, 1))
                    dve.wait_ge(g_ok, count(n, 1, 1))
                    wait(dve, aturned, count(n, 1, -1))
                    dve.tensor_tensor(act_[s][:], silu[s][:], pG[s][:, 0:HID2], ALU.mult).then_inc(act_ok, 1)
                if exists(nY, NB):
                    s, m = slot(nY, 2), later(nY, -2)
                    pairs = [(y_ok, count(nY, 1, 1))]
                    if exists(m, NB):
                        pairs.append((added[s], uses_value(m, 16, 2)))
                    waits(dve, ready, *pairs)
                    dve.tensor_scalar(ys[s][:], pY[s][:, 0:D], row_factor[:, at(nY)], None, ALU.mult)
                    dve.tensor_copy(to_row[s][:], token_row[:, at(nY)]).then_inc(ys_ok, 1)

            schedule(dve, body, **run)


def build(nc, a, out):
    with ExitStack() as ctx:
        sb = lambda name, shape, dt=F32: ctx.enter_context(nc.sbuf_tensor(name, shape, dt))
        dram = lambda name, shape: nc.dram_tensor(name, shape, F32, kind="Internal").ap()
        table0, done0 = dram("table0", [E * CAP, D]), dram("done0", [E * CAP, D])
        source, total = dram("source", [B * T + 128, D]), dram("total", [B * T + 128, D])
        pooled_dram = dram("pooled_context", [B, D])
        X = sb("X", [T, B, D])
        EMB, HID = sb("EMB", [T, B, D]), sb("HID", [T, B, D])
        RL, weight_kept = sb("RL", [T, B, E]), sb("weight_kept", [T, B])
        from_row = sb("from_row", [T, B], mybir.dt.uint32)
        W = {name: sb(name, shape) for name, shape in dict(
            b_wq=[128, KC, D], b_wk=[128, KC, D], b_wv=[128, KC, D], b_wr=[128, KC, E], b_qkb=[128, 2 * KC], b_vb=[128, D],
            b_rb=[128, E], m_w1=[128, KC, D], m_w2=[128, KC, D], m_wr2=[128, KC, E], m_b1=[128, D], m_gamma=[128, D], m_beta=[128, D]).items()}
        prefetch = [(t[:], a[name] if len(a[name].shape) > 1 else a[name].partition_broadcast(128)) for name, t in W.items()]
        prefetched, table0_zero = nc.alloc_semaphore("prefetched"), nc.alloc_semaphore("table0_zero")
        consts = constants(nc, ctx, a["gates"])
        zeros0 = zeroed(table0, consts["zero"])
        group = lambda prefix, of=a: {k[len(prefix):]: v for k, v in of.items() if k.startswith(prefix)}
        loaded = {"in": prefetched, "in_value": 16 * len(prefetch)}
        with nc.cleanup_on_exit():
            cross_attention(nc, a["x"], a["ctxT"], group("a_"), X, (W["m_w2"], W["m_b1"], pooled_dram), prefetch, prefetched, zeros0, table0_zero, consts)
        We, be = sb("We", [128, E, KC, D]), sb("be", [128, E, D])
        experts_in = nc.alloc_semaphore("experts_in")
        expert_loads = [(We[:, e], a["r_we"][:, e]) for e in range(E)]
        expert_loads.append((be[:].rearrange("p e d -> p (e d)"), a["r_be"].partition_broadcast(128)))
        with nc.cleanup_on_exit():
            self_attention(nc, dict(group("b_", W), **loaded), X, EMB, HID, RL, expert_loads, experts_in, consts)
        W13, W2s = sb("W13", [128, E, 2, KC, HID2]), sb("W2s", [128, E, HID2 // 128, D])
        ws_in = nc.alloc_semaphore("ws_in")
        first_mixture(nc, We, be, (experts_in, 16 * len(expert_loads)), EMB, HID, RL, table0, done0, weight_kept, from_row, (table0_zero, 16 * len(zeros0)), consts)
        middle(nc, dict(group("m_", W), **loaded), X, EMB, HID, RL, weight_kept, pooled_dram, done0, from_row,
               ((W13, a["w13"]), (W2s, a["w2s"])), ws_in, consts)
        second_mixture(nc, (W13, W2s, ws_in, 32), X, EMB, HID, RL, source, total, out, consts)


def arrays_of(inputs):
    import numpy as np

    i = {k: np.asarray(v) for k, v in inputs.items()}
    order = np.array([(2 * (p % 8) + m) * HD + p // 8 for m in range(KC) for p in range(128)])

    def chunks(wt):
        return np.ascontiguousarray(wt.reshape(KC, 128, -1).transpose(1, 0, 2))

    def columns(v):
        return np.ascontiguousarray(v.reshape(-1, 128).T)

    win, bin_ = i["L0_xattn_in_proj_weight"], i["L0_xattn_in_proj_bias"]
    flat = lambda k: i["L0_ffn_" + k].reshape(D, D)
    W = i["L1_xattn_W"]
    up = np.stack([i["L1_ffn_W1"], i["L1_ffn_W3"]], axis=1)
    out = {
        "x": i["x"], "ctxT": i["ctx_1024"].reshape(B, S, KC, 128).transpose(0, 3, 2, 1),
        "gates": np.concatenate([i["g_xattn"], i["g_ffn"]]),
        "a_wq": chunks(win[0:D][order].T), "a_wk": chunks(win[D:2 * D][order].T), "a_wv": chunks(win[2 * D:].T),
        "a_wo": chunks(i["L0_xattn_out_proj_weight"].T), "a_qb": columns(bin_[0:D][order]), "a_kb": columns(bin_[D:2 * D][order]),
        "a_vb": columns(bin_[2 * D:]), "a_ob": i["L0_xattn_out_proj_bias"], "a_gate": i["g_xattn"][0:1],
        "a_lam": np.stack([i["L0_xattn_lambda_" + k] for k in ("q1", "k1", "q2", "k2")]).reshape(-1),
        "b_wq": chunks(flat("Wq")[order].T), "b_wk": chunks(flat("Wk")[order].T), "b_wv": chunks(flat("Wv").T),
        "b_wr": chunks(i["L0_ffn_Wsw"].T), "b_qkb": columns(np.concatenate([i["L0_ffn_bq"].reshape(D)[order], i["L0_ffn_bk"].reshape(D)[order]])),
        "b_vb": i["L0_ffn_bv"].reshape(D), "b_rb": i["L0_ffn_bsw"],
        "r_we": i["L0_ffn_We"].reshape(E, D, KC, 128).transpose(3, 0, 2, 1), "r_be": i["L0_ffn_be"].reshape(E * D),
        "m_w1": chunks(W[:, 0:D].T), "m_w2": chunks(W[:, D:].T), "m_wr2": chunks(i["L1_ffn_Wr"]), "m_b1": i["L1_xattn_b"],
        "m_gamma": i["L0_ffn_gamma"], "m_beta": i["L0_ffn_beta"],
        "w13": up.reshape(E, 2, KC, 128, HID2).transpose(3, 0, 1, 2, 4),
        "w2s": i["L1_ffn_W2"].reshape(E, HID2 // 128, 128, D).transpose(2, 0, 1, 3),
    }
    return {k: np.ascontiguousarray(v) for k, v in out.items()}


def kernel(**inputs):
    import concourse.bacc as _bacc
    from concourse.bass_utils import run_bass_kernel_spmd as _run

    nc = _bacc.Bacc("TRN2", target_bir_lowering=False, num_devices=1)
    arrays = arrays_of(inputs)
    args = {k: nc.dram_tensor("in_" + k, v.shape, mybir.dt.from_np(v.dtype), kind="ExternalInput").ap() for k, v in arrays.items()}
    out = nc.dram_tensor("out_x", (B, T, D), F32, kind="ExternalOutput").ap()
    build(nc, args, out)
    r = _run(nc, [{"in_" + k: v for k, v in arrays.items()}], core_ids=[0])
    return r.results[0]["out_x"]
```
